# Optimizing a Trainium2 kernel written in Bass

```python
import numpy as np
import jax
import jax.numpy as jnp

def _softmax(x, axis=-1):
    return jax.nn.softmax(x, axis=axis)

def _gelu(x):
    return jax.nn.gelu(x, approximate=True)

def _silu(x):
    return jax.nn.silu(x)

def _sigmoid(x):
    return jax.nn.sigmoid(x)

def _layernorm(x, axis=-1, eps=1e-05):
    m = jnp.mean(x, axis=axis, keepdims=True)
    v = jnp.var(x, axis=axis, keepdims=True)
    return (x - m) / jnp.sqrt(v + eps)

def _scatter_add(tgt, idx, src, axis=0):
    return tgt.at[idx].add(src)

def _segment_sum(src, seg, n):
    return jax.ops.segment_sum(src, seg, n)
kernel_name = 'mk_prb_d2_jaxref_r4_f6049e'

def setup_inputs(seed: int=0):
    np.random.seed(seed)
    _w = jnp.asarray

    def _L0_attn_setup():
        import jax, jax.numpy as jnp
        import numpy as np
        EPS = 1e-06

        def _rmsnorm(x, w):
            dt = x.dtype
            xf = x.astype(jnp.float32)
            var = jnp.mean(xf * xf, axis=-1, keepdims=True)
            xf = xf * jax.lax.rsqrt(var + EPS)
            return xf.astype(dt) * w
        key = jax.random.key(seed)
        ks = jax.random.split(key, 4)
        B, N, C = (4, 512, 256)
        H = 16
        D = C // H
        x = jax.random.normal(ks[0], (B, N, C), dtype=jnp.float32)
        W_qkv = jax.random.normal(ks[1], (C, 3 * C), dtype=jnp.float32) * (1.0 / np.sqrt(C))
        b_qkv = jnp.zeros((3 * C,), dtype=jnp.float32)
        W_proj = jax.random.normal(ks[2], (C, C), dtype=jnp.float32) * (1.0 / np.sqrt(C))
        b_proj = jnp.zeros((C,), dtype=jnp.float32)
        qn_w = jnp.ones((D,), dtype=jnp.float32)
        kn_w = jnp.ones((D,), dtype=jnp.float32)
        return {'x': x, 'W_qkv': W_qkv, 'b_qkv': b_qkv, 'W_proj': W_proj, 'b_proj': b_proj, 'qn_w': qn_w, 'kn_w': kn_w}
    _L0_attn_in = _L0_attn_setup()

    def _L0_ffn_setup():
        import jax, jax.numpy as jnp
        import numpy as np
        E, TOPK, R = (8, 2, 16)
        D, H, GH = (256, 16, 64)
        HD = D // H
        SCALE = HD ** (-0.5)

        def _svd_moe(x, Wm, U, S, V, b, idx, gates):
            main = jnp.einsum('bsd,od->bso', x, Wm)
            Ug, Sg, Vg = (U[idx], S[idx], V[idx])
            xv = jnp.einsum('bsd,bkrd->bksr', x, Vg)
            xvs = xv * Sg[:, :, None, :]
            eo = jnp.einsum('bksr,bkor->bkso', xvs, Ug)
            expert = jnp.einsum('bkso,bk->bso', eo, gates)
            return main + expert + b
        key = jax.random.key(seed)
        ks = jax.random.split(key, 32)
        B, S = (32, 257)
        inp = {'hidden_states': jax.random.normal(ks[0], (B, S, D), jnp.float32)}
        inp['gw1'] = jax.random.normal(ks[1], (GH, D), jnp.float32) * 0.02
        inp['gb1'] = jnp.zeros((GH,), jnp.float32)
        inp['gw2'] = jax.random.normal(ks[2], (E, GH), jnp.float32) * 0.02
        inp['gb2'] = jnp.zeros((E,), jnp.float32)
        i = 3
        for p in ('q', 'k', 'v', 'o'):
            inp[p + 'Wm'] = jax.random.normal(ks[i], (D, D), jnp.float32) * 0.02
            i += 1
            inp[p + 'U'] = jax.random.normal(ks[i], (E, D, R), jnp.float32) * 0.02
            i += 1
            inp[p + 'S'] = jax.random.normal(ks[i], (E, R), jnp.float32) * 0.1
            i += 1
            inp[p + 'V'] = jax.random.normal(ks[i], (E, R, D), jnp.float32) * 0.02
            i += 1
            inp[p + 'b'] = jnp.zeros((D,), jnp.float32)
        return inp
    _L0_ffn_in = _L0_ffn_setup()

    def _L1_attn_setup():
        import jax, jax.numpy as jnp
        import numpy as np
        N_HEADS = 16

        def _rope_cos_sin(hs, T, dtype):
            t = jnp.arange(1, T + 1, dtype=dtype)[:, None]
            i = jnp.arange(hs // 2, dtype=dtype)
            theta = (1.0 / 10000.0) ** (2.0 * i / hs)
            ang = t * theta
            return (jnp.cos(ang), jnp.sin(ang))

        def _apply_rope(u, cos, sin):
            ue = u[..., ::2]
            uo = u[..., 1::2]
            real = cos * ue - sin * uo
            out = jnp.stack([real, jnp.zeros_like(real)], axis=-1)
            return out.reshape(u.shape)
        key = jax.random.key(seed)
        ks = jax.random.split(key, 6)
        B, T, H = (2, 512, 256)
        scale = 0.02
        return {'x': jax.random.normal(ks[0], (B, T, H), dtype=jnp.float32), 'Wq': jax.random.normal(ks[1], (H, H), dtype=jnp.float32) * scale, 'bq': jnp.zeros((H,), dtype=jnp.float32), 'Wk': jax.random.normal(ks[2], (H, H), dtype=jnp.float32) * scale, 'bk': jnp.zeros((H,), dtype=jnp.float32), 'Wv': jax.random.normal(ks[3], (H, H), dtype=jnp.float32) * scale, 'bv': jnp.zeros((H,), dtype=jnp.float32), 'Wo': jax.random.normal(ks[4], (H, H), dtype=jnp.float32) * scale, 'bo': jnp.zeros((H,), dtype=jnp.float32)}
    _L1_attn_in = _L1_attn_setup()

    def _L1_ffn_setup():
        import jax, jax.numpy as jnp
        import numpy as np
        S, B, H = (512, 2, 256)
        NUM_HEADS, NUM_KV_HEADS = (16, 4)
        HEAD_DIM = H // NUM_HEADS
        E, TOP_K, FFN = (16, 2, 512)
        CAP_FACTOR = 1.25
        EPS = 1e-05

        def _layernorm(x, w, b):
            mu = jnp.mean(x, axis=-1, keepdims=True)
            var = jnp.mean((x - mu) ** 2, axis=-1, keepdims=True)
            return (x - mu) * jax.lax.rsqrt(var + EPS) * w + b
        key = jax.random.key(seed)
        ks = jax.random.split(key, 6)
        qkv_out = (NUM_HEADS + 2 * NUM_KV_HEADS) * HEAD_DIM
        sdH = 1.0 / np.sqrt(H)
        sdF = 1.0 / np.sqrt(FFN)
        return {'hidden_states': jax.random.normal(ks[0], (S, B, H), jnp.float32), 'ln1_weight': jnp.ones((H,), jnp.float32), 'ln1_bias': jnp.zeros((H,), jnp.float32), 'ln2_weight': jnp.ones((H,), jnp.float32), 'ln2_bias': jnp.zeros((H,), jnp.float32), 'qkv_weight': jax.random.normal(ks[1], (qkv_out, H), jnp.float32) * sdH, 'proj_weight': jax.random.normal(ks[2], (H, H), jnp.float32) * sdH, 'router_weight': jax.random.normal(ks[3], (E, H), jnp.float32) * sdH, 'moe_w1': jax.random.normal(ks[4], (E, FFN, H), jnp.float32) * sdH, 'moe_w2': jax.random.normal(ks[5], (E, H, FFN), jnp.float32) * sdF}
    _L1_ffn_in = _L1_ffn_setup()
    _d = {'L0_attn_x': _L0_attn_in['x'], 'L0_attn_W_qkv': _L0_attn_in['W_qkv'], 'L0_attn_b_qkv': _L0_attn_in['b_qkv'], 'L0_attn_W_proj': _L0_attn_in['W_proj'], 'L0_attn_b_proj': _L0_attn_in['b_proj'], 'L0_attn_qn_w': _L0_attn_in['qn_w'], 'L0_attn_kn_w': _L0_attn_in['kn_w'], 'L0_ffn_gw1': _L0_ffn_in['gw1'], 'L0_ffn_gb1': _L0_ffn_in['gb1'], 'L0_ffn_gw2': _L0_ffn_in['gw2'], 'L0_ffn_gb2': _L0_ffn_in['gb2'], 'L0_ffn_qWm': _L0_ffn_in['qWm'], 'L0_ffn_qU': _L0_ffn_in['qU'], 'L0_ffn_qS': _L0_ffn_in['qS'], 'L0_ffn_qV': _L0_ffn_in['qV'], 'L0_ffn_qb': _L0_ffn_in['qb'], 'L0_ffn_kWm': _L0_ffn_in['kWm'], 'L0_ffn_kU': _L0_ffn_in['kU'], 'L0_ffn_kS': _L0_ffn_in['kS'], 'L0_ffn_kV': _L0_ffn_in['kV'], 'L0_ffn_kb': _L0_ffn_in['kb'], 'L0_ffn_vWm': _L0_ffn_in['vWm'], 'L0_ffn_vU': _L0_ffn_in['vU'], 'L0_ffn_vS': _L0_ffn_in['vS'], 'L0_ffn_vV': _L0_ffn_in['vV'], 'L0_ffn_vb': _L0_ffn_in['vb'], 'L0_ffn_oWm': _L0_ffn_in['oWm'], 'L0_ffn_oU': _L0_ffn_in['oU'], 'L0_ffn_oS': _L0_ffn_in['oS'], 'L0_ffn_oV': _L0_ffn_in['oV'], 'L0_ffn_ob': _L0_ffn_in['ob'], 'L1_attn_Wq': _L1_attn_in['Wq'], 'L1_attn_bq': _L1_attn_in['bq'], 'L1_attn_Wk': _L1_attn_in['Wk'], 'L1_attn_bk': _L1_attn_in['bk'], 'L1_attn_Wv': _L1_attn_in['Wv'], 'L1_attn_bv': _L1_attn_in['bv'], 'L1_attn_Wo': _L1_attn_in['Wo'], 'L1_attn_bo': _L1_attn_in['bo'], 'L1_ffn_ln1_weight': _L1_ffn_in['ln1_weight'], 'L1_ffn_ln1_bias': _L1_ffn_in['ln1_bias'], 'L1_ffn_ln2_weight': _L1_ffn_in['ln2_weight'], 'L1_ffn_ln2_bias': _L1_ffn_in['ln2_bias'], 'L1_ffn_qkv_weight': _L1_ffn_in['qkv_weight'], 'L1_ffn_proj_weight': _L1_ffn_in['proj_weight'], 'L1_ffn_router_weight': _L1_ffn_in['router_weight'], 'L1_ffn_moe_w1': _L1_ffn_in['moe_w1'], 'L1_ffn_moe_w2': _L1_ffn_in['moe_w2']}
    _x0 = _d['L0_attn_x']
    _d['L0_attn_x'] = jax.random.normal(jax.random.fold_in(jax.random.key(seed), 1), (8, 512, 256), dtype=_x0.dtype)
    del _x0
    return _d

def reference(L0_attn_x, L0_attn_W_qkv, L0_attn_b_qkv, L0_attn_W_proj, L0_attn_b_proj, L0_attn_qn_w, L0_attn_kn_w, L0_ffn_gw1, L0_ffn_gb1, L0_ffn_gw2, L0_ffn_gb2, L0_ffn_qWm, L0_ffn_qU, L0_ffn_qS, L0_ffn_qV, L0_ffn_qb, L0_ffn_kWm, L0_ffn_kU, L0_ffn_kS, L0_ffn_kV, L0_ffn_kb, L0_ffn_vWm, L0_ffn_vU, L0_ffn_vS, L0_ffn_vV, L0_ffn_vb, L0_ffn_oWm, L0_ffn_oU, L0_ffn_oS, L0_ffn_oV, L0_ffn_ob, L1_attn_Wq, L1_attn_bq, L1_attn_Wk, L1_attn_bk, L1_attn_Wv, L1_attn_bv, L1_attn_Wo, L1_attn_bo, L1_ffn_ln1_weight, L1_ffn_ln1_bias, L1_ffn_ln2_weight, L1_ffn_ln2_bias, L1_ffn_qkv_weight, L1_ffn_proj_weight, L1_ffn_router_weight, L1_ffn_moe_w1, L1_ffn_moe_w2):

    def _L0_attn_ref(x, W_qkv, b_qkv, W_proj, b_proj, qn_w, kn_w):
        import jax, jax.numpy as jnp
        import numpy as np
        EPS = 1e-06

        def _rmsnorm(x, w):
            dt = x.dtype
            xf = x.astype(jnp.float32)
            var = jnp.mean(xf * xf, axis=-1, keepdims=True)
            xf = xf * jax.lax.rsqrt(var + EPS)
            return xf.astype(dt) * w
        B, N, C = x.shape
        H = 16
        D = C // H
        qkv = jnp.einsum('bnc,cd->bnd', x, W_qkv) + b_qkv
        qkv = qkv.reshape(B, N, 3, H, D)
        q = qkv[:, :, 0].transpose(0, 2, 1, 3)
        k = qkv[:, :, 1].transpose(0, 2, 1, 3)
        v = qkv[:, :, 2].transpose(0, 2, 1, 3)
        q = _rmsnorm(q, qn_w)
        k = _rmsnorm(k, kn_w)
        scale = D ** (-0.5)
        attn = jnp.einsum('bhqd,bhkd->bhqk', q, k) * scale
        attn = jax.nn.softmax(attn, axis=-1)
        out = jnp.einsum('bhqk,bhkd->bhqd', attn, v)
        out = out.transpose(0, 2, 1, 3).reshape(B, N, C)
        out = jnp.einsum('bnc,cd->bnd', out, W_proj) + b_proj
        return out

    def _L0_ffn_ref(hidden_states, gw1, gb1, gw2, gb2, qWm, qU, qS, qV, qb, kWm, kU, kS, kV, kb, vWm, vU, vS, vV, vb, oWm, oU, oS, oV, ob):
        import jax, jax.numpy as jnp
        import numpy as np
        E, TOPK, R = (8, 2, 16)
        D, H, GH = (256, 16, 64)
        HD = D // H
        SCALE = HD ** (-0.5)

        def _svd_moe(x, Wm, U, S, V, b, idx, gates):
            main = jnp.einsum('bsd,od->bso', x, Wm)
            Ug, Sg, Vg = (U[idx], S[idx], V[idx])
            xv = jnp.einsum('bsd,bkrd->bksr', x, Vg)
            xvs = xv * Sg[:, :, None, :]
            eo = jnp.einsum('bksr,bkor->bkso', xvs, Ug)
            expert = jnp.einsum('bkso,bk->bso', eo, gates)
            return main + expert + b
        B, S, _ = hidden_states.shape
        pooled = hidden_states.mean(axis=1)
        h = jax.nn.relu(pooled @ gw1.T + gb1)
        logits = h @ gw2.T + gb2
        top_vals, top_idx = jax.lax.top_k(logits, TOPK)
        gates = jax.nn.softmax(top_vals, axis=-1)
        q = _svd_moe(hidden_states, qWm, qU, qS, qV, qb, top_idx, gates) * SCALE
        k = _svd_moe(hidden_states, kWm, kU, kS, kV, kb, top_idx, gates)
        v = _svd_moe(hidden_states, vWm, vU, vS, vV, vb, top_idx, gates)

        def shp(t):
            return t.reshape(B, S, H, HD).transpose(0, 2, 1, 3)
        q, k, v = (shp(q), shp(k), shp(v))
        attn = jax.nn.softmax(jnp.einsum('bhsd,bhtd->bhst', q, k), axis=-1)
        ctx = jnp.einsum('bhst,bhtd->bhsd', attn, v)
        ctx = ctx.transpose(0, 2, 1, 3).reshape(B, S, D)
        out = _svd_moe(ctx, oWm, oU, oS, oV, ob, top_idx, gates)
        return out

    def _L1_attn_ref(x, Wq, bq, Wk, bk, Wv, bv, Wo, bo):
        import jax, jax.numpy as jnp
        import numpy as np
        N_HEADS = 16

        def _rope_cos_sin(hs, T, dtype):
            t = jnp.arange(1, T + 1, dtype=dtype)[:, None]
            i = jnp.arange(hs // 2, dtype=dtype)
            theta = (1.0 / 10000.0) ** (2.0 * i / hs)
            ang = t * theta
            return (jnp.cos(ang), jnp.sin(ang))

        def _apply_rope(u, cos, sin):
            ue = u[..., ::2]
            uo = u[..., 1::2]
            real = cos * ue - sin * uo
            out = jnp.stack([real, jnp.zeros_like(real)], axis=-1)
            return out.reshape(u.shape)
        B, T, H = x.shape
        nh = N_HEADS
        hs = H // nh

        def proj(W, b):
            y = jnp.einsum('bth,oh->bto', x, W) + b
            return y.reshape(B, T, nh, hs).transpose(0, 2, 1, 3)
        Q = proj(Wq, bq)
        K = proj(Wk, bk)
        V = proj(Wv, bv)
        cos, sin = _rope_cos_sin(hs, T, x.dtype)
        Q = _apply_rope(Q, cos, sin)
        K = _apply_rope(K, cos, sin)
        scores = jnp.einsum('bhqd,bhkd->bhqk', Q, K) * (1.0 / jnp.sqrt(jnp.asarray(hs, x.dtype)))
        causal = jnp.tril(jnp.ones((T, T), dtype=bool))
        scores = jnp.where(causal, scores, jnp.asarray(-10000000000.0, x.dtype))
        att = jax.nn.softmax(scores, axis=-1)
        y = jnp.einsum('bhqk,bhkd->bhqd', att, V)
        y = y.transpose(0, 2, 1, 3).reshape(B, T, H)
        return jnp.einsum('bth,oh->bto', y, Wo) + bo

    def _L1_ffn_ref(hidden_states, ln1_weight, ln1_bias, ln2_weight, ln2_bias, qkv_weight, proj_weight, router_weight, moe_w1, moe_w2):
        import jax, jax.numpy as jnp
        import numpy as np
        S, B, H = (512, 2, 256)
        NUM_HEADS, NUM_KV_HEADS = (16, 4)
        HEAD_DIM = H // NUM_HEADS
        E, TOP_K, FFN = (16, 2, 512)
        CAP_FACTOR = 1.25
        EPS = 1e-05

        def _layernorm(x, w, b):
            mu = jnp.mean(x, axis=-1, keepdims=True)
            var = jnp.mean((x - mu) ** 2, axis=-1, keepdims=True)
            return (x - mu) * jax.lax.rsqrt(var + EPS) * w + b
        S_, B_, H_ = hidden_states.shape
        dtype = hidden_states.dtype
        ln1 = _layernorm(hidden_states, ln1_weight, ln1_bias)
        qkv = jnp.einsum('sbh,oh->sbo', ln1, qkv_weight)
        q_sz = NUM_HEADS * HEAD_DIM
        kv_sz = NUM_KV_HEADS * HEAD_DIM
        q = qkv[..., :q_sz].reshape(S_, B_, NUM_HEADS, HEAD_DIM)
        k = qkv[..., q_sz:q_sz + kv_sz].reshape(S_, B_, NUM_KV_HEADS, HEAD_DIM)
        v = qkv[..., q_sz + kv_sz:].reshape(S_, B_, NUM_KV_HEADS, HEAD_DIM)
        rep = NUM_HEADS // NUM_KV_HEADS
        k = jnp.repeat(k, rep, axis=2)
        v = jnp.repeat(v, rep, axis=2)
        scale = 1.0 / np.sqrt(HEAD_DIM)
        scores = jnp.einsum('qbhd,kbhd->bhqk', q, k) * scale
        causal = jnp.tril(jnp.ones((S_, S_), bool))
        scores = jnp.where(causal, scores, jnp.asarray(-1e+30, dtype))
        attn = jax.nn.softmax(scores, axis=-1)
        attn_out = jnp.einsum('bhqk,kbhd->qbhd', attn, v).reshape(S_, B_, H_)
        proj_out = jnp.einsum('sbh,oh->sbo', attn_out, proj_weight)
        hidden_after_attn = hidden_states + proj_out
        ln2 = _layernorm(hidden_after_attn, ln2_weight, ln2_bias).reshape(-1, H_)
        T = ln2.shape[0]
        logits = ln2 @ router_weight.T
        probs = jax.nn.softmax(logits, axis=-1)
        top_p, top_i = jax.lax.top_k(probs, TOP_K)
        cap = int(np.ceil(T * TOP_K / E * CAP_FACTOR))
        exp_idx = top_i.reshape(-1)
        gate = top_p.reshape(-1).astype(dtype)
        tok = jnp.repeat(jnp.arange(T), TOP_K)
        onehot = jax.nn.one_hot(exp_idx, E, dtype=jnp.int32)
        pos = (jnp.cumsum(onehot, axis=0) * onehot).sum(-1) - 1
        keep = pos < cap
        pos_c = jnp.where(keep, pos, cap)
        buf = jnp.zeros((E, cap + 1, H_), dtype)
        buf = buf.at[exp_idx, pos_c].add(ln2[tok] * keep[:, None].astype(dtype))
        h1 = jax.nn.gelu(jnp.einsum('ech,efh->ecf', buf, moe_w1))
        h2 = jnp.einsum('ecf,ehf->ech', h1, moe_w2)
        out_ent = h2[exp_idx, pos_c] * (gate * keep.astype(dtype))[:, None]
        moe_out = jnp.zeros((T, H_), dtype).at[tok].add(out_ent)
        return hidden_after_attn + moe_out.reshape(S_, B_, H_)
    x = L0_attn_x
    xn = _layernorm(x, axis=-1)
    x = x + _L0_attn_ref(xn, L0_attn_W_qkv, L0_attn_b_qkv, L0_attn_W_proj, L0_attn_b_proj, L0_attn_qn_w, L0_attn_kn_w) + _L0_ffn_ref(xn, L0_ffn_gw1, L0_ffn_gb1, L0_ffn_gw2, L0_ffn_gb2, L0_ffn_qWm, L0_ffn_qU, L0_ffn_qS, L0_ffn_qV, L0_ffn_qb, L0_ffn_kWm, L0_ffn_kU, L0_ffn_kS, L0_ffn_kV, L0_ffn_kb, L0_ffn_vWm, L0_ffn_vU, L0_ffn_vS, L0_ffn_vV, L0_ffn_vb, L0_ffn_oWm, L0_ffn_oU, L0_ffn_oS, L0_ffn_oV, L0_ffn_ob)
    xn = _layernorm(x, axis=-1)
    x = x + _L1_attn_ref(xn, L1_attn_Wq, L1_attn_bq, L1_attn_Wk, L1_attn_bk, L1_attn_Wv, L1_attn_bv, L1_attn_Wo, L1_attn_bo) + _L1_ffn_ref(xn, L1_ffn_ln1_weight, L1_ffn_ln1_bias, L1_ffn_ln2_weight, L1_ffn_ln2_bias, L1_ffn_qkv_weight, L1_ffn_proj_weight, L1_ffn_router_weight, L1_ffn_moe_w1, L1_ffn_moe_w2)
    return x

_drawn_inputs = setup_inputs


def setup_inputs(seed=0):
    import zlib

    import numpy as np

    out = dict(_drawn_inputs(seed))
    spreads = {'L0_attn_b_qkv': (0.0, 0.1),
     'L0_attn_b_proj': (0.0, 0.1),
     'L0_attn_qn_w': (1.0, 0.6),
     'L0_attn_kn_w': (1.0, 0.6),
     'L0_ffn_gb1': (0.0, 0.8),
     'L0_ffn_gb2': (0.0, 0.8),
     'L0_ffn_qb': (0.0, 0.8),
     'L0_ffn_kb': (0.0, 2.0),
     'L0_ffn_vb': (0.0, 0.1),
     'L0_ffn_ob': (0.0, 0.1),
     'L1_attn_bq': (0.0, 0.8),
     'L1_attn_bk': (0.0, 0.8),
     'L1_attn_bv': (0.0, 0.55),
     'L1_attn_bo': (0.0, 0.294),
     'L1_ffn_ln1_weight': (1.0, 0.2),
     'L1_ffn_ln1_bias': (0.0, 0.1),
     'L1_ffn_ln2_weight': (1.0, 0.6),
     'L1_ffn_ln2_bias': (0.0, 0.304)}
    factors = {'L0_ffn_gw1': 8.0,
     'L0_ffn_gw2': 8.0,
     'L0_ffn_qWm': 8.0,
     'L0_ffn_qU': 8.0,
     'L0_ffn_qS': 8.0,
     'L0_ffn_qV': 8.0,
     'L0_ffn_kWm': 8.0,
     'L0_ffn_kU': 8.0,
     'L0_ffn_kS': 8.0,
     'L0_ffn_kV': 8.0,
     'L0_ffn_vWm': 8.0,
     'L0_ffn_vU': 8.0,
     'L0_ffn_vS': 8.0,
     'L0_ffn_vV': 8.0,
     'L0_ffn_oU': 8.0,
     'L0_ffn_oS': 8.0,
     'L0_ffn_oV': 8.0,
     'L1_attn_Wq': 8.0,
     'L1_attn_Wk': 8.0,
     'L1_attn_Wv': 5.347,
     'L1_attn_Wo': 2.911}
    for name, (base, spread) in spreads.items():
        noise = np.random.default_rng([zlib.crc32(name.encode()), seed]).standard_normal(out[name].shape)
        drawn = base * np.exp(spread * noise) if base else spread * noise
        out[name] = jnp.asarray(drawn.astype(out[name].dtype))
    for name, factor in factors.items():
        out[name] = (out[name] * factor).astype(out[name].dtype)
    return out
```

```python
from contextlib import ExitStack

import concourse.bass as bass
from concourse import mybir

F32 = mybir.dt.float32
BF16 = mybir.dt.bfloat16
I32 = mybir.dt.int32
U32 = mybir.dt.uint32
ALU = mybir.AluOpType
ACT = mybir.ActivationFunctionType
AX = mybir.AxisListType

P = 128
BATCH, SEQ, C = 8, 512, 256
HEADS, HD = 16, 16
TOK = BATCH * SEQ
NT = TOK // P
TPB = SEQ // P
KT = C // P
GH = 4
GROUPS = HEADS // GH
GW = GH * HD
CYCLE = 8

SLOTS = 7
QPART = (0, 0, 0, 1, 1, 1, 2)
KPART = (0, 1, 2, 0, 1, 2, 0)
SROWS = SLOTS * HD
MPARTS = 3
KROWS = SROWS + MPARTS
NEG = -1.0e30

EXPERTS, FFN, TOPK = 16, 512, 2
CAP = -(-TOK * TOPK * 5 // (EXPERTS * 4))
SLOTROWS = EXPERTS * CAP
CT = CAP // P


def layernorm(nc, ctx, name, src, dst, eps):
    with ExitStack() as s:
        stats = s.enter_context(nc.sbuf_tensor(name + "_stats", [P, TPB, 6], F32))
        mv4 = s.enter_context(nc.sbuf_tensor(name + "_mv4", [P, TPB, 2], F32))
        mv = s.enter_context(nc.sbuf_tensor(name + "_mv", [P, NT, 2], F32))
        half = s.enter_context(nc.sbuf_tensor(name + "_half", [P, NT], F32))
        carry = s.enter_context(nc.sbuf_tensor(name + "_carry", [P, 2], F32))
        vare = s.enter_context(nc.sbuf_tensor(name + "_vare", [P, NT], F32))
        rstd = s.enter_context(nc.sbuf_tensor(name + "_rstd", [P, NT], F32))
        stat_done = s.enter_context(nc.semaphore(name + "_stat_done"))
        aggr_done = s.enter_context(nc.semaphore(name + "_aggr_done"))
        mv_done = s.enter_context(nc.semaphore(name + "_mv_done"))
        var_done = s.enter_context(nc.semaphore(name + "_var_done"))
        rstd_done = s.enter_context(nc.semaphore(name + "_rstd_done"))
        half_done = s.enter_context(nc.semaphore(name + "_half_done"))
        begun = s.enter_context(nc.semaphore(name + "_begun"))
        blk = s.enter_context(nc.Block())

        @blk.vector
        def _(dve):
            dve.memset(carry[:, :], 0.0).then_inc(begun, 1)
            dve.wait_ge(begun, 1)
            with dve.Fori(0, BATCH) as b:
                for t in range(TPB):
                    dve.bn_stats(stats[:, t, :], src[:, bass.ds(TPB * b + t, 1), :]).then_inc(stat_done, 1)
                dve.wait_ge(stat_done, TPB * (b + 1))
                dve.tensor_copy(carry[:, 1:2], carry[:, 0:1])
                for t in range(TPB):
                    dve.bn_aggr(mv4[:, t, :], stats[:, t, :]).then_inc(aggr_done, 1)
                dve.wait_ge(aggr_done, TPB * (b + 1))
                dve.tensor_copy(mv[:, bass.ds(TPB * b, TPB), :], mv4[:, :, :]).then_inc(mv_done, 1)
                dve.wait_ge(mv_done, b + 1)
            dve.tensor_scalar(vare[:, :], mv[:, :, 1], eps, None, ALU.add).then_inc(var_done, 1)
            dve.wait_ge(rstd_done, 1)
            with dve.Fori(0, BATCH) as b:
                for t in range(TPB):
                    j = TPB * b + t
                    dve.tensor_scalar(dst[:, bass.ds(j, 1), :], src[:, bass.ds(j, 1), :],
                                      mv[:, bass.ds(j, 1), 0], rstd[:, bass.ds(j, 1)],
                                      ALU.subtract, ALU.mult)

        @blk.gpsimd
        def _(pool):
            pool.memset(half[:, :], -0.5).then_inc(half_done, 1)
            pool.wait_ge(half_done, 1)
            pool.wait_ge(var_done, 1)
            pool.tensor_tensor(rstd[:, :], vare[:, :], half[:, :], ALU.pow).then_inc(rstd_done, 1)


def attention(nc, name, layer, X, XN, w, consts, dram):
    L0 = layer == 0
    UPB = CYCLE if L0 else GROUPS
    NU = BATCH * UPB
    TURNS = NU // CYCLE
    causal = not L0

    def kind(i):
        return "C" if not L0 else ("A" if i % CYCLE < GROUPS else "B")

    def live(n, k):
        return 0 <= n + k < NU

    OT_AT = {1: "B", 5: "A"} if L0 else {1: "C", 5: "C"}

    def rounds(n):
        r = []
        i = n % CYCLE
        if live(n, 6) and kind(i + 6) == "B":
            r.append((0, "weff"))
        if i in OT_AT and 0 <= n - 5 < NU:
            r.append((2, "ot"))
            if not (L0 and i == 5):
                r.append((3, "outproj"))
        if live(n, -1):
            r.append((4, "norm"))
        if live(n, 6):
            r.append((5, "proj"))
        if L0 and i == 1 and 0 <= n < NU:
            r.append((6, "weffo"))
        if i in ((1,) if L0 else (1, 5)) and live(n, 7):
            r.append((7, "xt"))
        return r

    first = -6
    last = NU + 1

    def total(f, n):
        if isinstance(n, tuple):
            turn, i = n
            per = sum(f(m) for m in range(CYCLE, 2 * CYCLE))
            return (turn - 1) * per + sum(f(m) for m in range(first, CYCLE + i))
        return sum(f(m) for m in range(first, n))

    def whole(n):
        return n if not isinstance(n, tuple) else CYCLE + n[1]

    def unit(n, k):
        return n + k if not isinstance(n, tuple) else n[0] * CYCLE + (n[1] + k)

    def wait(eng, semaphore, value):
        if isinstance(value, int) and value <= 0:
            return
        eng.wait_ge(semaphore, value)

    def ma_count(n, what):
        names = [x for _, x in rounds(whole(n))]
        return total(lambda m: len(rounds(m)), n) + names.index(what) + 1

    def xt_count(n):
        return total(lambda m: sum(x == "xt" for _, x in rounds(m)), n)

    def back(n, k):
        return n - k if not isinstance(n, tuple) else (n[0], n[1] - k)

    def mb_rounds(n):
        stacks, rows = live(n, 3), live(n, 1)
        return ([0, 1, 2] if stacks else []) + (["rows"] if rows else []) + ([3] if stacks else [])

    def mb_count(n, what=None):
        before = total(lambda m: len(mb_rounds(m)), n)
        return before if what is None else before + mb_rounds(whole(n)).index(what) + 1

    def steps(eng, step):
        for n in range(first, CYCLE):
            step(n)
        if TURNS > 2:
            with eng.Fori(1, TURNS - 1) as turn:
                for i in range(CYCLE):
                    step((turn, i))
        for n in range(NU - CYCLE, last + 1):
            step(n)

    with ExitStack() as s:
        def sb(nm, shape, dt=F32):
            return s.enter_context(nc.sbuf_tensor(name + nm, shape, dt))

        def sem(nm):
            return s.enter_context(nc.semaphore(name + nm))

        identf, identb = consts["identf"], consts["identb"]
        xs = sb("xs", [P, TPB, C])
        xT = sb("xT", [P, KT, SEQ])
        qkf = sb("qkf", [P, 2, 2, TPB * GH * HD])
        qkw = sb("qkw", [P, 2, 2, TPB * GH * HD])
        part = [sb(f"part{j}", [P, 2, TPB * GH * HD], BF16) for j in range(3)]
        rest = sb("rest", [P, 2, TPB * GH * HD])
        slots = sb("slots", [P, 2, 2, TPB * GH, SROWS], BF16)
        stack = sb("stack", [P, 4, 2, GH, SEQ], BF16)
        vbuf = sb("vbuf", [P, CYCLE, TPB, GH, 32])
        mx = sb("mx", [P, 2, TPB * GH])
        mres = sb("mres", [P, TPB * GH])
        minus = sb("minus", [P, TPB, GH])
        carry = sb("carry", [P, 3])
        mparts = sb("mparts", [P, TPB, MPARTS, GH], BF16)
        mrows = sb("mrows", [MPARTS * GH, SEQ], BF16)
        prob = sb("prob", [P, 2, GH, SEQ])
        oT = sb("oT", [P, SEQ])
        rsum = sb("rsum", [P, TPB, GH])
        onA = sb("onA", [P, TPB, C])
        onB = sb("onB", [P, TPB, C])
        otA = sb("otA", [P, KT, SEQ])
        otB = sb("otB", [P, KT, SEQ]) if L0 else otA
        if L0:
            sq = sb("sq", [P, 2 * TPB * GH * HD])
            ms = sb("ms", [P, 2 * TPB * GH])
            rstd = sb("rstd", [P, 2 * TPB * GH])
            neghalf = sb("neghalf", [P, 2 * TPB * GH])
            xin = sb("xin", [P, TPB, C])
            us = sb("us", [P, 4, C])
            weff = sb("weff", [P, KT, 3 * GW])
            weffo = sb("weffo", [P, KT, C])
        else:
            rot = sb("rot", [P, 3, TPB * GH, HD // 2])

        SC = s.enter_context(nc.psum_tensor(name + "SC", [P, 2, SEQ], F32))
        MX = s.enter_context(nc.psum_tensor(name + "MX", [P, 2, SEQ], F32))
        OV = s.enter_context(nc.psum_tensor(name + "OV", [P, SEQ], F32))
        MB = s.enter_context(nc.psum_tensor(name + "MB", [P, 8, P], BF16))
        MA = s.enter_context(nc.psum_tensor(name + "MA", [P, 1024], F32))

        ma_full = sem("ma_full")
        ma_free = sem("ma_free")
        mb_full = sem("mb_full")
        mb_free = sem("mb_free")
        score_ready = sem("score_ready")
        exp_done = sem("exp_done")
        smax_ready = sem("smax_ready")
        max_done = sem("max_done")
        pv_done = sem("pv_done")
        ov_read = sem("ov_read")
        qk_ready = sem("qk_ready")
        v_ready = sem("v_ready")
        sq_ready = sem("sq_ready")
        ss_ready = sem("ss_ready")
        ms_ready = sem("ms_ready")
        pool_norm = sem("pool_norm")
        split_done = sem("split_done")
        slots_done = sem("slots_done")
        mprep = sem("mprep")
        mrow_sent = sem("mrow_sent")
        xs_loaded = sem("xs_loaded")
        xin_loaded = sem("xin_loaded")
        xin_biased = sem("xin_biased")
        us_done = sem("us_done")
        recip_done = sem("recip_done")
        init = sem("init")
        pool_init = sem("pool_init")
        out_sent = sem("out_sent")

        MM_NORM = {"A": 3, "B": 1, "C": 6}

        def norm_steps(m):
            return MM_NORM[kind(m + 5)] if live(m, 5) else 0

        def a_units(k):
            return lambda m: int(live(m, k) and kind(m + k) == "A")

        def has(n, k):
            return live(whole(n), k)

        blk = s.enter_context(nc.Block())

        @blk.sync
        def _(sp):
            def load_xs(batch):
                sp.dma_start(xs[:, :, :], XN[:, bass.ds(batch * TPB, TPB), :]).then_inc(xs_loaded, 16)

            load_xs(0)

            def step(n):
                w_ = whole(n)
                i = w_ % CYCLE
                if i in ((0,) if L0 else (0, 4)) and (isinstance(n, tuple) or 0 < (w_ + 8) // UPB < BATCH):
                    past = back(n, 7 if L0 else 3)
                    if isinstance(past, int) and "xt" not in [x for _, x in rounds(past)]:
                        sp.wait_ge(ma_full, 1)
                    else:
                        sp.wait_ge(ma_full, ma_count(past, "xt") + 1)
                    load_xs((w_ + 8) // UPB if isinstance(n, int) else n[0] * (CYCLE // UPB) + (i + 8) // UPB)
                if has(n, 1):
                    sp.wait_ge(mb_free, mb_count(n, "rows"))
                    for j in range(MPARTS):
                        sp.dma_start(stack[SROWS + j:SROWS + j + 1, (w_ + 1) % 4, 0, :, :],
                                     mrows[j * GH:(j + 1) * GH, :]).then_inc(mrow_sent, 16)
                if L0 and i == 2 and 0 <= w_ < NU:
                    batch = w_ // CYCLE if isinstance(n, int) else n[0]
                    if isinstance(n, tuple) or n > CYCLE:
                        sp.wait_ge(ma_free, ma_count(back(n, 1), "outproj") + 1)
                    sp.dma_start(xin[:, :, :], dram["x"][:, bass.ds(batch * TPB, TPB), :]).then_inc(xin_loaded, 16)
                if not L0 and "outproj" in [x for _, x in rounds(w_)]:
                    batch = (w_ - 5) // UPB if isinstance(n, int) else 2 * n[0] + (n[1] - 5) // UPB
                    sp.wait_ge(ma_free, ma_count(n, "outproj") + 1)
                    sp.dma_start(dram["out"][:, bass.ds(batch * TPB, TPB), :],
                                 X[:, bass.ds(batch * TPB, TPB), :]).then_inc(out_sent, 16)

            steps(sp, step)
            if not L0:
                sp.wait_ge(out_sent, 16 * BATCH)

        @blk.tensor
        def _(pe):
            pe.wait_ge(init, 3)

            def xt_round(n):
                wait(pe, xs_loaded, 16 if n is None else 16 * (xt_count(n) + 2))
                for t in range(TPB):
                    for kt in range(KT):
                        mm = pe.transpose(MA[:, kt * SEQ + t * P:kt * SEQ + (t + 1) * P],
                                          xs[:, t, kt * P:(kt + 1) * P], identf[:, :])
                mm.then_inc(ma_full, 1)

            def ma_round(n, what):
                w_ = whole(n)
                i = w_ % CYCLE
                wait(pe, ma_free, ma_count(n, what))
                if what == "weff":
                    g = (i + 6) % GROUPS
                    nb = (w_ + 6) // CYCLE if isinstance(n, int) else n[0] + (n[1] + 6) // CYCLE
                    wait(pe, us_done, 4 * (nb + 1))
                    for kt in range(KT):
                        for j in range(3):
                            mm = pe.matmul(MA[:, kt * 3 * GW + j * GW:kt * 3 * GW + (j + 1) * GW],
                                           w["V"][:, j, kt * P:(kt + 1) * P], us[:, j, g * GW:(g + 1) * GW],
                                           start=True, stop=True)
                elif what == "weffo":
                    for kt in range(KT):
                        mm = pe.matmul(MA[:, kt * SEQ:kt * SEQ + C], w["V"][:, 3, kt * P:(kt + 1) * P],
                                       us[:, 3, :], start=True, stop=True)
                elif what == "proj":
                    kd = kind(i + 6)
                    g = (i + 6) % GROUPS
                    for t in range(TPB):
                        for kt in range(KT):
                            rhs = weff[:, kt, :] if kd == "B" else w["W" + kd][:, kt, g, :]
                            mm = pe.matmul(MA[:, t * C:t * C + 3 * GW], xT[:, kt, t * P:(t + 1) * P], rhs,
                                           start=(kt == 0), stop=(kt == KT - 1))
                elif what == "ot":
                    src = onB if i == 1 else onA
                    for t in range(TPB):
                        for kt in range(KT):
                            mm = pe.transpose(MA[:, kt * SEQ + t * P:kt * SEQ + (t + 1) * P],
                                              src[:, t, kt * P:(kt + 1) * P], identf[:, :])
                elif what == "outproj":
                    pairs = [(otA, w["WoA"]), (otB, weffo)] if L0 else [(otA, w["WoC"])]
                    for t in range(TPB):
                        for q, (ot, wo) in enumerate(pairs):
                            for kt in range(KT):
                                mm = pe.matmul(MA[:, t * C:(t + 1) * C], ot[:, kt, t * P:(t + 1) * P],
                                               wo[:, kt, :], start=(q == 0 and kt == 0),
                                               stop=(q == len(pairs) - 1 and kt == KT - 1))
                elif what == "norm":
                    wait(pe, ov_read, unit(n, 0))
                    for t in range(TPB):
                        mm = pe.transpose(MA[:, t * P:(t + 1) * P], oT[:, t * P:(t + 1) * P], identf[:, :])
                mm.then_inc(ma_full, 1)

            def stack_round(n, r):
                qk, half = r // 2, r % 2
                wait(pe, slots_done, 6 * (unit(n, 3) + 1))
                wait(pe, mb_free, mb_count(n, r) - 1)
                for j in range(8):
                    t, h = 2 * half + j // GH, j % GH
                    mm = pe.transpose(MB[0:SROWS, (j % GH) * 2 + j // GH, :],
                                      slots[:, (whole(n) + 3) % 2, qk, t * GH + h, :], identb[:, :])
                mm.then_inc(mb_full, 1)

            def mrow_round(n):
                wait(pe, mprep, 5 * (unit(n, 1) + 1))
                wait(pe, mb_free, mb_count(n, "rows") - 1)
                for t in range(TPB):
                    mm = pe.transpose(MB[0:MPARTS * GH, t, :], mparts[:, t, :, :], identb[:, :])
                mm.then_inc(mb_full, 1)

            def score(n, sl, h):
                u4 = whole(n) % 4
                if sl == 0 and h == 0:
                    wait(pe, mrow_sent, 16 * MPARTS * (unit(n, 0) + 1))
                wait(pe, exp_done, 16 * unit(n, 0) + 4 * sl + h - 1)
                lo = sl * P if causal else 0
                mm = pe.matmul(SC[:, h % 2, lo:SEQ], stack[0:KROWS, u4, 1, h, sl * P:(sl + 1) * P],
                               stack[0:KROWS, u4, 0, h, lo:SEQ], start=True, stop=not causal)
                if causal:
                    mm = pe.matmul(SC[:, h % 2, lo:lo + P], identb[:, :], consts["mask_kq"][:, :],
                                   start=False, stop=True)
                mm.then_inc(score_ready, 1)

            def maxmm(n, sl, h):
                u4 = (whole(n) + 2) % 4
                if sl == 0 and h == 0:
                    wait(pe, mb_free, mb_count(n))
                wait(pe, max_done, 16 * unit(n, 2) + 4 * sl + h - 1)
                hi = (sl + 1) * P if causal else SEQ
                mm = pe.matmul(MX[:, h % 2, 0:hi], stack[0:SROWS, u4, 0, h, sl * P:(sl + 1) * P],
                               stack[0:SROWS, u4, 1, h, 0:hi], start=True, stop=not causal)
                if causal:
                    mm = pe.matmul(MX[:, h % 2, hi - P:hi], identb[:, :], consts["mask_qk"][:, :],
                                   start=False, stop=True)
                mm.then_inc(smax_ready, 1)

            def pv(n, k, sl, h):
                v8 = (whole(n) + k) % CYCLE
                u = unit(n, k)
                wait(pe, exp_done, 16 * u + 4 * sl + h + 1)
                if sl == 0 and h == 0:
                    wait(pe, ov_read, u)
                    wait(pe, v_ready, u + 1)
                lo = sl * P if causal else 0
                mm = pe.matmul(OV[32 * h:32 * h + 32, lo:SEQ], vbuf[:, v8, sl, h, :],
                               prob[:, sl % 2, h, lo:SEQ], start=(sl == 0), stop=(sl == TPB - 1),
                               skip_group_check=True)
                if h == GH - 1:
                    mm.then_inc(pv_done, 1)

            xt_round(None)

            PV_HEADS = ((0,), (1,), (2,), (3,))
            PV_LATE = ((), (0, 1), (2,), (3,))

            def step(n):
                r = dict(rounds(whole(n)))
                for p in range(8):
                    sl, hp = p // 2, p % 2
                    if p in r:
                        if r[p] == "xt":
                            wait(pe, ma_free, ma_count(n, "xt"))
                            xt_round(n)
                        else:
                            ma_round(n, r[p])
                    if has(n, 3) and p in (0, 2, 4, 6):
                        stack_round(n, p // 2)
                    if has(n, 1) and p == 5:
                        mrow_round(n)
                    for h in (2 * hp, 2 * hp + 1):
                        if has(n, 0):
                            score(n, sl, h)
                        if has(n, 2):
                            maxmm(n, sl, h)
                        for hv in (PV_LATE if sl == 1 else PV_HEADS)[h]:
                            if sl == 0:
                                if has(n, -1):
                                    pv(n, -1, TPB - 1, hv)
                            elif has(n, 0):
                                pv(n, 0, sl - 1, hv)

            steps(pe, step)

        @blk.scalar
        def _(act):
            act.wait_ge(init, 3)
            STACK_COPIES = [(0, 0), (0, 1), (2, 0), (2, 1), (4, 0), (4, 1), (6, 0), (6, 1)]
            act.wait_ge(ma_full, 1)
            act.copy(xT[:, :, :], MA[:, :].rearrange("p (k n) -> p k n", k=KT)).then_inc(ma_free, 1)

            def step(n):
                w_ = whole(n)
                r = dict(rounds(w_))
                for p in range(8):
                    sl, hp = p // 2, p % 2
                    if r.get(p) in ("xt", "ot"):
                        wait(act, ma_full, ma_count(n, r[p]) + 1)
                        if r[p] == "xt":
                            dst = xT
                        else:
                            dst = otB if L0 and w_ % CYCLE == 1 else otA
                        act.copy(dst[:, :, :], MA[:, :].rearrange("p (k n) -> p k n", k=KT)).then_inc(ma_free, 1)
                    if has(n, 1) and p == 5:
                        wait(act, mb_full, mb_count(n, "rows"))
                        wait(act, mrow_sent, 16 * MPARTS * unit(n, 1))
                        act.copy(mrows[:, :].rearrange("p (t n) -> p t n", t=TPB),
                                 MB[0:MPARTS * GH, 0:TPB, :]).then_inc(mb_free, 1)
                    if p == 2 and has(n, -1):
                        wait(act, pv_done, 4 * unit(n, 0))
                        if has(n, -2):
                            wait(act, ma_full, ma_count(back(n, 1), "norm") + 1)
                        act.copy(oT[:, :], OV[:, :]).then_inc(ov_read, 1)
                    for h in (2 * hp, 2 * hp + 1):
                        if has(n, 0):
                            wait(act, score_ready, 16 * unit(n, 0) + 4 * sl + h + 1)
                            wait(act, pv_done, 4 * unit(n, 0) + sl - 1)
                            lo = sl * P if causal else 0
                            act.activation(prob[:, sl % 2, h, lo:SEQ], SC[:, h % 2, lo:SEQ], ACT.Exp,
                                           scale=float(HD) ** -0.5).then_inc(exp_done, 1)
                        if has(n, 3) and (p, h % 2) in STACK_COPIES:
                            rr, pair = divmod(STACK_COPIES.index((p, h % 2)), 2)
                            half = rr % 2
                            wait(act, mb_full, mb_count(n, rr))
                            copied = act.copy(
                                stack[0:SROWS, (w_ + 3) % 4, rr // 2, 2 * pair:2 * pair + 2,
                                      half * 2 * P:(half + 1) * 2 * P],
                                MB[0:SROWS, 4 * pair:4 * pair + 4, :].rearrange("p (h t) n -> p h (t n)", h=2))
                            if pair:
                                copied.then_inc(mb_free, 1)

            steps(act, step)

        @blk.vector
        def _(dve):
            dve.memset(vbuf[:, :, :, :, :].rearrange("p a t h d -> p (a t h d)"), 1.0).then_inc(init, 1)
            dve.memset(stack[96:P, :, :, :, :].rearrange("p a q h n -> p (a q h n)"), 1.0).then_inc(init, 1)
            if L0:
                dve.memset(neghalf[:, :], -0.5).then_inc(init, 1)
            else:
                dve.memset(qkw[:, :, :, :].rearrange("p a q n -> p (a q n)"), 0.0).then_inc(init, 1)
            dve.wait_ge(init, 3)

            def gate_factors(batch):
                for j in range(4):
                    dve.tensor_scalar(us[:, j, :], w["UT"][:, j, :], w["gS"][:, j, bass.ds(batch, 1)], None,
                                      ALU.mult).then_inc(us_done, 1)

            def ma_round(n, what):
                w_ = whole(n)
                i = w_ % CYCLE
                wait(dve, ma_full, ma_count(n, what) + 1)
                if what == "weff":
                    g = (i + 6) % GROUPS
                    dve.tensor_tensor(weff[:, :, :], MA[:, 0:KT * 3 * GW].rearrange("p (k n) -> p k n", k=KT),
                                      w["WB"][:, :, g, :], ALU.add).then_inc(ma_free, 1)
                elif what == "weffo":
                    dve.tensor_tensor(weffo[:, :, :], MA[:, :].rearrange("p (k n) -> p k n", k=KT)[:, :, 0:C],
                                      w["WoB"][:, :, :], ALU.add).then_inc(ma_free, 1)
                elif what == "proj":
                    kd = kind(i + 6)
                    g = (i + 6) % GROUPS
                    u = unit(n, 6)
                    ps = MA[:, :].rearrange("p (t n) -> p t n", t=TPB)
                    bias = w["b" + kd]
                    wait(dve, pool_norm, total(norm_steps, n))
                    if has(n, -1):
                        wait(dve, pv_done, 4 * unit(n, -1))
                    dve.tensor_tensor(
                        vbuf[:, (w_ + 6) % CYCLE, :, :, 0:HD],
                        ps[:, :, 2 * GW:3 * GW].rearrange("p t (h d) -> p t h d", h=GH),
                        bias[:, g, 2 * GW:3 * GW].rearrange("p (h d) -> p h d", h=GH).unsqueeze(1)
                        .to_broadcast([P, TPB, GH, HD]), ALU.add).then_inc(v_ready, 1)
                    for qk in range(2):
                        dve.tensor_tensor(
                            qkf[:, (w_ + 6) % 2, qk, :].rearrange("p (t n) -> p t n", t=TPB),
                            ps[:, :, qk * GW:(qk + 1) * GW],
                            bias[:, g, qk * GW:(qk + 1) * GW].unsqueeze(1).to_broadcast([P, TPB, GW]),
                            ALU.add).then_inc((qk_ready, ma_free)[qk], 1)
                elif what == "outproj":
                    res = MA[:, :].rearrange("p (t n) -> p t n", t=TPB)
                    if L0:
                        batch = (w_ - 9) // CYCLE if isinstance(n, int) else n[0] - 1
                        wait(dve, xin_biased, batch + 1)
                        dve.tensor_tensor(X[:, bass.ds(batch * TPB, TPB), :], res, xin[:, :, :],
                                          ALU.add).then_inc(ma_free, 1)
                    else:
                        batch = (w_ - 5) // UPB if isinstance(n, int) else 2 * n[0] + (n[1] - 5) // UPB
                        rows = X[:, bass.ds(batch * TPB, TPB), :]
                        dve.tensor_tensor(rows, res, rows, ALU.add).then_inc(ma_free, 1)
                elif what == "norm":
                    u = unit(n, -1)
                    g = (w_ - 1) % GROUPS
                    dst = onA if (w_ - 1) % CYCLE < GROUPS else onB
                    o = MA[:, 0:SEQ].rearrange("p (t h d) -> p t h d", t=TPB, h=GH)
                    dve.reciprocal(rsum[:, :, :], o[:, :, :, HD]).then_inc(recip_done, 1)
                    wait(dve, recip_done, u + 1)
                    dve.tensor_tensor(dst[:, :, g * GW:(g + 1) * GW].rearrange("p t (h d) -> p t h d", h=GH),
                                      o[:, :, :, 0:HD],
                                      rsum[:, :, :].unsqueeze(3).to_broadcast([P, TPB, GH, HD]),
                                      ALU.mult).then_inc(ma_free, 1)

            def squares_sum(n, j):
                k = total(a_units(5), n)
                if j == 1:
                    wait(dve, ss_ready, k + 1)
                    dve.tensor_scalar(ms[:, :], ms[:, :], 1.0 / HD, 1e-6, ALU.mult, ALU.add).then_inc(ms_ready, 1)
                    return
                wait(dve, sq_ready, k + 1)
                wait(dve, pool_norm, total(norm_steps, n))
                dve.tensor_reduce(ms[:, :], sq[:, :].rearrange("p (a d) -> p a d", d=HD), AX.X,
                                  ALU.add).then_inc(ss_ready, 1)

            def split(n, j):
                u = unit(n, 4)
                src = qkw[:, (whole(n) + 4) % 2, :, :]
                if j == 0:
                    wait(dve, pool_norm, total(norm_steps, n))
                    wait(dve, slots_done, 6 * u)
                    dve.tensor_copy(part[0][:, :, :], src).then_inc(split_done, 1)
                    return
                wait(dve, split_done, 4 * u + j)
                if j == 1:
                    ins = dve.tensor_tensor(rest[:, :, :], src, part[0][:, :, :], ALU.subtract)
                elif j == 2:
                    ins = dve.tensor_copy(part[1][:, :, :], rest[:, :, :])
                else:
                    ins = dve.tensor_tensor(part[2][:, :, :], rest[:, :, :], part[1][:, :, :], ALU.subtract)
                ins.then_inc(split_done, 1)

            def lay_slots(n, j):
                u = unit(n, 4)
                qk = j // 3
                src = [part[k][:, qk, :].rearrange("p (a d) -> p a d", d=HD) for k in range(3)]
                dst = slots[:, (whole(n) + 4) % 2, qk, :, :].rearrange("p a (s d) -> p a s d", d=HD)
                if j == 0:
                    wait(dve, split_done, 4 * (u + 1))
                    wait(dve, mb_full, mb_count(n))
                k = j % 3
                wide, at = ((3, slice(0, 3)), (3, slice(3, 6)), (1, slice(6, 7)),
                            (3, slice(0, 7, 3)), (2, slice(1, 5, 3)), (2, slice(2, 6, 3)))[j]
                dve.tensor_copy(dst[:, :, at, :], src[k].unsqueeze(2).to_broadcast([P, TPB * GH, wide, HD]))\
                   .then_inc(slots_done, 1)

            if L0:
                gate_factors(0)

            def step(n):
                w_ = whole(n)
                r = dict(rounds(w_))
                for p in range(8):
                    sl, hp = p // 2, p % 2
                    if p in r and r[p] not in ("xt", "ot"):
                        ma_round(n, r[p])
                    if L0 and p == 4 and w_ % CYCLE == 3 and 0 <= w_ < NU - CYCLE:
                        batch = w_ // CYCLE + 1 if isinstance(n, int) else n[0] + 1
                        wait(dve, ma_full, ma_count(back(n, 2), "weffo") + 1)
                        gate_factors(batch)
                    for h in (2 * hp, 2 * hp + 1):
                        m = 2 * p + h % 2
                        if has(n, 2):
                            u = unit(n, 2)
                            wait(dve, smax_ready, 16 * u + 4 * sl + h + 1)
                            if sl == 0 and h == 0:
                                wait(dve, mprep, 5 * unit(n, 1))
                            hi = (sl + 1) * P if causal else SEQ
                            dve.tensor_reduce(mx[:, (w_ + 2) % 2, sl * GH + h:sl * GH + h + 1],
                                              MX[:, h % 2, 0:hi], AX.X, ALU.max).then_inc(max_done, 1)
                        if m in (0, 2) and has(n, 5) and kind(w_ + 5) == "A":
                            squares_sum(n, m // 2)
                        if m in (1, 3, 5, 7) and has(n, 4):
                            split(n, m // 2)
                        if m in (8, 9, 11, 12, 13, 14) and has(n, 4):
                            lay_slots(n, (8, 9, 11, 12, 13, 14).index(m))

            steps(dve, step)

        @blk.gpsimd
        def _(pool):
            pool.memset(minus[:, :, :], -1.0).then_inc(pool_init, 1)
            pool.memset(carry[:, :], 0.0).then_inc(pool_init, 1)
            pool.wait_ge(pool_init, 2)
            pool.wait_ge(init, 3)

            def maxima(n):
                u = unit(n, 1)
                m = mx[:, (whole(n) + 1) % 2, :]
                wait(pool, max_done, 16 * (u + 1))
                if has(n, 0):
                    wait(pool, mb_full, mb_count(back(n, 1), "rows"))
                mv = m.rearrange("p (t h) -> p t h", t=TPB)
                rv = mres[:, :].rearrange("p (t h) -> p t h", t=TPB)
                pool.tensor_tensor(mparts[:, :, 0, :], mv, minus[:, :, :], ALU.mult).then_inc(mprep, 1)
                wait(pool, mprep, 5 * u + 1)
                pool.tensor_tensor(rv, mv, mparts[:, :, 0, :], ALU.add).then_inc(mprep, 1)
                wait(pool, mprep, 5 * u + 2)
                pool.tensor_tensor(mparts[:, :, 1, :], rv, minus[:, :, :], ALU.mult).then_inc(mprep, 1)
                wait(pool, mprep, 5 * u + 3)
                pool.tensor_tensor(rv, rv, mparts[:, :, 1, :], ALU.add).then_inc(mprep, 1)
                wait(pool, mprep, 5 * u + 4)
                pool.tensor_tensor(mparts[:, :, 2, :], rv, minus[:, :, :], ALU.mult).then_inc(mprep, 1)

            def norm_qk(n):
                w_ = whole(n)
                kd = kind(w_ + 5)
                u = unit(n, 5)
                src, dst = qkf[:, (w_ + 5) % 2, :, :], qkw[:, (w_ + 5) % 2, :, :]
                done = total(norm_steps, n)
                wait(pool, ma_free, ma_count(back(n, 1), "proj") + 1)
                wait(pool, pool_norm, done)
                wait(pool, split_done, 4 * unit(n, 4))
                if kd == "B":
                    pool.tensor_tensor(carry[:, 2:3], carry[:, 0:1], carry[:, 0:1], ALU.add)
                    pool.tensor_copy(dst, src).then_inc(pool_norm, 1)
                elif kd == "A":
                    wait(pool, ms_ready, total(a_units(5), n) + 1)
                    pool.tensor_tensor(rstd[:, :], ms[:, :], neghalf[:, :], ALU.pow).then_inc(pool_norm, 1)
                    wait(pool, pool_norm, done + 1)
                    d3 = dst.rearrange("p q (a d) -> p (q a) d", d=HD)
                    pool.tensor_tensor(d3, src.rearrange("p q (a d) -> p (q a) d", d=HD),
                                       rstd[:, :].unsqueeze(2).to_broadcast([P, 2 * TPB * GH, HD]),
                                       ALU.mult).then_inc(pool_norm, 1)
                    wait(pool, pool_norm, done + 2)
                    d4 = dst.rearrange("p q (a d) -> p q a d", d=HD)
                    pool.tensor_tensor(d4, d4, w["qkn"][:, :, :].unsqueeze(2)
                                       .to_broadcast([P, 2, TPB * GH, HD]), ALU.mult).then_inc(pool_norm, 1)
                else:
                    for qk in range(2):
                        ue = src[:, qk, :].rearrange("p (t h d e) -> p t h d e", t=TPB, h=GH, e=2)[:, :, :, :, 0]
                        uo = src[:, qk, :].rearrange("p (t h d e) -> p t h d e", t=TPB, h=GH, e=2)[:, :, :, :, 1]
                        r0 = rot[:, 0, :, :].rearrange("p (t h) d -> p t h d", t=TPB)
                        r1 = rot[:, 1, :, :].rearrange("p (t h) d -> p t h d", t=TPB)
                        cb = w["cos"][:, :, :].unsqueeze(2).to_broadcast([P, TPB, GH, HD // 2])
                        sb_ = w["sin"][:, :, :].unsqueeze(2).to_broadcast([P, TPB, GH, HD // 2])
                        pool.tensor_tensor(r0, ue, cb, ALU.mult).then_inc(pool_norm, 1)
                        pool.tensor_tensor(r1, uo, sb_, ALU.mult).then_inc(pool_norm, 1)
                        wait(pool, pool_norm, done + 3 * qk + 2)
                        out = dst[:, qk, :].rearrange("p (a d) -> p a d", d=HD)[:, :, 0:HD // 2]
                        pool.tensor_tensor(out, rot[:, 0, :, :], rot[:, 1, :, :],
                                           ALU.subtract).then_inc(pool_norm, 1)
                        wait(pool, pool_norm, done + 3 * qk + 3)

            def squares(n):
                u = unit(n, 6)
                wait(pool, ma_free, ma_count(n, "proj") + 1)
                wait(pool, ss_ready, total(a_units(6), n))
                src = qkf[:, (whole(n) + 6) % 2, :, :].rearrange("p q n -> p (q n)")
                pool.tensor_tensor(sq[:, :], src, src, ALU.mult).then_inc(sq_ready, 1)

            def step(n):
                w_ = whole(n)
                if has(n, 1):
                    maxima(n)
                if has(n, 5):
                    norm_qk(n)
                if L0 and w_ % CYCLE == 3 and 0 <= w_ < NU:
                    batch = w_ // CYCLE if isinstance(n, int) else n[0]
                    wait(pool, xin_loaded, 16 * (batch + 1))
                    pool.tensor_tensor(xin[:, :, :], xin[:, :, :],
                                       w["bout"][:, :].unsqueeze(1).to_broadcast([P, TPB, C]),
                                       ALU.add).then_inc(xin_biased, 1)
                if has(n, 6) and kind(w_ + 6) == "A":
                    squares(n)

            steps(pool, step)


def top_two(dve, link, vals, desc, eq, top, best, hot, rest):
    p_, g_, e_ = vals.shape
    cur = vals
    for k in range(2):
        link(dve.tensor_reduce(top[k], cur, AX.X, ALU.max))
        link(dve.tensor_tensor(eq, cur, top[k].unsqueeze(2).to_broadcast([p_, g_, e_]), ALU.is_equal))
        link(dve.tensor_tensor(eq, eq, desc, ALU.mult))
        link(dve.tensor_reduce(best, eq, AX.X, ALU.max))
        link(dve.tensor_tensor(hot[k], eq, best.unsqueeze(2).to_broadcast([p_, g_, e_]), ALU.is_equal))
        if k == 0:
            link(dve.tensor_scalar(eq, hot[0], NEG, None, ALU.mult))
            link(dve.tensor_tensor(rest, vals, eq, ALU.add))
            cur = rest


def gates(nc, XN, gate_w, gS, consts, S4):
    E, GHID = 8, 64
    with ExitStack() as s:
        def sb(nm, shape, dt=F32):
            return s.enter_context(nc.sbuf_tensor("gate_" + nm, shape, dt))

        pooled = sb("pooled", [P, KT, BATCH])
        mean = sb("mean", [P, 1])
        hid = sb("hid", [GHID, BATCH])
        logit = sb("logit", [BATCH, 1, E])
        eq = sb("eq", [BATCH, 1, E])
        rest = sb("rest", [BATCH, 1, E])
        hot = [sb(f"hot{k}", [BATCH, 1, E]) for k in range(2)]
        top = [sb(f"top{k}", [BATCH, 1]) for k in range(2)]
        best = sb("best", [BATCH, 1])
        gap, e2, den, g1, g2 = (sb(nm, [BATCH, 1]) for nm in ("gap", "e2", "den", "g1", "g2"))
        gate = sb("gate", [BATCH, E])
        gateT = sb("gateT", [E, BATCH])
        ps = s.enter_context(nc.psum_tensor("gate_ps", [P, 5, 512], F32))
        chain = s.enter_context(nc.semaphore("gate_chain"))
        mm_done = s.enter_context(nc.semaphore("gate_mm"))
        for_pe = s.enter_context(nc.semaphore("gate_for_pe"))
        exp_in = s.enter_context(nc.semaphore("gate_exp_in"))
        exp_out = s.enter_context(nc.semaphore("gate_exp_out"))
        blk = s.enter_context(nc.Block())

        @blk.tensor
        def _(pe):
            pe.wait_ge(for_pe, 1)
            for b in range(BATCH):
                for kt in range(KT):
                    for t in range(TPB):
                        mm = pe.matmul(ps[:, 0, kt * BATCH + b:kt * BATCH + b + 1],
                                       XN[:, b * TPB + t, kt * P:(kt + 1) * P], mean[:, :],
                                       start=(t == 0), stop=(t == TPB - 1))
            mm.then_inc(mm_done, 1)
            pe.wait_ge(for_pe, 2)
            for kt in range(KT):
                mm = pe.matmul(ps[0:GHID, 1, 0:BATCH], gate_w["gw1"][:, kt, :], pooled[:, kt, :],
                               start=(kt == 0), stop=(kt == KT - 1))
            mm.then_inc(mm_done, 1)
            pe.wait_ge(for_pe, 3)
            pe.matmul(ps[0:BATCH, 2, 0:E], hid[:, :], gate_w["gw2"][:, :], start=True, stop=True).then_inc(mm_done, 1)
            pe.wait_ge(for_pe, 4)
            pe.transpose(ps[0:E, 3, 0:BATCH], gate[:, :], consts["identf"][0:BATCH, 0:BATCH]).then_inc(mm_done, 1)
            pe.wait_ge(for_pe, 5)
            pe.matmul(ps[:, 4, 0:BATCH], gate_w["rep"][:, :], gateT[:, :], start=True, stop=True).then_inc(mm_done, 1)

        @blk.scalar
        def _(act):
            act.wait_ge(exp_in, 1)
            act.activation(e2[:, :], gap[:, :], ACT.Exp).then_inc(exp_out, 1)

        @blk.vector
        def _(dve):
            steps = [0]

            def link(ins):
                steps[0] += 1
                ins.then_inc(chain, 1)
                dve.wait_ge(chain, steps[0])

            dve.memset(mean[:, :], 1.0 / SEQ).then_inc(for_pe, 1)
            dve.wait_ge(mm_done, 1)
            dve.tensor_copy(pooled[:, :, :], ps[:, 0, 0:KT * BATCH].rearrange("p (k b) -> p k b", k=KT)).then_inc(for_pe, 1)
            dve.wait_ge(mm_done, 2)
            dve.tensor_scalar(hid[:, :], ps[0:GHID, 1, 0:BATCH], gate_w["gb1"][:, 0:1], 0.0, ALU.add,
                              ALU.max).then_inc(for_pe, 1)
            dve.wait_ge(mm_done, 3)
            link(dve.tensor_tensor(logit[:, 0, :], ps[0:BATCH, 2, 0:E], gate_w["gb2"][:, :], ALU.add))
            top_two(dve, link, logit[:, :, :], gate_w["desc8"][:, :].unsqueeze(1), eq[:, :, :],
                    [t[:, :] for t in top], best[:, :], [h[:, :, :] for h in hot], rest[:, :, :])
            dve.tensor_tensor(gap[:, :], top[1][:, :], top[0][:, :], ALU.subtract).then_inc(exp_in, 1)
            dve.wait_ge(exp_out, 1)
            link(dve.tensor_scalar(den[:, :], e2[:, :], 1.0, None, ALU.add))
            link(dve.reciprocal(g1[:, :], den[:, :]))
            link(dve.tensor_tensor(g2[:, :], g1[:, :], e2[:, :], ALU.mult))
            link(dve.tensor_scalar(gate[:, :], hot[0][:, 0, :], g1[:, 0:1], None, ALU.mult))
            dve.scalar_tensor_tensor(out=gate[:, :], in0=hot[1][:, 0, :], scalar=g2[:, 0:1], in1=gate[:, :],
                                     op0=ALU.mult, op1=ALU.add).then_inc(for_pe, 1)
            dve.wait_ge(mm_done, 4)
            dve.tensor_copy(gateT[:, :], ps[0:E, 3, 0:BATCH]).then_inc(for_pe, 1)
            dve.wait_ge(mm_done, 5)
            for j in range(4):
                dve.tensor_scalar(gS[:, j, :], ps[:, 4, 0:BATCH], S4[:, j:j + 1], None, ALU.mult)


def block_d(nc, X, XN, Z, logits, w, consts):
    S = BATCH
    KVH = 4
    QKV = C + 2 * KVH * HD
    Xv = X[:, :, :].rearrange("p (s t) c -> p s t c", t=TPB)
    XNv = XN[:, :, :].rearrange("p (s t) c -> p s t c", t=TPB)
    Zv = Z[:, :, :].rearrange("p (s t) c -> p s t c", t=TPB)
    Lv = logits[:, :, :].rearrange("p (s t) e -> p s t e", t=TPB)
    with ExitStack() as s_:
        def sb(nm, shape, dt=F32):
            return s_.enter_context(nc.sbuf_tensor("d_" + nm, shape, dt))

        def sem(nm):
            return s_.enter_context(nc.semaphore("d_" + nm))

        z = sb("z", [P, S, C])
        zT = sb("zT", [P, KT, S * P])
        q = sb("q", [P, S, C])
        k = sb("k", [P, S, C])
        v = sb("v", [P, S, C])
        prod = sb("prod", [P, S, C])
        prod2 = sb("prod2", [P, 2, S, C])
        sc = sb("sc", [P, S, S, HEADS])
        top = sb("top", [P, S, HEADS])
        den = sb("den", [P, S, HEADS])
        o = sb("o", [P, S, C])
        h = sb("h", [P, S, C])
        stats = sb("stats", [P, S, 6])
        mv = sb("mv", [P, S, 2])
        vare = sb("vare", [P, S])
        rstd = sb("rstd", [P, S])
        half = sb("half", [P, S])
        carry = sb("carry", [P, 2])
        T = s_.enter_context(nc.psum_tensor("d_T", [P, 2, 4, P], F32))
        Y = s_.enter_context(nc.psum_tensor("d_Y", [P, 4, 512], F32))

        t_full, t_free = sem("t_full"), sem("t_free")
        y_full, y_free = sem("y_full"), sem("y_free")
        chain = sem("chain")
        zw = sem("zw")
        kvq = sem("kvq")
        sc_ready, ex_ready = sem("sc_ready"), sem("ex_ready")
        pv_ready, pv_read = sem("pv_ready"), sem("pv_read")
        o_ready, h_ready = sem("o_ready"), sem("h_ready")
        var_ready, rstd_ready = sem("var_ready"), sem("rstd_ready")
        ln_ready = sem("ln_ready")
        half_done = sem("half_done")
        sc_init = sem("sc_init")
        TR = 3 * KT * S // 4
        YR = 3 * S
        DV = 1 + 3 + 1 + S * 2 + 4 + 1 + 2
        blk = s_.enter_context(nc.Block())

        @blk.tensor
        def _(pe):
            def body(b):
                tr = [0]
                yr = [0]

                def turn_over(src):
                    for kt in range(KT):
                        for half_ in range(2):
                            r = TR * b + tr[0]
                            if isinstance(r, int):
                                if r >= 2:
                                    pe.wait_ge(t_free, r - 1)
                            else:
                                pe.wait_ge(t_free, r - 1)
                            for j in range(4):
                                mm = pe.transpose(T[:, tr[0] % 2, j, :],
                                                  src[:, 4 * half_ + j, kt * P:(kt + 1) * P], consts["identf"][:, :])
                            mm.then_inc(t_full, 1)
                            tr[0] += 1
                    pe.wait_ge(t_free, TR * b + tr[0])

                def product(wt, width):
                    for s in range(S):
                        r = YR * b + yr[0]
                        if not isinstance(r, int) or r >= 4:
                            pe.wait_ge(y_free, r - 3)
                        for kt in range(KT):
                            mm = pe.matmul(Y[:, yr[0] % 4, 0:width], zT[:, kt, s * P:(s + 1) * P], wt[:, kt, :],
                                           start=(kt == 0), stop=(kt == KT - 1))
                        mm.then_inc(y_full, 1)
                        yr[0] += 1

                pe.wait_ge(zw, 2 * (b + 1))
                turn_over(z)
                product(w["qkv"], QKV)
                pe.wait_ge(o_ready, S * (b + 1))
                turn_over(o)
                product(w["proj"], C)
                pe.wait_ge(ln_ready, 2 * (b + 1))
                turn_over(o)
                product(w["router"], EXPERTS)

            body(0)
            with pe.Fori(1, TPB) as b:
                body(b)

        @blk.scalar
        def _(act):
            def body(b):
                def copy_back(part_):
                    for kt in range(KT):
                        for half_ in range(2):
                            r = 4 * part_ + 2 * kt + half_
                            act.wait_ge(t_full, TR * b + r + 1)
                            act.copy(zT[:, kt, half_ * 4 * P:(half_ + 1) * 4 * P],
                                     T[:, r % 2, :, :].rearrange("p j n -> p (j n)")).then_inc(t_free, 1)

                copy_back(0)
                for s in range(S):
                    act.wait_ge(y_full, YR * b + s + 1)
                    ps = Y[:, s % 4, :]
                    if s == 0:
                        if not isinstance(b, int) or b > 0:
                            act.wait_ge(o_ready, S * b)
                    act.copy(q[:, s, :], ps[:, 0:C]).then_inc(kvq, 1)
                    for dst, off in ((k, C), (v, C + KVH * HD)):
                        src = ps[:, off:off + KVH * HD].rearrange("p (g d) -> p g d", g=KVH)
                        act.copy(dst[:, s, :].rearrange("p (g r d) -> p g r d", g=KVH, d=HD),
                                 src.unsqueeze(2).to_broadcast([P, KVH, HEADS // KVH, HD]))\
                           .then_inc(kvq if dst is k else y_free, 1)
                act.wait_ge(sc_ready, b + 1)
                act.activation(sc[:, :, :, :].rearrange("p s m h -> p (s m h)"),
                               sc[:, :, :, :].rearrange("p s m h -> p (s m h)"), ACT.Exp,
                               scale=float(HD) ** -0.5).then_inc(ex_ready, 1)
                copy_back(1)
                copy_back(2)
                for s in range(S):
                    act.wait_ge(y_full, YR * b + 2 * S + s + 1)
                    act.copy(Lv[:, s, bass.ds(b, 1), :].rearrange("p t e -> p (t e)"),
                             Y[:, (2 * S + s) % 4, 0:EXPERTS]).then_inc(y_free, 1)

            body(0)
            with act.Fori(1, TPB) as b:
                body(b)

        @blk.gpsimd
        def _(pool):
            pool.memset(half[:, :], -0.5).then_inc(half_done, 1)
            pool.wait_ge(half_done, 1)

            def body(b):
                first = isinstance(b, int)
                zin = Zv[:, :, bass.ds(b, 1), :].rearrange("p s t c -> p s (t c)")
                if not first:
                    pool.wait_ge(t_full, TR * (b - 1) + 4)
                pool.tensor_tensor(z[:, :, :], zin, w["ln1w"][:, :].unsqueeze(1).to_broadcast([P, S, C]),
                                   ALU.mult).then_inc(zw, 1)
                pool.wait_ge(zw, 2 * b + 1)
                pool.tensor_tensor(z[:, :, :], z[:, :, :], w["ln1b"][:, :].unsqueeze(1).to_broadcast([P, S, C]),
                                   ALU.add).then_inc(zw, 1)
                pool.wait_ge(ex_ready, b + 1)
                for s in range(S):
                    m = s + 1
                    g = S * b + s
                    if not first or s >= 2:
                        pool.wait_ge(pv_read, g - 1)
                    pool.tensor_tensor(
                        prod2[:, s % 2, 0:m, :].rearrange("p m (h d) -> p (m h) d", d=HD),
                        v[:, 0:m, :].rearrange("p m (h d) -> p (m h) d", d=HD),
                        sc[:, s, 0:m, :].rearrange("p m h -> p (m h)").unsqueeze(2)
                        .to_broadcast([P, m * HEADS, HD]), ALU.mult).then_inc(pv_ready, 1)
                pool.wait_ge(var_ready, b + 1)
                pool.tensor_tensor(rstd[:, :], vare[:, :], half[:, :], ALU.pow).then_inc(rstd_ready, 1)

            body(0)
            with pool.Fori(1, TPB) as b:
                body(b)

        @blk.vector
        def _(dve):
            dve.memset(carry[:, :], 0.0).then_inc(sc_init, 1)
            dve.memset(sc[:, :, :, :].rearrange("p s m h -> p (s m h)"), NEG).then_inc(sc_init, 1)

            def body(b, per):
                first = isinstance(b, int)
                n = [0]

                def link(ins):
                    n[0] += 1
                    ins.then_inc(chain, 1)
                    dve.wait_ge(chain, per * b + n[0])

                if not first:
                    dve.wait_ge(pv_ready, S * b)
                    link(dve.memset(sc[:, :, :, :].rearrange("p s m h -> p (s m h)"), NEG))
                else:
                    dve.wait_ge(sc_init, 2)
                    link(dve.memset(top[:, :, :], 0.0))
                dve.wait_ge(y_free, YR * b + S)
                for s in range(S):
                    m = s + 1
                    link(dve.tensor_tensor(prod[:, 0:m, :], k[:, 0:m, :],
                                           q[:, s, :].unsqueeze(1).to_broadcast([P, m, C]), ALU.mult))
                    link(dve.tensor_reduce(sc[:, s, 0:m, :].rearrange("p m h -> p (m h)"),
                                           prod[:, 0:m, :].rearrange("p m (h d) -> p (m h) d", d=HD),
                                           AX.X, ALU.add))
                by_key = sc[:, :, :, :].rearrange("p s m h -> p s h m")
                link(dve.tensor_reduce(top[:, :, :], by_key, AX.X, ALU.max))
                dve.tensor_tensor(sc[:, :, :, :], sc[:, :, :, :],
                                  top[:, :, :].unsqueeze(2).to_broadcast([P, S, S, HEADS]),
                                  ALU.subtract).then_inc(sc_ready, 1)
                dve.wait_ge(ex_ready, b + 1)
                link(dve.tensor_reduce(top[:, :, :], by_key, AX.X, ALU.add))
                link(dve.reciprocal(den[:, :, :], top[:, :, :]))
                if not first:
                    dve.wait_ge(t_full, TR * b)
                for s in range(S):
                    m = s + 1
                    dve.wait_ge(pv_ready, S * b + s + 1)
                    dve.tensor_reduce(h[:, s, :], prod2[:, s % 2, 0:m, :].rearrange("p m c -> p c m"),
                                      AX.X, ALU.add).then_inc(pv_read, 1)
                    dve.wait_ge(pv_read, S * b + s + 1)
                    dve.tensor_tensor(o[:, s, :].rearrange("p (h d) -> p h d", d=HD),
                                      h[:, s, :].rearrange("p (h d) -> p h d", d=HD),
                                      den[:, s, :].unsqueeze(2).to_broadcast([P, HEADS, HD]),
                                      ALU.mult).then_inc(o_ready, 1)
                for s in range(S):
                    dve.wait_ge(y_full, YR * b + S + s + 1)
                    if s == 0:
                        dve.wait_ge(o_ready, S * (b + 1))
                    dve.tensor_tensor(h[:, s, :], Y[:, (S + s) % 4, 0:C],
                                      XNv[:, s, bass.ds(b, 1), :].rearrange("p t c -> p (t c)"),
                                      ALU.add).then_inc(y_free, 1)
                    dve.wait_ge(y_free, YR * b + S + s + 1)
                    dve.bn_stats(stats[:, s, :], h[:, s, :]).then_inc(h_ready, 1)
                dve.wait_ge(h_ready, S * (b + 1))
                dve.tensor_copy(carry[:, 1:2], carry[:, 0:1])
                for s in range(S):
                    ins = dve.bn_aggr(mv[:, s, :], stats[:, s, :])
                link(ins)
                dve.tensor_scalar(vare[:, :], mv[:, :, 1], 1e-5, None, ALU.add).then_inc(var_ready, 1)
                xo = Xv[:, :, bass.ds(b, 1), :].rearrange("p s t c -> p s (t c)")
                link(dve.tensor_tensor(xo, xo, h[:, :, :], ALU.add))
                dve.tensor_tensor(xo, xo, w["bo"][:, :].unsqueeze(1).to_broadcast([P, S, C]), ALU.add)
                dve.wait_ge(rstd_ready, b + 1)
                for s in range(S):
                    ins = dve.tensor_scalar(h[:, s, :], h[:, s, :], mv[:, s, 0:1], rstd[:, s:s + 1],
                                            ALU.subtract, ALU.mult)
                link(ins)
                dve.tensor_tensor(o[:, :, :], h[:, :, :], w["ln2w"][:, :].unsqueeze(1).to_broadcast([P, S, C]),
                                  ALU.mult).then_inc(ln_ready, 1)
                dve.wait_ge(ln_ready, 2 * b + 1)
                dve.tensor_tensor(o[:, :, :], o[:, :, :], w["ln2b"][:, :].unsqueeze(1).to_broadcast([P, S, C]),
                                  ALU.add).then_inc(ln_ready, 1)
                dve.wait_ge(ln_ready, 2 * b + 2)
                link(dve.tensor_copy(Zv[:, :, bass.ds(b, 1), :].rearrange("p s t c -> p s (t c)"), o[:, :, :]))
                return n[0]

            per = 1 + 2 * S + 1 + 2 + 1 + 1 + 1 + 1
            assert body(0, per) == per
            with dve.Fori(1, TPB) as b:
                body(b, per)


def route(nc, logits, slot_id, gather_id, gate, consts):
    G, E = NT, EXPERTS
    with ExitStack() as s:
        def sb(nm, shape, dt=F32):
            return s.enter_context(nc.sbuf_tensor("r_" + nm, shape, dt))

        prb = sb("prb", [P, G, E])
        eq = sb("eq", [P, G, E])
        rest = sb("rest", [P, G, E])
        hot = [sb(f"hot{k}", [P, G, E]) for k in range(2)]
        top = [sb(f"top{k}", [P, G]) for k in range(2)]
        best = sb("best", [P, G])
        member = sb("member", [P, G * E], BF16)
        run = [sb(f"run{k}", [P, G, E]) for k in range(2)]
        place = sb("place", [P, G])
        expert = sb("expert", [P, G])
        keep = sb("keep", [P, G])
        lost = sb("lost", [P, G])
        ps = s.enter_context(nc.psum_tensor("r_ps", [P, 2, G * E], F32))
        chain = s.enter_context(nc.semaphore("r_chain"))
        exp_in, exp_out = s.enter_context(nc.semaphore("r_exp_in")), s.enter_context(nc.semaphore("r_exp_out"))
        mem_ready, cum_ready = s.enter_context(nc.semaphore("r_mem")), s.enter_context(nc.semaphore("r_cum"))
        blk = s.enter_context(nc.Block())

        @blk.scalar
        def _(act):
            act.wait_ge(exp_in, 1)
            act.activation(prb[:, :, :], prb[:, :, :], ACT.Exp).then_inc(exp_out, 1)

        @blk.tensor
        def _(pe):
            pe.wait_ge(mem_ready, 1)
            pe.matmul(ps[:, 0, :], consts["before"][:, :], member[:, :], start=True, stop=True)
            pe.matmul(ps[:, 1, :], consts["ones"][:, :], member[:, :], start=True, stop=True).then_inc(cum_ready, 1)

        @blk.vector
        def _(dve):
            steps = [0]

            def link(ins):
                steps[0] += 1
                ins.then_inc(chain, 1)
                dve.wait_ge(chain, steps[0])

            def wide(x):
                return x.unsqueeze(2).to_broadcast([P, G, E])

            link(dve.tensor_reduce(top[0][:, :], logits[:, :, :], AX.X, ALU.max))
            dve.tensor_tensor(prb[:, :, :], logits[:, :, :], wide(top[0][:, :]), ALU.subtract).then_inc(exp_in, 1)
            dve.wait_ge(exp_out, 1)
            link(dve.tensor_reduce(best[:, :], prb[:, :, :], AX.X, ALU.add))
            link(dve.reciprocal(best[:, :], best[:, :]))
            link(dve.tensor_tensor(prb[:, :, :], prb[:, :, :], wide(best[:, :]), ALU.mult))
            top_two(dve, link, prb[:, :, :], consts["desc16"][:, :].unsqueeze(1).to_broadcast([P, G, E]),
                    eq[:, :, :], [t[:, :] for t in top], best[:, :], [x[:, :, :] for x in hot], rest[:, :, :])
            dve.tensor_tensor(member[:, :].rearrange("p (g e) -> p g e", e=E), hot[0][:, :, :], hot[1][:, :, :],
                              ALU.add).then_inc(mem_ready, 1)
            dve.wait_ge(cum_ready, 1)
            link(dve.tensor_copy(run[0][:, :, :], ps[:, 1, :].rearrange("p (g e) -> p g e", e=E)))
            a, b, d = 0, 1, 1
            while d < G:
                link(dve.tensor_tensor(run[b][:, d:G, :], run[a][:, d:G, :], run[a][:, 0:G - d, :], ALU.add))
                link(dve.tensor_copy(run[b][:, 0:d, :], run[a][:, 0:d, :]))
                a, b, d = b, a, 2 * d
            link(dve.tensor_copy(run[b][:, 0, :], ps[:, 0, 0:E]))
            link(dve.tensor_tensor(run[b][:, 1:G, :], run[a][:, 0:G - 1, :],
                                   ps[:, 0, :].rearrange("p (g e) -> p g e", e=E)[:, 1:G, :], ALU.add))
            for k in range(2):
                link(dve.tensor_tensor(eq[:, :, :], run[b][:, :, :], hot[k][:, :, :], ALU.mult))
                link(dve.tensor_reduce(place[:, :], eq[:, :, :], AX.X, ALU.add))
                link(dve.tensor_tensor(eq[:, :, :], hot[k][:, :, :],
                                       consts["base16"][:, :].unsqueeze(1).to_broadcast([P, G, E]), ALU.mult))
                link(dve.tensor_reduce(expert[:, :], eq[:, :, :], AX.X, ALU.add))
                link(dve.tensor_scalar(keep[:, :], place[:, :], float(CAP), None, ALU.is_lt))
                link(dve.tensor_tensor(place[:, :], place[:, :], expert[:, :], ALU.add))
                link(dve.tensor_tensor(gate[:, :, k], top[k][:, :], keep[:, :], ALU.mult))
                link(dve.tensor_tensor(place[:, :], place[:, :], keep[:, :], ALU.mult))
                link(dve.tensor_copy(gather_id[:, :, k], place[:, :]))
                link(dve.tensor_scalar(lost[:, :], keep[:, :], -float(2 * SLOTROWS), float(2 * SLOTROWS),
                                       ALU.mult, ALU.add))
                link(dve.tensor_tensor(lost[:, :], place[:, :], lost[:, :], ALU.add))
                link(dve.tensor_copy(slot_id[:, :, k], lost[:, :]))


def experts(nc, X, Z, slot_id, gather_id, gate, consts, dram):
    E = EXPERTS
    FT = FFN // P
    with ExitStack() as s:
        def sb(nm, shape, dt=F32):
            return s.enter_context(nc.sbuf_tensor("e_" + nm, shape, dt))

        def sem(nm):
            return s.enter_context(nc.semaphore("e_" + nm))

        scattered = sem("scattered")
        blk = s.enter_context(nc.Block())

        @blk.gpsimd
        def _(pool):
            for j in range(NT):
                for k in range(TOPK):
                    pool.indirect_dma_start(dram["rows"], bass.IndirectOffsetOnAxis(ap=slot_id[:, j, k:k + 1], axis=0),
                                            Z[:, j, :], None, bounds_check=SLOTROWS - 1,
                                            oob_is_err=False).then_inc(scattered, 16)
            pool.wait_ge(scattered, 16 * NT * TOPK)

    with ExitStack() as s:
        def sb(nm, shape, dt=F32):
            return s.enter_context(nc.sbuf_tensor("e_" + nm, shape, dt))

        def sem(nm):
            return s.enter_context(nc.semaphore("e_" + nm))

        w1 = sb("w1", [P, 2, KT, FFN])
        w2 = sb("w2", [P, 2, FT, C])
        rows = sb("rows", [P, 2, CT, C])
        rowsT = sb("rowsT", [P, KT, CAP])
        hid = sb("hid", [P, FT, CAP])
        outs = sb("outs", [P, 2, CT, C])
        OT = s.enter_context(nc.psum_tensor("e_OT", [P, 4, 512], F32))
        HB = s.enter_context(nc.psum_tensor("e_HB", [P, 2, 2, 512], F32))
        HC = CAP // 2
        loaded = [sem("loaded0"), sem("loaded1")]
        t_full, t_free = sem("t_full"), sem("t_free")
        h_full, h_free = sem("h_full"), sem("h_free")
        o_full, o_free = sem("o_full"), sem("o_free")
        stored = [sem("stored0"), sem("stored1")]
        blk = s.enter_context(nc.Block())

        def turns(eng, body):
            for e in range(2):
                body(e, e)
            with eng.Fori(1, E // 2) as pair:
                for e in range(2):
                    body(2 * pair + e, e, pair)

        @blk.sync
        def _(sp):
            def body(e, par, pair=None):
                if pair is not None:
                    sp.wait_ge(o_full, CT * (e - 1))
                sp.dma_start(w1[:, par, :, :], dram["w1"][:, bass.ds(e, 1), :, :].rearrange("p e k f -> p (e k) f"))\
                  .then_inc(loaded[par], 16)
                sp.dma_start(w2[:, par, :, :], dram["w2"][:, bass.ds(e, 1), :, :].rearrange("p e k c -> p (e k) c"))\
                  .then_inc(loaded[par], 16)
                sp.dma_start(rows[:, par, :, :], dram["rows_v"][:, bass.ds(CT * e, CT), :]).then_inc(loaded[par], 16)

            turns(sp, body)

        @blk.gpsimd
        def _(pool):
            def body(e, par, pair=None):
                pool.wait_ge(o_free, CT * (e + 1))
                pool.dma_start(dram["outs_v"][:, bass.ds(CT * e, CT), :], outs[:, par, :, :]).then_inc(stored[par], 16)

            turns(pool, body)
            for par in range(2):
                pool.wait_ge(stored[par], 16 * (E // 2))

        @blk.tensor
        def _(pe):
            def body(e, par, pair=None):
                first = pair is None and e == 0
                count = 1 if pair is None else pair + 1
                pe.wait_ge(loaded[par], 48 * count)
                if not first:
                    pe.wait_ge(o_free, CT * e)
                for kt in range(KT):
                    if kt:
                        pe.wait_ge(t_free, KT * e + 1)
                    for c in range(CT):
                        mm = pe.transpose(OT[:, c // 4, (c % 4) * P:(c % 4 + 1) * P],
                                          rows[:, par, c, kt * P:(kt + 1) * P], consts["identf"][:, :])
                    mm.then_inc(t_full, 1)
                pe.wait_ge(t_free, KT * (e + 1))
                for f in range(FT):
                    r = FT * e + f
                    if not (first and f < 2):
                        pe.wait_ge(h_free, r - 1)
                    for half_ in range(2):
                        for kt in range(KT):
                            mm = pe.matmul(HB[:, f % 2, half_, 0:HC], w1[:, par, kt, f * P:(f + 1) * P],
                                           rowsT[:, kt, half_ * HC:(half_ + 1) * HC],
                                           start=(kt == 0), stop=(kt == KT - 1))
                    mm.then_inc(h_full, 1)
                pe.wait_ge(h_free, FT * (e + 1))
                for c in range(CT):
                    if c == 4:
                        pe.wait_ge(o_free, CT * e + 1)
                    for f in range(FT):
                        mm = pe.matmul(OT[:, c % 4, 0:C], hid[:, f, c * P:(c + 1) * P], w2[:, par, f, :],
                                       start=(f == 0), stop=(f == FT - 1))
                    mm.then_inc(o_full, 1)

            turns(pe, body)

        @blk.scalar
        def _(act):
            def body(e, par, pair=None):
                for f in range(FT):
                    act.wait_ge(h_full, FT * e + f + 1)
                    act.activation(hid[:, f, :].rearrange("p (a n) -> p a n", a=2), HB[:, f % 2, :, 0:HC],
                                   ACT.Gelu_apprx_tanh).then_inc(h_free, 1)

            turns(act, body)

        @blk.vector
        def _(dve):
            def body(e, par, pair=None):
                for kt in range(KT):
                    dve.wait_ge(t_full, KT * e + kt + 1)
                    dve.tensor_copy(rowsT[:, kt, :], OT[:, 0:2, :].rearrange("p a n -> p (a n)")[:, 0:CAP])\
                       .then_inc(t_free, 1)
                for c in range(CT):
                    dve.wait_ge(o_full, CT * e + c + 1)
                    if c == 0 and pair is not None:
                        dve.wait_ge(stored[par], 16 * pair)
                    dve.tensor_copy(outs[:, par, c, :], OT[:, c % 4, 0:C]).then_inc(o_free, 1)

            turns(dve, body)

    with ExitStack() as s:
        RING = 4
        got = s.enter_context(nc.sbuf_tensor("m_got", [P, RING, TOPK, C], F32))
        got_sem = [s.enter_context(nc.semaphore(f"m_got{r}")) for r in range(RING)]
        added = s.enter_context(nc.semaphore("m_added"))
        blk = s.enter_context(nc.Block())

        @blk.gpsimd
        def _(pool):
            for j in range(NT):
                if j >= RING:
                    pool.wait_ge(added, 2 * (j - RING + 1))
                for k in range(TOPK):
                    pool.indirect_dma_start(got[:, j % RING, k, :], None, dram["outs"],
                                            bass.IndirectOffsetOnAxis(ap=gather_id[:, j, k:k + 1], axis=0),
                                            bounds_check=SLOTROWS - 1, oob_is_err=False)\
                        .then_inc(got_sem[j % RING], 16)

        @blk.vector
        def _(dve):
            for j in range(NT):
                dve.wait_ge(got_sem[j % RING], 32 * (j // RING + 1))
                for k in range(TOPK):
                    dve.scalar_tensor_tensor(out=X[:, j, :], in0=got[:, j % RING, k, :], scalar=gate[:, j, k:k + 1],
                                             in1=X[:, j, :], op0=ALU.mult, op1=ALU.add).then_inc(added, 1)
                    if k == 0:
                        dve.wait_ge(added, 2 * j + 1)


def two_layers(nc, d, out):
    rows_d = nc.dram_tensor("expert_rows", (SLOTROWS, C), F32, kind="Internal").ap()
    outs_d = nc.dram_tensor("expert_outs", (SLOTROWS, C), F32, kind="Internal").ap()
    out_v = out.rearrange("b (t p) c -> p (b t) c", p=P)
    x_v = d["x"].rearrange("b (t p) c -> p (b t) c", p=P)
    with ExitStack() as s:
        def sb(nm, shape, dt=F32, st=s):
            return st.enter_context(nc.sbuf_tensor(nm, shape, dt))

        X = sb("X", [P, NT, C])
        identf = sb("identf", [P, P])
        identb = sb("identb", [P, P], BF16)
        mask_kq = sb("mask_kq", [P, P], BF16)
        mask_qk = sb("mask_qk", [P, P], BF16)
        before = sb("before", [P, P], BF16)
        ones = sb("ones", [P, P], BF16)
        desc16 = sb("desc16", [P, EXPERTS])
        base16 = sb("base16", [P, EXPERTS])
        consts = dict(identf=identf, identb=identb, mask_kq=mask_kq, mask_qk=mask_qk, before=before,
                      ones=ones, desc16=desc16, base16=base16)
        zeroed = s.enter_context(nc.semaphore("zeroed"))

        with ExitStack() as l0:
            w = {}
            w["WA"] = sb("WA", [P, KT, GROUPS, 3 * GW], st=l0)
            w["WB"] = sb("WB", [P, KT, GROUPS, 3 * GW], st=l0)
            w["WoA"] = sb("WoA", [P, KT, C], st=l0)
            w["WoB"] = sb("WoB", [P, KT, C], st=l0)
            w["V"] = sb("V", [P, 4, C], st=l0)
            w["UT"] = sb("UT", [P, 4, C], st=l0)
            w["gS"] = sb("gS", [P, 4, BATCH], st=l0)
            w["bA"] = sb("bA", [P, GROUPS, 3 * GW], st=l0)
            w["bB"] = sb("bB", [P, GROUPS, 3 * GW], st=l0)
            w["bout"] = sb("bout", [P, C], st=l0)
            w["qkn"] = sb("qkn", [P, 2, HD], st=l0)
            with ExitStack() as g0:
                zeros = sb("zeros", [P, 2048], st=g0)
                stage = sb("stage", [P, 5, P], st=g0)
                b2 = sb("b2", [P, C], st=g0)
                S4 = sb("S4", [P, 4], st=g0)
                gw = dict(gw1=sb("gw1", [P, KT, 64], st=g0), gw2=sb("gw2", [64, 8], st=g0),
                          gb1=sb("gb1", [64, 1], st=g0), gb2=sb("gb2", [BATCH, 8], st=g0),
                          rep=sb("rep", [8, P], st=g0), desc8=sb("desc8", [BATCH, 8], st=g0))
                with ExitStack() as q:
                    x_in = q.enter_context(nc.semaphore("x_in"))
                    w_in = q.enter_context(nc.semaphore("w_in"))
                    z_set = q.enter_context(nc.semaphore("z_set"))
                    blk = q.enter_context(nc.Block())

                    @blk.sync
                    def _(sp):
                        for b in range(4):
                            sp.dma_start(X[:, 8 * b:8 * b + 8, :], x_v[:, 8 * b:8 * b + 8, :]).then_inc(x_in, 16)
                        sp.wait_ge(x_in, 64)

                    @blk.scalar
                    def _(act):
                        loads = [(stage[:, :, :], d["c_stage"]), (identf[:, :], d["c_ident"]),
                                 (desc16[:, :], d["c_desc16"].partition_broadcast(P)),
                                 (base16[:, :], d["c_base16"].partition_broadcast(P)),
                                 (w["WA"][:, :, :, :], d["WA"].rearrange("(k p) g n -> p k g n", p=P)),
                                 (w["WB"][:, :, :, :], d["WB"].rearrange("(k p) g n -> p k g n", p=P)),
                                 (w["WoA"][:, :, :], d["WoA"].rearrange("(k p) n -> p k n", p=P)),
                                 (w["WoB"][:, :, :], d["WoB"].rearrange("(k p) n -> p k n", p=P)),
                                 (w["V"][:, :, :], d["V4"].rearrange("j p n -> p j n")),
                                 (w["UT"][:, :, :], d["UT4"].rearrange("j p n -> p j n")),
                                 (w["bA"][:, :, :], d["bA"].partition_broadcast(P)),
                                 (w["bB"][:, :, :], d["bB"].partition_broadcast(P)),
                                 (w["bout"][:, :], d["boA"].partition_broadcast(P)),
                                 (b2[:, :], d["boB"].partition_broadcast(P)),
                                 (w["qkn"][:, 0, :], d["qn"].partition_broadcast(P)),
                                 (w["qkn"][:, 1, :], d["kn"].partition_broadcast(P)),
                                 (S4[:, :], d["S4"]),
                                 (gw["gw1"][:, :, :], d["gw1T"].rearrange("(k p) n -> p k n", p=P)),
                                 (gw["gw2"][:, :], d["gw2T"]), (gw["gb1"][:, :], d["gb1"]),
                                 (gw["gb2"][:, :], d["gb2"].partition_broadcast(BATCH)),
                                 (gw["rep"][:, :], d["c_rep"]),
                                 (gw["desc8"][:, :], d["c_desc8"].partition_broadcast(BATCH))]
                        for dst, src in loads:
                            act.dma_start(dst, src).then_inc(w_in, 16)
                        act.wait_ge(w_in, 16 * len(loads))

                    @blk.vector
                    def _(dve):
                        dve.memset(zeros[:, :], 0.0).then_inc(z_set, 1)
                        dve.memset(ones[:, :], 1.0)
                        dve.wait_ge(w_in, 16 * 23)
                        for dst, j in ((identb, 0), (mask_kq, 1), (mask_qk, 2), (before, 3)):
                            dve.tensor_copy(dst[:, :], stage[:, j, :])
                        dve.tensor_tensor(w["bout"][:, :], w["bout"][:, :], b2[:, :], ALU.add)

                    @blk.gpsimd
                    def _(pool):
                        pool.wait_ge(z_set, 1)
                        zv = rows_d.rearrange("(a p q) c -> a p (q c)", p=P, q=8)
                        for a in range(SLOTROWS // (8 * P)):
                            pool.dma_start(zv[a], zeros[:, :]).then_inc(zeroed, 16)
                        pool.wait_ge(zeroed, 16 * (SLOTROWS // (8 * P)))

                layernorm(nc, s, "ln0", X, X, 1e-5)
                gates(nc, X, gw, w["gS"], consts, S4)
            attention(nc, "L0", 0, X, X, w, consts, dict(x=x_v))

        XN = sb("XN", [P, NT, C])
        layernorm(nc, s, "ln1", X, XN, 1e-5)
        with ExitStack() as m:
            Z = sb("Z", [P, NT, C], st=m)
            logits = sb("logits", [P, NT, EXPERTS], st=m)
            slot_id = sb("slot_id", [P, NT, TOPK], U32, st=m)
            gather_id = sb("gather_id", [P, NT, TOPK], U32, st=m)
            gate = sb("gate", [P, NT, TOPK], st=m)
            layernorm(nc, s, "ln2", XN, Z, 1e-5)
            with ExitStack() as q:
                w = dict(qkv=sb("Dqkv", [P, KT, C + 8 * HD], st=q), proj=sb("Dproj", [P, KT, C], st=q),
                         router=sb("Drouter", [P, KT, EXPERTS], st=q), ln1w=sb("Dln1w", [P, C], st=q),
                         ln1b=sb("Dln1b", [P, C], st=q), ln2w=sb("Dln2w", [P, C], st=q),
                         ln2b=sb("Dln2b", [P, C], st=q), bo=sb("Dbo", [P, C], st=q))
                with ExitStack() as q2:
                    w_in = q2.enter_context(nc.semaphore("d_w_in"))
                    blk = q2.enter_context(nc.Block())

                    @blk.sync
                    def _(sp):
                        for dst, src in ((w["qkv"], "DqkvT"), (w["proj"], "DprojT"), (w["router"], "DrouterT")):
                            sp.dma_start(dst[:, :, :], d[src].rearrange("(k p) n -> p k n", p=P)).then_inc(w_in, 16)
                        for dst, src in ((w["ln1w"], "ln1w"), (w["ln1b"], "ln1b"), (w["ln2w"], "ln2w"),
                                         (w["ln2b"], "ln2b"), (w["bo"], "boC")):
                            sp.dma_start(dst[:, :], d[src].partition_broadcast(P)).then_inc(w_in, 16)
                        sp.wait_ge(w_in, 16 * 8)

                block_d(nc, X, XN, Z, logits, w, consts)
            route(nc, logits, slot_id, gather_id, gate, consts)
            experts(nc, X, Z, slot_id, gather_id, gate, consts,
                    dict(w1=d["w1T"].rearrange("e (k p) f -> p e k f", p=P),
                         w2=d["w2T"].rearrange("e (k p) c -> p e k c", p=P), rows=rows_d, outs=outs_d,
                         rows_v=rows_d.rearrange("(t p) c -> p t c", p=P),
                         outs_v=outs_d.rearrange("(t p) c -> p t c", p=P)))
        with ExitStack() as q:
            w = dict(WC=sb("WC", [P, KT, GROUPS, 3 * GW], st=q), WoC=sb("WoC", [P, KT, C], st=q),
                     bC=sb("bC", [P, GROUPS, 3 * GW], st=q), cos=sb("cos", [P, TPB, HD // 2], st=q),
                     sin=sb("sin", [P, TPB, HD // 2], st=q))
            with ExitStack() as q2:
                w_in = q2.enter_context(nc.semaphore("c_w_in"))
                blk = q2.enter_context(nc.Block())

                @blk.sync
                def _(sp):
                    sp.dma_start(w["WC"][:, :, :, :], d["WC"].rearrange("(k p) g n -> p k g n", p=P)).then_inc(w_in, 16)
                    sp.dma_start(w["WoC"][:, :, :], d["WoC"].rearrange("(k p) n -> p k n", p=P)).then_inc(w_in, 16)
                    sp.dma_start(w["bC"][:, :, :], d["bC"].partition_broadcast(P)).then_inc(w_in, 16)
                    sp.dma_start(w["cos"][:, :, :], d["c_cos"].rearrange("(t p) n -> p t n", p=P)).then_inc(w_in, 16)
                    sp.dma_start(w["sin"][:, :, :], d["c_sin"].rearrange("(t p) n -> p t n", p=P)).then_inc(w_in, 16)
                    sp.wait_ge(w_in, 16 * 5)

            attention(nc, "L1", 1, X, XN, w, consts, dict(out=out_v))


def kernel(**inputs):
    import numpy as np
    import concourse.bacc as _bacc
    from concourse import mybir as _mybir
    from concourse.bass_utils import run_bass_kernel_spmd as _run

    a = {k: np.asarray(v) for k, v in inputs.items()}

    def grouped(parts):
        return np.stack([m.reshape(m.shape[0], GROUPS, GW) for m in parts], axis=2).reshape(-1, GROUPS, 3 * GW)

    def grouped_bias(parts):
        return np.stack([m.reshape(GROUPS, GW) for m in parts], axis=1).reshape(GROUPS, 3 * GW)

    n = {}
    n["x"] = a["L0_attn_x"]
    wa = a["L0_attn_W_qkv"]
    n["WA"] = grouped([wa[:, 0:C], wa[:, C:2 * C], wa[:, 2 * C:]])
    ba = a["L0_attn_b_qkv"]
    n["bA"] = grouped_bias([ba[0:C], ba[C:2 * C], ba[2 * C:]])
    n["WoA"] = a["L0_attn_W_proj"]
    n["boA"] = a["L0_attn_b_proj"]
    n["qn"], n["kn"] = a["L0_attn_qn_w"], a["L0_attn_kn_w"]
    n["WB"] = grouped([a[f"L0_ffn_{p}Wm"].T for p in "qkv"])
    n["bB"] = grouped_bias([a[f"L0_ffn_{p}b"] for p in "qkv"])
    n["WoB"] = a["L0_ffn_oWm"].T
    n["boB"] = a["L0_ffn_ob"]
    n["V4"] = np.stack([a[f"L0_ffn_{p}V"].reshape(P, C) for p in "qkvo"])
    n["UT4"] = np.stack([a[f"L0_ffn_{p}U"].transpose(0, 2, 1).reshape(P, C) for p in "qkvo"])
    n["S4"] = np.stack([a[f"L0_ffn_{p}S"].reshape(P) for p in "qkvo"], axis=1)
    n["gw1T"], n["gw2T"] = a["L0_ffn_gw1"].T, a["L0_ffn_gw2"].T
    n["gb1"], n["gb2"] = a["L0_ffn_gb1"].reshape(-1, 1), a["L0_ffn_gb2"]
    n["WC"] = grouped([a[f"L1_attn_W{p}"].T for p in "qkv"])
    n["bC"] = grouped_bias([a[f"L1_attn_b{p}"] for p in "qkv"])
    n["WoC"], n["boC"] = a["L1_attn_Wo"].T, a["L1_attn_bo"]
    n["DqkvT"] = a["L1_ffn_qkv_weight"].T
    n["DprojT"] = a["L1_ffn_proj_weight"].T
    n["DrouterT"] = a["L1_ffn_router_weight"].T
    for m in ("ln1", "ln2"):
        n[m + "w"], n[m + "b"] = a[f"L1_ffn_{m}_weight"], a[f"L1_ffn_{m}_bias"]
    n["w1T"] = a["L1_ffn_moe_w1"].transpose(0, 2, 1)
    n["w2T"] = a["L1_ffn_moe_w2"].transpose(0, 2, 1)

    f = np.float32
    i = np.arange(P)
    behind = np.where(i[:, None] > i[None, :], f(NEG), f(0))
    n["c_ident"] = np.eye(P, dtype=f)
    n["c_stage"] = np.stack([np.eye(P, dtype=f), behind, behind.T, (i[:, None] < i[None, :]).astype(f),
                             np.zeros((P, P), f)], axis=1)
    n["c_desc16"] = f(EXPERTS) - np.arange(EXPERTS, dtype=f)
    n["c_base16"] = f(CAP) * np.arange(EXPERTS, dtype=f)
    n["c_desc8"] = f(8) - np.arange(8, dtype=f)
    n["c_rep"] = (np.arange(8)[:, None] == i[None, :] // 16).astype(f)
    theta = (f(1.0) / f(10000.0)) ** (f(2.0) * np.arange(HD // 2, dtype=f) / f(HD))
    angle = np.arange(1, SEQ + 1, dtype=f)[:, None] * theta.astype(f)
    n["c_cos"], n["c_sin"] = np.cos(angle).astype(f), np.sin(angle).astype(f)

    nc = _bacc.Bacc("TRN2", target_bir_lowering=False, num_devices=1)
    arrays, d = {}, {}
    for name, arr in n.items():
        arr = np.ascontiguousarray(arr)
        arrays[f"in_{name}"] = arr
        d[name] = nc.dram_tensor(f"in_{name}", arr.shape, _mybir.dt.from_np(arr.dtype), kind="ExternalInput").ap()
    out = nc.dram_tensor("out_0", (BATCH, SEQ, C), F32, kind="ExternalOutput").ap()
    two_layers(nc, d, out)
    r = _run(nc, [arrays], core_ids=[0])
    return r.results[0]["out_0"]
```

```python
from contextlib import ExitStack

import concourse.bass as bass
from concourse import mybir

F32 = mybir.dt.float32
BF16 = mybir.dt.bfloat16
I32 = mybir.dt.int32
U32 = mybir.dt.uint32
ALU = mybir.AluOpType
ACT = mybir.ActivationFunctionType
AX = mybir.AxisListType

P = 128
BATCH, SEQ, C = 8, 512, 256
HEADS, HD = 16, 16
TOK = BATCH * SEQ
NT = TOK // P
TPB = SEQ // P
KT = C // P
GH = 4
GROUPS = HEADS // GH
GW = GH * HD
CYCLE = 8

SLOTS = 7
QPART = (0, 0, 0, 1, 1, 1, 2)
KPART = (0, 1, 2, 0, 1, 2, 0)
SROWS = SLOTS * HD
MPARTS = 3
KROWS = SROWS + MPARTS
NEG = -1.0e30

EXPERTS, FFN, TOPK = 16, 512, 2
CAP = -(-TOK * TOPK * 5 // (EXPERTS * 4))
SLOTROWS = EXPERTS * CAP
CT = CAP // P
ZFILLS = SLOTROWS // (8 * P)


def layernorm(nc, name, src, dst, eps, again=None):
    with ExitStack() as s:
        stats = s.enter_context(nc.sbuf_tensor(name + "_stats", [P, TPB, 6], F32))
        mv4 = s.enter_context(nc.sbuf_tensor(name + "_mv4", [P, TPB, 2], F32))
        mv = s.enter_context(nc.sbuf_tensor(name + "_mv", [P, NT, 2], F32))
        half = s.enter_context(nc.sbuf_tensor(name + "_half", [P, NT], F32))
        carry = s.enter_context(nc.sbuf_tensor(name + "_carry", [P, 2], F32))
        vare = s.enter_context(nc.sbuf_tensor(name + "_vare", [P, NT], F32))
        rstd = s.enter_context(nc.sbuf_tensor(name + "_rstd", [P, NT], F32))
        stat_done = s.enter_context(nc.semaphore(name + "_stat_done"))
        aggr_done = s.enter_context(nc.semaphore(name + "_aggr_done"))
        mv_done = s.enter_context(nc.semaphore(name + "_mv_done"))
        var_done = s.enter_context(nc.semaphore(name + "_var_done"))
        rstd_done = s.enter_context(nc.semaphore(name + "_rstd_done"))
        half_done = s.enter_context(nc.semaphore(name + "_half_done"))
        begun = s.enter_context(nc.semaphore(name + "_begun"))
        blk = s.enter_context(nc.Block())

        @blk.vector
        def _(dve):
            dve.memset(carry[:, :], 0.0).then_inc(begun, 1)
            dve.wait_ge(begun, 1)
            with dve.Fori(0, BATCH) as b:
                for t in range(TPB):
                    dve.bn_stats(stats[:, t, :], src[:, bass.ds(TPB * b + t, 1), :]).then_inc(stat_done, 1)
                dve.wait_ge(stat_done, TPB * (b + 1))
                dve.tensor_copy(carry[:, 1:2], carry[:, 0:1])
                for t in range(TPB):
                    dve.bn_aggr(mv4[:, t, :], stats[:, t, :]).then_inc(aggr_done, 1)
                dve.wait_ge(aggr_done, TPB * (b + 1))
                dve.tensor_copy(mv[:, bass.ds(TPB * b, TPB), :], mv4[:, :, :]).then_inc(mv_done, 1)
                dve.wait_ge(mv_done, b + 1)
            dve.tensor_scalar(vare[:, :], mv[:, :, 1], eps, None, ALU.add).then_inc(var_done, 1)
            dve.wait_ge(rstd_done, 1)
            if again is not None:
                dve.tensor_tensor(vare[:, :], mv[:, :, 1], rstd[:, :], ALU.mult).then_inc(var_done, 1)
                dve.wait_ge(var_done, 2)
                dve.tensor_tensor(vare[:, :], vare[:, :], rstd[:, :], ALU.mult).then_inc(var_done, 1)
                dve.wait_ge(var_done, 3)
                dve.tensor_scalar(vare[:, :], vare[:, :], eps, None, ALU.add).then_inc(var_done, 1)
            with dve.Fori(0, BATCH) as b:
                for t in range(TPB):
                    j = TPB * b + t
                    dve.tensor_scalar(dst[:, bass.ds(j, 1), :], src[:, bass.ds(j, 1), :],
                                      mv[:, bass.ds(j, 1), 0], rstd[:, bass.ds(j, 1)],
                                      ALU.subtract, ALU.mult)

        @blk.gpsimd
        def _(pool):
            pool.memset(half[:, :], -0.5).then_inc(half_done, 1)
            pool.wait_ge(half_done, 1)
            pool.wait_ge(var_done, 1)
            pool.tensor_tensor(rstd[:, :], vare[:, :], half[:, :], ALU.pow).then_inc(rstd_done, 1)
            if again is not None:
                pool.wait_ge(var_done, 4)
                pool.tensor_tensor(again[:, :], vare[:, :], half[:, :], ALU.pow)


def attention(nc, name, layer, X, XN, w, consts, dram):
    L0 = layer == 0
    UPB = CYCLE if L0 else GROUPS
    NU = BATCH * UPB
    TURNS = NU // CYCLE
    causal = not L0

    def kind(i):
        return "C" if not L0 else ("A" if i % CYCLE < GROUPS else "B")

    def live(n, k):
        return 0 <= n + k < NU

    OT_AT = {1: "B", 5: "A"} if L0 else {1: "C", 5: "C"}

    def rounds(n):
        r = []
        i = n % CYCLE
        if live(n, 6) and kind(i + 6) == "B":
            r.append((0, "weff"))
        if i in OT_AT and 0 <= n - 5 < NU:
            r.append((2, "ot"))
            if not (L0 and i == 5):
                r.append((3, "outproj"))
        if live(n, -1):
            r.append((4, "norm"))
        if live(n, 6):
            r.append((5, "proj"))
        if L0 and i == 1 and 0 <= n < NU:
            r.append((6, "weffo"))
        if i in ((1,) if L0 else (1, 5)) and live(n, 7):
            r.append((7, "xt"))
        return r

    first = -6
    last = NU + 1

    def total(f, n):
        if isinstance(n, tuple):
            turn, i = n
            per = sum(f(m) for m in range(CYCLE, 2 * CYCLE))
            return (turn - 1) * per + sum(f(m) for m in range(first, CYCLE + i))
        return sum(f(m) for m in range(first, n))

    def whole(n):
        return n if not isinstance(n, tuple) else CYCLE + n[1]

    def unit(n, k):
        return n + k if not isinstance(n, tuple) else n[0] * CYCLE + (n[1] + k)

    def wait(eng, semaphore, value):
        if isinstance(value, int) and value <= 0:
            return
        eng.wait_ge(semaphore, value)

    def ma_count(n, what):
        names = [x for _, x in rounds(whole(n))]
        return total(lambda m: len(rounds(m)), n) + names.index(what) + 1

    def xt_count(n):
        return total(lambda m: sum(x == "xt" for _, x in rounds(m)), n)

    def back(n, k):
        return n - k if not isinstance(n, tuple) else (n[0], n[1] - k)

    def mb_rounds(n):
        stacks, rows = live(n, 3), live(n, 1)
        return ([0, 1, 2] if stacks else []) + (["rows"] if rows else []) + ([3] if stacks else [])

    def mb_count(n, what=None):
        before = total(lambda m: len(mb_rounds(m)), n)
        return before if what is None else before + mb_rounds(whole(n)).index(what) + 1

    def steps(eng, step):
        for n in range(first, CYCLE):
            step(n)
        if TURNS > 2:
            with eng.Fori(1, TURNS - 1) as turn:
                for i in range(CYCLE):
                    step((turn, i))
        for n in range(NU - CYCLE, last + 1):
            step(n)

    with ExitStack() as s:
        def sb(nm, shape, dt=F32):
            return s.enter_context(nc.sbuf_tensor(name + nm, shape, dt))

        def sem(nm):
            return s.enter_context(nc.semaphore(name + nm))

        identf, identb = consts["identf"], consts["identb"]
        xs = sb("xs", [P, TPB, C])
        xT = sb("xT", [P, KT, SEQ])
        qkf = sb("qkf", [P, 2, 2, TPB * GH * HD])
        qkw = sb("qkw", [P, 2, 2, TPB * GH * HD])
        part = [sb(f"part{j}", [P, 2, TPB * GH * HD], BF16) for j in range(3)]
        rest = sb("rest", [P, 2, TPB * GH * HD])
        slots = sb("slots", [P, 2, 2, TPB * GH, SROWS], BF16)
        stack = sb("stack", [P, 4, 2, GH, SEQ], BF16)
        vbuf = sb("vbuf", [P, CYCLE, TPB, GH, 32])
        mx = sb("mx", [P, 2, TPB * GH])
        mres = sb("mres", [P, TPB * GH])
        minus = sb("minus", [P, TPB, GH])
        carry = sb("carry", [P, 3])
        mparts = sb("mparts", [P, TPB, MPARTS, GH], BF16)
        mrows = sb("mrows", [MPARTS * GH, SEQ], BF16)
        prob = sb("prob", [P, 2, GH, SEQ])
        oT = sb("oT", [P, SEQ])
        rsum = sb("rsum", [P, TPB, GH])
        onA = sb("onA", [P, TPB, C])
        onB = sb("onB", [P, TPB, C])
        otA = sb("otA", [P, KT, SEQ])
        otB = sb("otB", [P, KT, SEQ]) if L0 else otA
        if L0:
            sq = sb("sq", [P, 2 * TPB * GH * HD])
            ms = sb("ms", [P, 2 * TPB * GH])
            rstd = sb("rstd", [P, 2 * TPB * GH])
            neghalf = sb("neghalf", [P, 2 * TPB * GH])
            xin = sb("xin", [P, TPB, C])
            us = sb("us", [P, 4, C])
            weff = sb("weff", [P, KT, 3 * GW])
            weffo = sb("weffo", [P, KT, C])
        else:
            rot = sb("rot", [P, 3, TPB * GH, HD // 2])
            RING = 4
            got = sb("got", [P, RING, TOPK, C])
            got_sem = [sem(f"got{i}") for i in range(RING)]
            added = sem("added")

        SC = s.enter_context(nc.psum_tensor(name + "SC", [P, 2, SEQ], F32))
        MX = s.enter_context(nc.psum_tensor(name + "MX", [P, 2, SEQ], F32))
        OV = s.enter_context(nc.psum_tensor(name + "OV", [P, SEQ], F32))
        MB = s.enter_context(nc.psum_tensor(name + "MB", [P, 8, P], BF16))
        MA = s.enter_context(nc.psum_tensor(name + "MA", [P, 1024], F32))

        ma_full = sem("ma_full")
        ma_free = sem("ma_free")
        mb_full = sem("mb_full")
        mb_free = sem("mb_free")
        score_ready = sem("score_ready")
        exp_done = sem("exp_done")
        smax_ready = sem("smax_ready")
        max_done = sem("max_done")
        pv_done = sem("pv_done")
        ov_read = sem("ov_read")
        qk_ready = sem("qk_ready")
        v_ready = sem("v_ready")
        sq_ready = sem("sq_ready")
        ss_ready = sem("ss_ready")
        ms_ready = sem("ms_ready")
        pool_norm = sem("pool_norm")
        split_done = sem("split_done")
        slots_done = sem("slots_done")
        mprep = sem("mprep")
        mrow_sent = sem("mrow_sent")
        xs_loaded = sem("xs_loaded")
        xin_loaded = sem("xin_loaded")
        xin_biased = sem("xin_biased")
        us_done = sem("us_done")
        recip_done = sem("recip_done")
        init = sem("init")
        pool_init = sem("pool_init")
        out_sent = sem("out_sent")

        MM_NORM = {"A": 3, "B": 1, "C": 6}

        def norm_steps(m):
            return MM_NORM[kind(m + 5)] if live(m, 5) else 0

        def a_units(k):
            return lambda m: int(live(m, k) and kind(m + k) == "A")

        def has(n, k):
            return live(whole(n), k)

        blk = s.enter_context(nc.Block())

        @blk.sync
        def _(sp):
            def load_xs(batch):
                sp.dma_start(xs[:, :, :], XN[:, bass.ds(batch * TPB, TPB), :]).then_inc(xs_loaded, 16)

            load_xs(0)

            def step(n):
                w_ = whole(n)
                i = w_ % CYCLE
                if i in ((0,) if L0 else (0, 4)) and (isinstance(n, tuple) or 0 < (w_ + 8) // UPB < BATCH):
                    past = back(n, 7 if L0 else 3)
                    if isinstance(past, int) and "xt" not in [x for _, x in rounds(past)]:
                        sp.wait_ge(ma_full, 1)
                    else:
                        sp.wait_ge(ma_full, ma_count(past, "xt") + 1)
                    load_xs((w_ + 8) // UPB if isinstance(n, int) else n[0] * (CYCLE // UPB) + (i + 8) // UPB)
                if has(n, 1):
                    sp.wait_ge(mb_free, mb_count(n, "rows"))
                    for j in range(MPARTS):
                        sp.dma_start(stack[SROWS + j:SROWS + j + 1, (w_ + 1) % 4, 0, :, :],
                                     mrows[j * GH:(j + 1) * GH, :]).then_inc(mrow_sent, 16)
                if L0 and i == 2 and 0 <= w_ < NU:
                    batch = w_ // CYCLE if isinstance(n, int) else n[0]
                    if isinstance(n, tuple) or n > CYCLE:
                        sp.wait_ge(ma_free, ma_count(back(n, 1), "outproj") + 1)
                    sp.dma_start(xin[:, :, :], dram["x"][:, bass.ds(batch * TPB, TPB), :]).then_inc(xin_loaded, 16)
                if not L0 and "outproj" in [x for _, x in rounds(w_)]:
                    batch = (w_ - 5) // UPB if isinstance(n, int) else 2 * n[0] + (n[1] - 5) // UPB
                    sp.wait_ge(ma_free, ma_count(n, "outproj") + 1)
                    sp.dma_start(dram["out"][:, bass.ds(batch * TPB, TPB), :],
                                 X[:, bass.ds(batch * TPB, TPB), :]).then_inc(out_sent, 16)

            steps(sp, step)
            if not L0:
                sp.wait_ge(out_sent, 16 * BATCH)

        @blk.tensor
        def _(pe):
            pe.wait_ge(init, 3)

            def xt_round(n):
                wait(pe, xs_loaded, 16 if n is None else 16 * (xt_count(n) + 2))
                for t in range(TPB):
                    for kt in range(KT):
                        mm = pe.transpose(MA[:, kt * SEQ + t * P:kt * SEQ + (t + 1) * P],
                                          xs[:, t, kt * P:(kt + 1) * P], identf[:, :])
                mm.then_inc(ma_full, 1)

            def ma_round(n, what):
                w_ = whole(n)
                i = w_ % CYCLE
                wait(pe, ma_free, ma_count(n, what))
                if what == "weff":
                    g = (i + 6) % GROUPS
                    nb = (w_ + 6) // CYCLE if isinstance(n, int) else n[0] + (n[1] + 6) // CYCLE
                    wait(pe, us_done, 4 * (nb + 1))
                    for kt in range(KT):
                        for j in range(3):
                            mm = pe.matmul(MA[:, kt * 3 * GW + j * GW:kt * 3 * GW + (j + 1) * GW],
                                           w["V"][:, j, kt * P:(kt + 1) * P], us[:, j, g * GW:(g + 1) * GW],
                                           start=True, stop=True)
                elif what == "weffo":
                    for kt in range(KT):
                        mm = pe.matmul(MA[:, kt * SEQ:kt * SEQ + C], w["V"][:, 3, kt * P:(kt + 1) * P],
                                       us[:, 3, :], start=True, stop=True)
                elif what == "proj":
                    kd = kind(i + 6)
                    g = (i + 6) % GROUPS
                    for t in range(TPB):
                        for kt in range(KT):
                            rhs = weff[:, kt, :] if kd == "B" else w["W" + kd][:, kt, g, :]
                            mm = pe.matmul(MA[:, t * C:t * C + 3 * GW], xT[:, kt, t * P:(t + 1) * P], rhs,
                                           start=(kt == 0), stop=(kt == KT - 1))
                elif what == "ot":
                    src = onB if i == 1 else onA
                    for t in range(TPB):
                        for kt in range(KT):
                            mm = pe.transpose(MA[:, kt * SEQ + t * P:kt * SEQ + (t + 1) * P],
                                              src[:, t, kt * P:(kt + 1) * P], identf[:, :])
                elif what == "outproj":
                    pairs = [(otA, w["WoA"]), (otB, weffo)] if L0 else [(otA, w["WoC"])]
                    for t in range(TPB):
                        for q, (ot, wo) in enumerate(pairs):
                            for kt in range(KT):
                                mm = pe.matmul(MA[:, t * C:(t + 1) * C], ot[:, kt, t * P:(t + 1) * P],
                                               wo[:, kt, :], start=(q == 0 and kt == 0),
                                               stop=(q == len(pairs) - 1 and kt == KT - 1))
                elif what == "norm":
                    wait(pe, ov_read, unit(n, 0))
                    for t in range(TPB):
                        mm = pe.transpose(MA[:, t * P:(t + 1) * P], oT[:, t * P:(t + 1) * P], identf[:, :])
                mm.then_inc(ma_full, 1)

            def stack_round(n, r):
                qk, half = r // 2, r % 2
                wait(pe, slots_done, 6 * (unit(n, 3) + 1))
                wait(pe, mb_free, mb_count(n, r) - 1)
                for j in range(8):
                    t, h = 2 * half + j // GH, j % GH
                    mm = pe.transpose(MB[0:SROWS, (j % GH) * 2 + j // GH, :],
                                      slots[:, (whole(n) + 3) % 2, qk, t * GH + h, :], identb[:, :])
                mm.then_inc(mb_full, 1)

            def mrow_round(n):
                wait(pe, mprep, 5 * (unit(n, 1) + 1))
                wait(pe, mb_free, mb_count(n, "rows") - 1)
                for t in range(TPB):
                    mm = pe.transpose(MB[0:MPARTS * GH, t, :], mparts[:, t, :, :], identb[:, :])
                mm.then_inc(mb_full, 1)

            def score(n, sl, h):
                u4 = whole(n) % 4
                if sl == 0 and h == 0:
                    wait(pe, mrow_sent, 16 * MPARTS * (unit(n, 0) + 1))
                wait(pe, exp_done, 16 * unit(n, 0) + 4 * sl + h - 1)
                lo = sl * P if causal else 0
                mm = pe.matmul(SC[:, h % 2, lo:SEQ], stack[0:KROWS, u4, 1, h, sl * P:(sl + 1) * P],
                               stack[0:KROWS, u4, 0, h, lo:SEQ], start=True, stop=not causal)
                if causal:
                    mm = pe.matmul(SC[:, h % 2, lo:lo + P], identb[:, :], consts["mask_kq"][:, :],
                                   start=False, stop=True)
                mm.then_inc(score_ready, 1)

            def maxmm(n, sl, h):
                u4 = (whole(n) + 2) % 4
                if sl == 0 and h == 0:
                    wait(pe, mb_free, mb_count(n))
                wait(pe, max_done, 16 * unit(n, 2) + 4 * sl + h - 1)
                hi = (sl + 1) * P if causal else SEQ
                mm = pe.matmul(MX[:, h % 2, 0:hi], stack[0:SROWS, u4, 0, h, sl * P:(sl + 1) * P],
                               stack[0:SROWS, u4, 1, h, 0:hi], start=True, stop=not causal)
                if causal:
                    mm = pe.matmul(MX[:, h % 2, hi - P:hi], identb[:, :], consts["mask_qk"][:, :],
                                   start=False, stop=True)
                mm.then_inc(smax_ready, 1)

            def pv(n, k, sl, h):
                v8 = (whole(n) + k) % CYCLE
                u = unit(n, k)
                wait(pe, exp_done, 16 * u + 4 * sl + h + 1)
                if sl == 0 and h == 0:
                    wait(pe, ov_read, u)
                    wait(pe, v_ready, u + 1)
                lo = sl * P if causal else 0
                mm = pe.matmul(OV[32 * h:32 * h + 32, lo:SEQ], vbuf[:, v8, sl, h, :],
                               prob[:, sl % 2, h, lo:SEQ], start=(sl == 0), stop=(sl == TPB - 1),
                               skip_group_check=True)
                if h == GH - 1:
                    mm.then_inc(pv_done, 1)

            xt_round(None)

            PV_HEADS = ((0,), (1,), (2,), (3,))
            PV_LATE = ((), (0, 1), (2,), (3,))

            def step(n):
                r = dict(rounds(whole(n)))
                for p in range(8):
                    sl, hp = p // 2, p % 2
                    if p in r:
                        if r[p] == "xt":
                            wait(pe, ma_free, ma_count(n, "xt"))
                            xt_round(n)
                        else:
                            ma_round(n, r[p])
                    if has(n, 3) and p in (0, 2, 4, 6):
                        stack_round(n, p // 2)
                    if has(n, 1) and p == 5:
                        mrow_round(n)
                    for h in (2 * hp, 2 * hp + 1):
                        if has(n, 0):
                            score(n, sl, h)
                        if has(n, 2):
                            maxmm(n, sl, h)
                        for hv in (PV_LATE if sl == 1 else PV_HEADS)[h]:
                            if sl == 0:
                                if has(n, -1):
                                    pv(n, -1, TPB - 1, hv)
                            elif has(n, 0):
                                pv(n, 0, sl - 1, hv)

            steps(pe, step)

        @blk.scalar
        def _(act):
            act.wait_ge(init, 3)
            STACK_COPIES = [(0, 0), (0, 1), (2, 0), (2, 1), (4, 0), (4, 1), (6, 0), (6, 1)]
            act.wait_ge(ma_full, 1)
            act.copy(xT[:, :, :], MA[:, :].rearrange("p (k n) -> p k n", k=KT)).then_inc(ma_free, 1)

            def step(n):
                w_ = whole(n)
                r = dict(rounds(w_))
                for p in range(8):
                    sl, hp = p // 2, p % 2
                    if r.get(p) in ("xt", "ot"):
                        wait(act, ma_full, ma_count(n, r[p]) + 1)
                        if r[p] == "xt":
                            dst = xT
                        else:
                            dst = otB if L0 and w_ % CYCLE == 1 else otA
                        act.copy(dst[:, :, :], MA[:, :].rearrange("p (k n) -> p k n", k=KT)).then_inc(ma_free, 1)
                    if has(n, 1) and p == 5:
                        wait(act, mb_full, mb_count(n, "rows"))
                        wait(act, mrow_sent, 16 * MPARTS * unit(n, 1))
                        act.copy(mrows[:, :].rearrange("p (t n) -> p t n", t=TPB),
                                 MB[0:MPARTS * GH, 0:TPB, :]).then_inc(mb_free, 1)
                    if p == 2 and has(n, -1):
                        wait(act, pv_done, 4 * unit(n, 0))
                        if has(n, -2):
                            wait(act, ma_full, ma_count(back(n, 1), "norm") + 1)
                        act.copy(oT[:, :], OV[:, :]).then_inc(ov_read, 1)
                    for h in (2 * hp, 2 * hp + 1):
                        if has(n, 0):
                            wait(act, score_ready, 16 * unit(n, 0) + 4 * sl + h + 1)
                            wait(act, pv_done, 4 * unit(n, 0) + sl - 1)
                            lo = sl * P if causal else 0
                            act.activation(prob[:, sl % 2, h, lo:SEQ], SC[:, h % 2, lo:SEQ], ACT.Exp,
                                           scale=float(HD) ** -0.5).then_inc(exp_done, 1)
                        if has(n, 3) and (p, h % 2) in STACK_COPIES:
                            rr, pair = divmod(STACK_COPIES.index((p, h % 2)), 2)
                            half = rr % 2
                            wait(act, mb_full, mb_count(n, rr))
                            copied = act.copy(
                                stack[0:SROWS, (w_ + 3) % 4, rr // 2, 2 * pair:2 * pair + 2,
                                      half * 2 * P:(half + 1) * 2 * P],
                                MB[0:SROWS, 4 * pair:4 * pair + 4, :].rearrange("p (h t) n -> p h (t n)", h=2))
                            if pair:
                                copied.then_inc(mb_free, 1)

            steps(act, step)

        @blk.vector
        def _(dve):
            dve.memset(vbuf[:, :, :, :, :].rearrange("p a t h d -> p (a t h d)"), 1.0).then_inc(init, 1)
            dve.memset(stack[96:P, :, :, :, :].rearrange("p a q h n -> p (a q h n)"), 1.0).then_inc(init, 1)
            if L0:
                dve.memset(neghalf[:, :], -0.5).then_inc(init, 1)
            else:
                dve.memset(qkw[:, :, :, :].rearrange("p a q n -> p (a q n)"), 0.0).then_inc(init, 1)
            dve.wait_ge(init, 3)

            def gate_factors(batch):
                for j in range(4):
                    dve.tensor_scalar(us[:, j, :], w["UT"][:, j, :], w["gS"][:, j, bass.ds(batch, 1)], None,
                                      ALU.mult).then_inc(us_done, 1)

            def ma_round(n, what):
                w_ = whole(n)
                i = w_ % CYCLE
                wait(dve, ma_full, ma_count(n, what) + 1)
                if what == "weff":
                    g = (i + 6) % GROUPS
                    dve.tensor_tensor(weff[:, :, :], MA[:, 0:KT * 3 * GW].rearrange("p (k n) -> p k n", k=KT),
                                      w["WB"][:, :, g, :], ALU.add).then_inc(ma_free, 1)
                elif what == "weffo":
                    dve.tensor_tensor(weffo[:, :, :], MA[:, :].rearrange("p (k n) -> p k n", k=KT)[:, :, 0:C],
                                      w["WoB"][:, :, :], ALU.add).then_inc(ma_free, 1)
                elif what == "proj":
                    kd = kind(i + 6)
                    g = (i + 6) % GROUPS
                    u = unit(n, 6)
                    ps = MA[:, :].rearrange("p (t n) -> p t n", t=TPB)
                    bias = w["b" + kd]
                    wait(dve, pool_norm, total(norm_steps, n))
                    if has(n, -1):
                        wait(dve, pv_done, 4 * unit(n, -1))
                    dve.tensor_tensor(
                        vbuf[:, (w_ + 6) % CYCLE, :, :, 0:HD],
                        ps[:, :, 2 * GW:3 * GW].rearrange("p t (h d) -> p t h d", h=GH),
                        bias[:, g, 2 * GW:3 * GW].rearrange("p (h d) -> p h d", h=GH).unsqueeze(1)
                        .to_broadcast([P, TPB, GH, HD]), ALU.add).then_inc(v_ready, 1)
                    for qk in range(2):
                        dve.tensor_tensor(
                            qkf[:, (w_ + 6) % 2, qk, :].rearrange("p (t n) -> p t n", t=TPB),
                            ps[:, :, qk * GW:(qk + 1) * GW],
                            bias[:, g, qk * GW:(qk + 1) * GW].unsqueeze(1).to_broadcast([P, TPB, GW]),
                            ALU.add).then_inc((qk_ready, ma_free)[qk], 1)
                elif what == "outproj":
                    res = MA[:, :].rearrange("p (t n) -> p t n", t=TPB)
                    if L0:
                        batch = (w_ - 9) // CYCLE if isinstance(n, int) else n[0] - 1
                        wait(dve, xin_biased, batch + 1)
                        dve.tensor_tensor(X[:, bass.ds(batch * TPB, TPB), :], res, xin[:, :, :],
                                          ALU.add).then_inc(ma_free, 1)
                    else:
                        batch = (w_ - 5) // UPB if isinstance(n, int) else 2 * n[0] + (n[1] - 5) // UPB
                        rows = X[:, bass.ds(batch * TPB, TPB), :]
                        wait(dve, added, TOPK * TPB * (batch + 1))
                        dve.tensor_tensor(rows, res, rows, ALU.add).then_inc(ma_free, 1)
                elif what == "norm":
                    u = unit(n, -1)
                    g = (w_ - 1) % GROUPS
                    dst = onA if (w_ - 1) % CYCLE < GROUPS else onB
                    o = MA[:, 0:SEQ].rearrange("p (t h d) -> p t h d", t=TPB, h=GH)
                    dve.reciprocal(rsum[:, :, :], o[:, :, :, HD]).then_inc(recip_done, 1)
                    wait(dve, recip_done, u + 1)
                    dve.tensor_tensor(dst[:, :, g * GW:(g + 1) * GW].rearrange("p t (h d) -> p t h d", h=GH),
                                      o[:, :, :, 0:HD],
                                      rsum[:, :, :].unsqueeze(3).to_broadcast([P, TPB, GH, HD]),
                                      ALU.mult).then_inc(ma_free, 1)

            def squares_sum(n, j):
                k = total(a_units(5), n)
                if j == 1:
                    wait(dve, ss_ready, k + 1)
                    dve.tensor_scalar(ms[:, :], ms[:, :], 1.0 / HD, 1e-6, ALU.mult, ALU.add).then_inc(ms_ready, 1)
                    return
                wait(dve, sq_ready, k + 1)
                wait(dve, pool_norm, total(norm_steps, n))
                dve.tensor_reduce(ms[:, :], sq[:, :].rearrange("p (a d) -> p a d", d=HD), AX.X,
                                  ALU.add).then_inc(ss_ready, 1)

            def split(n, j):
                u = unit(n, 4)
                src = qkw[:, (whole(n) + 4) % 2, :, :]
                if j == 0:
                    wait(dve, pool_norm, total(norm_steps, n))
                    wait(dve, slots_done, 6 * u)
                    dve.tensor_copy(part[0][:, :, :], src).then_inc(split_done, 1)
                    return
                wait(dve, split_done, 4 * u + j)
                if j == 1:
                    ins = dve.tensor_tensor(rest[:, :, :], src, part[0][:, :, :], ALU.subtract)
                elif j == 2:
                    ins = dve.tensor_copy(part[1][:, :, :], rest[:, :, :])
                else:
                    ins = dve.tensor_tensor(part[2][:, :, :], rest[:, :, :], part[1][:, :, :], ALU.subtract)
                ins.then_inc(split_done, 1)

            def lay_slots(n, j):
                u = unit(n, 4)
                qk = j // 3
                src = [part[k][:, qk, :].rearrange("p (a d) -> p a d", d=HD) for k in range(3)]
                dst = slots[:, (whole(n) + 4) % 2, qk, :, :].rearrange("p a (s d) -> p a s d", d=HD)
                if j == 0:
                    wait(dve, split_done, 4 * (u + 1))
                    wait(dve, mb_full, mb_count(n))
                k = j % 3
                wide, at = ((3, slice(0, 3)), (3, slice(3, 6)), (1, slice(6, 7)),
                            (3, slice(0, 7, 3)), (2, slice(1, 5, 3)), (2, slice(2, 6, 3)))[j]
                dve.tensor_copy(dst[:, :, at, :], src[k].unsqueeze(2).to_broadcast([P, TPB * GH, wide, HD]))\
                   .then_inc(slots_done, 1)

            def add_experts(n):
                j = unit(n, 0)
                ring = whole(n) % RING
                turn_ = j // RING if isinstance(j, int) else n[0] * (CYCLE // RING) + n[1] // RING
                wait(dve, got_sem[ring], 16 * TOPK * (turn_ + 1))
                row = X[:, bass.ds(j, 1), :]
                for k in range(TOPK):
                    if k:
                        wait(dve, added, TOPK * j + k)
                    dve.scalar_tensor_tensor(out=row, in0=got[:, ring:ring + 1, k, :],
                                             scalar=w["gate"][:, bass.ds(j, 1), k], in1=row,
                                             op0=ALU.mult, op1=ALU.add).then_inc(added, 1)

            if L0:
                gate_factors(0)

            SPLIT_AT = (1, 3, 5, 7) if L0 else (0, 1, 2, 3)
            SLOTS_AT = (8, 9, 11, 12, 13, 14) if L0 else (4, 5, 6, 8, 9, 10)

            def step(n):
                w_ = whole(n)
                r = dict(rounds(w_))
                for p in range(8):
                    sl, hp = p // 2, p % 2
                    if p in r and r[p] not in ("xt", "ot"):
                        ma_round(n, r[p])
                    if L0 and p == 4 and w_ % CYCLE == 3 and 0 <= w_ < NU - CYCLE:
                        batch = w_ // CYCLE + 1 if isinstance(n, int) else n[0] + 1
                        wait(dve, ma_full, ma_count(back(n, 2), "weffo") + 1)
                        gate_factors(batch)
                    for h in (2 * hp, 2 * hp + 1):
                        m = 2 * p + h % 2
                        if has(n, 2):
                            u = unit(n, 2)
                            wait(dve, smax_ready, 16 * u + 4 * sl + h + 1)
                            if sl == 0 and h == 0:
                                wait(dve, mprep, 5 * unit(n, 1))
                            hi = (sl + 1) * P if causal else SEQ
                            dve.tensor_reduce(mx[:, (w_ + 2) % 2, sl * GH + h:sl * GH + h + 1],
                                              MX[:, h % 2, 0:hi], AX.X, ALU.max).then_inc(max_done, 1)
                        if m in (0, 2) and has(n, 5) and kind(w_ + 5) == "A":
                            squares_sum(n, m // 2)
                        if m in SPLIT_AT and has(n, 4):
                            split(n, SPLIT_AT.index(m))
                        if not L0 and m == 7 and has(n, 0):
                            add_experts(n)
                        if m in SLOTS_AT and has(n, 4):
                            lay_slots(n, SLOTS_AT.index(m))

            steps(dve, step)

        @blk.gpsimd
        def _(pool):
            pool.memset(minus[:, :, :], -1.0).then_inc(pool_init, 1)
            pool.memset(carry[:, :], 0.0).then_inc(pool_init, 1)
            pool.wait_ge(pool_init, 2)
            pool.wait_ge(init, 3)

            def maxima(n):
                u = unit(n, 1)
                m = mx[:, (whole(n) + 1) % 2, :]
                wait(pool, max_done, 16 * (u + 1))
                if has(n, 0):
                    wait(pool, mb_full, mb_count(back(n, 1), "rows"))
                mv = m.rearrange("p (t h) -> p t h", t=TPB)
                rv = mres[:, :].rearrange("p (t h) -> p t h", t=TPB)
                pool.tensor_tensor(mparts[:, :, 0, :], mv, minus[:, :, :], ALU.mult).then_inc(mprep, 1)
                wait(pool, mprep, 5 * u + 1)
                pool.tensor_tensor(rv, mv, mparts[:, :, 0, :], ALU.add).then_inc(mprep, 1)
                wait(pool, mprep, 5 * u + 2)
                pool.tensor_tensor(mparts[:, :, 1, :], rv, minus[:, :, :], ALU.mult).then_inc(mprep, 1)
                wait(pool, mprep, 5 * u + 3)
                pool.tensor_tensor(rv, rv, mparts[:, :, 1, :], ALU.add).then_inc(mprep, 1)
                wait(pool, mprep, 5 * u + 4)
                pool.tensor_tensor(mparts[:, :, 2, :], rv, minus[:, :, :], ALU.mult).then_inc(mprep, 1)

            def norm_qk(n):
                w_ = whole(n)
                kd = kind(w_ + 5)
                u = unit(n, 5)
                src, dst = qkf[:, (w_ + 5) % 2, :, :], qkw[:, (w_ + 5) % 2, :, :]
                done = total(norm_steps, n)
                wait(pool, ma_free, ma_count(back(n, 1), "proj") + 1)
                wait(pool, pool_norm, done)
                wait(pool, split_done, 4 * unit(n, 4))
                if kd == "B":
                    pool.tensor_tensor(carry[:, 2:3], carry[:, 0:1], carry[:, 0:1], ALU.add)
                    pool.tensor_copy(dst, src).then_inc(pool_norm, 1)
                elif kd == "A":
                    wait(pool, ms_ready, total(a_units(5), n) + 1)
                    pool.tensor_tensor(rstd[:, :], ms[:, :], neghalf[:, :], ALU.pow).then_inc(pool_norm, 1)
                    wait(pool, pool_norm, done + 1)
                    d3 = dst.rearrange("p q (a d) -> p (q a) d", d=HD)
                    pool.tensor_tensor(d3, src.rearrange("p q (a d) -> p (q a) d", d=HD),
                                       rstd[:, :].unsqueeze(2).to_broadcast([P, 2 * TPB * GH, HD]),
                                       ALU.mult).then_inc(pool_norm, 1)
                    wait(pool, pool_norm, done + 2)
                    d4 = dst.rearrange("p q (a d) -> p q a d", d=HD)
                    pool.tensor_tensor(d4, d4, w["qkn"][:, :, :].unsqueeze(2)
                                       .to_broadcast([P, 2, TPB * GH, HD]), ALU.mult).then_inc(pool_norm, 1)
                else:
                    for qk in range(2):
                        ue = src[:, qk, :].rearrange("p (t h d e) -> p t h d e", t=TPB, h=GH, e=2)[:, :, :, :, 0]
                        uo = src[:, qk, :].rearrange("p (t h d e) -> p t h d e", t=TPB, h=GH, e=2)[:, :, :, :, 1]
                        r0 = rot[:, 0, :, :].rearrange("p (t h) d -> p t h d", t=TPB)
                        r1 = rot[:, 1, :, :].rearrange("p (t h) d -> p t h d", t=TPB)
                        cb = w["cos"][:, :, :].unsqueeze(2).to_broadcast([P, TPB, GH, HD // 2])
                        sb_ = w["sin"][:, :, :].unsqueeze(2).to_broadcast([P, TPB, GH, HD // 2])
                        pool.tensor_tensor(r0, ue, cb, ALU.mult).then_inc(pool_norm, 1)
                        pool.tensor_tensor(r1, uo, sb_, ALU.mult).then_inc(pool_norm, 1)
                        wait(pool, pool_norm, done + 3 * qk + 2)
                        out = dst[:, qk, :].rearrange("p (a d) -> p a d", d=HD)[:, :, 0:HD // 2]
                        pool.tensor_tensor(out, rot[:, 0, :, :], rot[:, 1, :, :],
                                           ALU.subtract).then_inc(pool_norm, 1)
                        wait(pool, pool_norm, done + 3 * qk + 3)

            def squares(n):
                u = unit(n, 6)
                wait(pool, ma_free, ma_count(n, "proj") + 1)
                wait(pool, ss_ready, total(a_units(6), n))
                src = qkf[:, (whole(n) + 6) % 2, :, :].rearrange("p q n -> p (q n)")
                pool.tensor_tensor(sq[:, :], src, src, ALU.mult).then_inc(sq_ready, 1)

            def fetch(j):
                if j >= RING:
                    wait(pool, added, TOPK * (j - RING + 1))
                for k in range(TOPK):
                    pool.indirect_dma_start(got[:, j % RING, k, :], None, dram["outs"],
                                            bass.IndirectOffsetOnAxis(ap=w["gather_id"][:, j, k:k + 1], axis=0),
                                            bounds_check=SLOTROWS - 1, oob_is_err=False)\
                        .then_inc(got_sem[j % RING], 16)

            def step(n):
                w_ = whole(n)
                if has(n, 1):
                    maxima(n)
                if has(n, 5):
                    norm_qk(n)
                if L0 and w_ % CYCLE == 3 and 0 <= w_ < NU:
                    batch = w_ // CYCLE if isinstance(n, int) else n[0]
                    wait(pool, xin_loaded, 16 * (batch + 1))
                    pool.tensor_tensor(xin[:, :, :], xin[:, :, :],
                                       w["bout"][:, :].unsqueeze(1).to_broadcast([P, TPB, C]),
                                       ALU.add).then_inc(xin_biased, 1)
                if has(n, 6) and kind(w_ + 6) == "A":
                    squares(n)
                if not L0 and 0 <= n + 2 < NT:
                    fetch(n + 2)

            if L0:
                steps(pool, step)
            else:
                for n in range(first, last + 1):
                    step(n)


def top_two(dve, link, vals, desc, eq, top, best, hot, rest):
    p_, g_, e_ = vals.shape
    cur = vals
    for k in range(2):
        link(dve.tensor_reduce(top[k], cur, AX.X, ALU.max))
        link(dve.tensor_tensor(eq, cur, top[k].unsqueeze(2).to_broadcast([p_, g_, e_]), ALU.is_equal))
        link(dve.tensor_tensor(eq, eq, desc, ALU.mult))
        link(dve.tensor_reduce(best, eq, AX.X, ALU.max))
        link(dve.tensor_tensor(hot[k], eq, best.unsqueeze(2).to_broadcast([p_, g_, e_]), ALU.is_equal))
        if k == 0:
            link(dve.tensor_scalar(eq, hot[0], NEG, None, ALU.mult))
            link(dve.tensor_tensor(rest, vals, eq, ALU.add))
            cur = rest


def gates(nc, XN, gate_w, gS, consts, S4, zeroed):
    E, GHID = 8, 64
    with ExitStack() as s:
        def sb(nm, shape, dt=F32):
            return s.enter_context(nc.sbuf_tensor("gate_" + nm, shape, dt))

        pooled = sb("pooled", [P, KT, BATCH])
        mean = sb("mean", [P, 1])
        hid = sb("hid", [GHID, BATCH])
        logit = sb("logit", [BATCH, 1, E])
        eq = sb("eq", [BATCH, 1, E])
        rest = sb("rest", [BATCH, 1, E])
        hot = [sb(f"hot{k}", [BATCH, 1, E]) for k in range(2)]
        top = [sb(f"top{k}", [BATCH, 1]) for k in range(2)]
        best = sb("best", [BATCH, 1])
        gap, e2, den, g1, g2 = (sb(nm, [BATCH, 1]) for nm in ("gap", "e2", "den", "g1", "g2"))
        gate = sb("gate", [BATCH, E])
        gateT = sb("gateT", [E, BATCH])
        ps = s.enter_context(nc.psum_tensor("gate_ps", [P, 5, 512], F32))
        chain = s.enter_context(nc.semaphore("gate_chain"))
        mm_done = s.enter_context(nc.semaphore("gate_mm"))
        for_pe = s.enter_context(nc.semaphore("gate_for_pe"))
        exp_in = s.enter_context(nc.semaphore("gate_exp_in"))
        exp_out = s.enter_context(nc.semaphore("gate_exp_out"))
        blk = s.enter_context(nc.Block())

        @blk.tensor
        def _(pe):
            pe.wait_ge(for_pe, 1)
            for b in range(BATCH):
                for kt in range(KT):
                    for t in range(TPB):
                        mm = pe.matmul(ps[:, 0, kt * BATCH + b:kt * BATCH + b + 1],
                                       XN[:, b * TPB + t, kt * P:(kt + 1) * P], mean[:, :],
                                       start=(t == 0), stop=(t == TPB - 1))
            mm.then_inc(mm_done, 1)
            pe.wait_ge(for_pe, 2)
            for kt in range(KT):
                mm = pe.matmul(ps[0:GHID, 1, 0:BATCH], gate_w["gw1"][:, kt, :], pooled[:, kt, :],
                               start=(kt == 0), stop=(kt == KT - 1))
            mm.then_inc(mm_done, 1)
            pe.wait_ge(for_pe, 3)
            pe.matmul(ps[0:BATCH, 2, 0:E], hid[:, :], gate_w["gw2"][:, :], start=True, stop=True).then_inc(mm_done, 1)
            pe.wait_ge(for_pe, 4)
            pe.transpose(ps[0:E, 3, 0:BATCH], gate[:, :], consts["identf"][0:BATCH, 0:BATCH]).then_inc(mm_done, 1)
            pe.wait_ge(for_pe, 5)
            pe.matmul(ps[:, 4, 0:BATCH], gate_w["rep"][:, :], gateT[:, :], start=True, stop=True).then_inc(mm_done, 1)

        @blk.gpsimd
        def _(pool):
            pool.wait_ge(zeroed, 16 * ZFILLS)

        @blk.scalar
        def _(act):
            act.wait_ge(exp_in, 1)
            act.activation(e2[:, :], gap[:, :], ACT.Exp).then_inc(exp_out, 1)

        @blk.vector
        def _(dve):
            steps = [0]

            def link(ins):
                steps[0] += 1
                ins.then_inc(chain, 1)
                dve.wait_ge(chain, steps[0])

            dve.memset(mean[:, :], 1.0 / SEQ).then_inc(for_pe, 1)
            dve.wait_ge(mm_done, 1)
            dve.tensor_copy(pooled[:, :, :], ps[:, 0, 0:KT * BATCH].rearrange("p (k b) -> p k b", k=KT)).then_inc(for_pe, 1)
            dve.wait_ge(mm_done, 2)
            dve.tensor_scalar(hid[:, :], ps[0:GHID, 1, 0:BATCH], gate_w["gb1"][:, 0:1], 0.0, ALU.add,
                              ALU.max).then_inc(for_pe, 1)
            dve.wait_ge(mm_done, 3)
            link(dve.tensor_tensor(logit[:, 0, :], ps[0:BATCH, 2, 0:E], gate_w["gb2"][:, :], ALU.add))
            top_two(dve, link, logit[:, :, :], gate_w["desc8"][:, :].unsqueeze(1), eq[:, :, :],
                    [t[:, :] for t in top], best[:, :], [h[:, :, :] for h in hot], rest[:, :, :])
            dve.tensor_tensor(gap[:, :], top[1][:, :], top[0][:, :], ALU.subtract).then_inc(exp_in, 1)
            dve.wait_ge(exp_out, 1)
            link(dve.tensor_scalar(den[:, :], e2[:, :], 1.0, None, ALU.add))
            link(dve.reciprocal(g1[:, :], den[:, :]))
            link(dve.tensor_tensor(g2[:, :], g1[:, :], e2[:, :], ALU.mult))
            link(dve.tensor_scalar(gate[:, :], hot[0][:, 0, :], g1[:, 0:1], None, ALU.mult))
            dve.scalar_tensor_tensor(out=gate[:, :], in0=hot[1][:, 0, :], scalar=g2[:, 0:1], in1=gate[:, :],
                                     op0=ALU.mult, op1=ALU.add).then_inc(for_pe, 1)
            dve.wait_ge(mm_done, 4)
            dve.tensor_copy(gateT[:, :], ps[0:E, 3, 0:BATCH]).then_inc(for_pe, 1)
            dve.wait_ge(mm_done, 5)
            for j in range(4):
                dve.tensor_scalar(gS[:, j, :], ps[:, 4, 0:BATCH], S4[:, j:j + 1], None, ALU.mult)


def block_d(nc, X, XN, Z, again, logits, w, consts):
    S = BATCH
    KVH = 4
    REP = HEADS // KVH
    KV = KVH * HD
    QKV = C + 2 * KV
    Xv = X[:, :, :].rearrange("p (s t) c -> p s t c", t=TPB)
    XNv = XN[:, :, :].rearrange("p (s t) c -> p s t c", t=TPB)
    Zv = Z[:, :, :].rearrange("p (s t) c -> p s t c", t=TPB)
    Lv = logits[:, :, :].rearrange("p (s t) e -> p s t e", t=TPB)
    with ExitStack() as s_:
        def sb(nm, shape, dt=F32):
            return s_.enter_context(nc.sbuf_tensor("d_" + nm, shape, dt))

        def sem(nm):
            return s_.enter_context(nc.semaphore("d_" + nm))

        z = sb("z", [P, S, C])
        zT = sb("zT", [P, KT, S * P])
        q = sb("q", [P, 2, S, C])
        kv = sb("kv", [P, 2, S, 2, KV])
        prod = sb("prod", [P, S, C])
        prod2 = sb("prod2", [P, 2, S, C])
        sc = sb("sc", [P, S, S, HEADS])
        top = sb("top", [P, S, HEADS])
        sums = sb("sums", [P, S, HEADS])
        den = sb("den", [P, S, HEADS])
        o = sb("o", [P, S, C])
        h = sb("h", [P, S, C])
        stats = sb("stats", [P, S, 6])
        mv = sb("mv", [P, S, 2])
        vare = sb("vare", [P, S])
        nmu = sb("nmu", [P, S])
        rstd = sb("rstd", [P, S])
        nmr = sb("nmr", [P, S])
        half = sb("half", [P, S])
        carry = sb("carry", [P, 2])
        T = s_.enter_context(nc.psum_tensor("d_T", [P, 2, 4, P], F32))
        Y = s_.enter_context(nc.psum_tensor("d_Y", [P, 2, 512], F32))
        H = s_.enter_context(nc.psum_tensor("d_H", [P, S, C], F32))

        t_full, t_free = sem("t_full"), sem("t_free")
        y_full, y_free = sem("y_full"), sem("y_free")
        h_full = sem("h_full")
        chain = sem("chain")
        scaled = sem("scaled")
        zw = sem("zw")
        x_biased = sem("x_biased")
        sc_ready, ex_ready = sem("sc_ready"), sem("ex_ready")
        pp_ready, pp_read = sem("pp_ready"), sem("pp_read")
        o_ready, var_ready = sem("o_ready"), sem("var_ready")
        rstd_ready, normed = sem("rstd_ready"), sem("normed")
        ln_ready = sem("ln_ready")
        half_done = sem("half_done")

        jobs = [("front", 0)]
        for b in range(TPB + 1):
            jobs += ([("oproj", b - 1)] if b else []) + ([("front", b + 1)] if b + 1 < TPB else []) + \
                    ([("router", b - 1)] if b else [])
        TR = 2 * KT

        def t_before(job):
            return TR * jobs.index(job)

        def y_before(job):
            return S * sum(what != "oproj" for what, _ in jobs[:jobs.index(job)])

        PP = 1 + S

        def wait(eng, semaphore, value):
            if value > 0:
                eng.wait_ge(semaphore, value)

        blk = s_.enter_context(nc.Block())

        @blk.tensor
        def _(pe):
            def turn_over(job, src):
                for j in range(TR):
                    kt, half_ = divmod(j, 2)
                    r = t_before(job) + j
                    wait(pe, t_free, r - 1)
                    for i in range(4):
                        mm = pe.transpose(T[:, r % 2, i, :], src(4 * half_ + i, kt), consts["identf"][:, :])
                    mm.then_inc(t_full, 1)
                wait(pe, t_free, t_before(job) + TR)

            def product(out, s, wt):
                for kt in range(KT):
                    mm = pe.matmul(out, zT[:, kt, s * P:(s + 1) * P], wt[:, kt, :],
                                   start=(kt == 0), stop=(kt == KT - 1))
                return mm

            for job in jobs:
                what, b = job
                if what == "front":
                    wait(pe, zw, 2 * (b + 1))
                    turn_over(job, lambda s, kt: z[:, s, kt * P:(kt + 1) * P])
                    wt, width = w["qkv"], QKV
                elif what == "oproj":
                    wait(pe, o_ready, S * (b + 1))
                    turn_over(job, lambda s, kt: o[:, s, kt * P:(kt + 1) * P])
                    wait(pe, var_ready, b)
                    for s in range(S):
                        product(H[:, s, :], s, w["proj"]).then_inc(h_full, 1)
                    continue
                else:
                    wait(pe, ln_ready, 2 * (b + 1))
                    turn_over(job, lambda s, kt: Zv[:, s, b, kt * P:(kt + 1) * P])
                    wt, width = w["router"], EXPERTS
                for s in range(S):
                    r = y_before(job) + s
                    wait(pe, y_free, r - 1)
                    product(Y[:, r % 2, 0:width], s, wt).then_inc(y_full, 1)

        @blk.scalar
        def _(act):
            def scale(b):
                if b:
                    wait(act, t_full, t_before(("front", b - 1)) + TR)
                for s in range(S):
                    j = TPB * s + b
                    mm = act.activation(z[:, s, :], XNv[:, s, b, :], ACT.Copy, scale=again[:, j:j + 1])
                mm.then_inc(scaled, 1)

            def copy_back(job):
                for j in range(TR):
                    kt, half_ = divmod(j, 2)
                    r = t_before(job) + j
                    wait(act, t_full, r + 1)
                    act.copy(zT[:, kt, half_ * 4 * P:(half_ + 1) * 4 * P],
                             T[:, r % 2, :, :].rearrange("p j n -> p (j n)")).then_inc(t_free, 1)

            def front(b):
                job = ("front", b)
                copy_back(job)
                wait(act, o_ready, S * (b - 1))
                for s in range(S):
                    r = y_before(job) + s
                    wait(act, y_full, r + 1)
                    act.copy(q[:, b % 2, s, :].rearrange("p (r g d) -> p g r d", g=KVH, d=HD),
                             Y[:, r % 2, 0:C].rearrange("p (g r d) -> p g r d", g=KVH, d=HD))
                    act.copy(kv[:, b % 2, s, :, :].rearrange("p a d -> p (a d)"),
                             Y[:, r % 2, C:QKV]).then_inc(y_free, 1)

            scale(0)
            front(0)
            for b in range(TPB + 1):
                if b + 1 < TPB:
                    scale(b + 1)
                if b:
                    copy_back(("oproj", b - 1))
                if b + 1 < TPB:
                    front(b + 1)
                if b < TPB:
                    wait(act, sc_ready, b + 1)
                    act.activation(sc[:, :, :, :].rearrange("p s m h -> p (s m h)"),
                                   sc[:, :, :, :].rearrange("p s m h -> p (s m h)"), ACT.Exp,
                                   scale=float(HD) ** -0.5).then_inc(ex_ready, 1)
                if b:
                    wait(act, rstd_ready, 2 * b)
                    for s in range(S):
                        mm = act.activation(Zv[:, s, b - 1, :], h[:, s, :], ACT.Identity,
                                            scale=rstd[:, s:s + 1], bias=nmr[:, s:s + 1])
                    mm.then_inc(normed, 1)
                    job = ("router", b - 1)
                    copy_back(job)
                    for s in range(S):
                        r = y_before(job) + s
                        wait(act, y_full, r + 1)
                        act.copy(Lv[:, s, b - 1, :], Y[:, r % 2, 0:EXPERTS]).then_inc(y_free, 1)

        @blk.gpsimd
        def _(pool):
            def ln1(b):
                wait(pool, scaled, b + 1)
                pool.tensor_tensor(z[:, :, :], z[:, :, :], w["ln1w"][:, :].unsqueeze(1).to_broadcast([P, S, C]),
                                   ALU.mult).then_inc(zw, 1)
                wait(pool, zw, 2 * b + 1)
                pool.tensor_tensor(z[:, :, :], z[:, :, :], w["ln1b"][:, :].unsqueeze(1).to_broadcast([P, S, C]),
                                   ALU.add).then_inc(zw, 1)

            pool.memset(half[:, :], -0.5).then_inc(half_done, 1)
            pool.wait_ge(half_done, 1)
            ln1(0)
            for b in range(TPB + 1):
                if b < TPB:
                    wait(pool, y_free, y_before(("front", b)) + S)
                    wait(pool, pp_read, PP * b - 1)
                    pool.tensor_tensor(
                        prod2[:, (PP * b) % 2, :, :].rearrange("p m (r n) -> p m r n", r=REP),
                        q[:, b % 2, S - 1, :].rearrange("p (r n) -> p r n", r=REP).unsqueeze(1)
                        .to_broadcast([P, S, REP, KV]),
                        kv[:, b % 2, :, 0, :].unsqueeze(2).to_broadcast([P, S, REP, KV]), ALU.mult).then_inc(pp_ready, 1)
                if b + 1 < TPB:
                    ln1(b + 1)
                if b < TPB:
                    xo = Xv[:, :, b, :]
                    pool.tensor_tensor(xo, xo, w["bo"][:, :].unsqueeze(1).to_broadcast([P, S, C]),
                                       ALU.add).then_inc(x_biased, 1)
                if b:
                    wait(pool, var_ready, b)
                    wait(pool, normed, b - 1)
                    pool.tensor_tensor(rstd[:, :], vare[:, :], half[:, :], ALU.pow).then_inc(rstd_ready, 1)
                    wait(pool, rstd_ready, 2 * b - 1)
                    pool.tensor_tensor(nmr[:, :], nmu[:, :], rstd[:, :], ALU.mult).then_inc(rstd_ready, 1)
                if b < TPB:
                    wait(pool, ex_ready, b + 1)
                    for s in range(S):
                        m = s + 1
                        r = PP * b + 1 + s
                        wait(pool, pp_read, r - 1)
                        pool.tensor_tensor(
                            prod2[:, r % 2, 0:m, :].rearrange("p m (r g d) -> p m r g d", r=REP, d=HD),
                            kv[:, b % 2, 0:m, 1, :].rearrange("p m (g d) -> p m g d", g=KVH).unsqueeze(2)
                            .to_broadcast([P, m, REP, KVH, HD]),
                            sc[:, s, 0:m, :].rearrange("p m (r g) -> p m r g", r=REP).unsqueeze(4)
                            .to_broadcast([P, m, REP, KVH, HD]), ALU.mult).then_inc(pp_ready, 1)

        @blk.vector
        def _(dve):
            n = [0]

            def link(ins):
                n[0] += 1
                ins.then_inc(chain, 1)
                dve.wait_ge(chain, n[0])

            def by_head(rows, m):
                return rows.rearrange("p m (h d) -> p (m h) d", d=HD)

            link(dve.memset(carry[:, :], 0.0))
            for b in range(TPB + 1):
                if b < TPB:
                    link(dve.memset(sc[:, :, :, :].rearrange("p s m h -> p (s m h)"), NEG))
                    wait(dve, y_free, y_before(("front", b)) + S)
                    for s in range(S - 1):
                        m = s + 1
                        link(dve.tensor_tensor(
                            prod[:, 0:m, :].rearrange("p m (r n) -> p m r n", r=REP),
                            q[:, b % 2, s, :].rearrange("p (r n) -> p r n", r=REP).unsqueeze(1)
                            .to_broadcast([P, m, REP, KV]),
                            kv[:, b % 2, 0:m, 0, :].unsqueeze(2).to_broadcast([P, m, REP, KV]), ALU.mult))
                        link(dve.tensor_reduce(sc[:, s, 0:m, :].rearrange("p m h -> p (m h)"),
                                               by_head(prod[:, 0:m, :], m), AX.X, ALU.add))
                    wait(dve, pp_ready, PP * b + 1)
                    dve.tensor_reduce(sc[:, S - 1, :, :].rearrange("p m h -> p (m h)"),
                                      by_head(prod2[:, (PP * b) % 2, :, :], S), AX.X, ALU.add).then_inc(pp_read, 1)
                    wait(dve, pp_read, PP * b + 1)
                    by_key = sc[:, :, :, :].rearrange("p s m h -> p s h m")
                    link(dve.tensor_reduce(top[:, :, :], by_key, AX.X, ALU.max))
                    dve.tensor_tensor(sc[:, :, :, :], sc[:, :, :, :],
                                      top[:, :, :].unsqueeze(2).to_broadcast([P, S, S, HEADS]),
                                      ALU.subtract).then_inc(sc_ready, 1)
                if b:
                    wait(dve, normed, b - 1)
                    for i in range(0, S, 2):
                        wait(dve, h_full, S * (b - 1) + i + 2)
                        ins = dve.tensor_tensor(h[:, i:i + 2, :], H[:, i:i + 2, :], XNv[:, i:i + 2, b - 1, :], ALU.add)
                    link(ins)
                    for s in range(S):
                        ins = dve.bn_stats(stats[:, s, :], h[:, s, :])
                    link(ins)
                    dve.tensor_copy(carry[:, 1:2], carry[:, 0:1])
                    for s in range(S):
                        ins = dve.bn_aggr(mv[:, s, :], stats[:, s, :])
                    link(ins)
                    wait(dve, rstd_ready, 2 * (b - 1))
                    dve.tensor_scalar(nmu[:, :], mv[:, :, 0], -1.0, None, ALU.mult)
                    dve.tensor_scalar(vare[:, :], mv[:, :, 1], 1e-5, None, ALU.add).then_inc(var_ready, 1)
                    wait(dve, x_biased, b)
                    xo = Xv[:, :, b - 1, :]
                    dve.tensor_tensor(xo, xo, h[:, :, :], ALU.add)
                if b < TPB:
                    wait(dve, ex_ready, b + 1)
                    link(dve.tensor_reduce(sums[:, :, :], by_key, AX.X, ALU.add))
                    link(dve.reciprocal(den[:, :, :], sums[:, :, :]))
                if b:
                    wait(dve, normed, b)
                    zo = Zv[:, :, b - 1, :]
                    dve.tensor_tensor(zo, zo, w["ln2w"][:, :].unsqueeze(1).to_broadcast([P, S, C]),
                                      ALU.mult).then_inc(ln_ready, 1)
                    wait(dve, ln_ready, 2 * b - 1)
                    dve.tensor_tensor(zo, zo, w["ln2b"][:, :].unsqueeze(1).to_broadcast([P, S, C]),
                                      ALU.add).then_inc(ln_ready, 1)
                if b < TPB:
                    if b:
                        wait(dve, t_full, t_before(("oproj", b - 1)) + TR)
                    for s in range(S):
                        m = s + 1
                        r = PP * b + 1 + s
                        wait(dve, pp_ready, r + 1)
                        dve.tensor_reduce(prod[:, s, :], prod2[:, r % 2, 0:m, :].rearrange("p m c -> p c m"),
                                          AX.X, ALU.add).then_inc(pp_read, 1)
                        wait(dve, pp_read, r + 1)
                        dve.tensor_tensor(o[:, s, :].rearrange("p (g r d) -> p r g d", g=KVH, d=HD),
                                          prod[:, s, :].rearrange("p (r g d) -> p r g d", g=KVH, d=HD),
                                          den[:, s, :].rearrange("p (r g) -> p r g", g=KVH).unsqueeze(3)
                                          .to_broadcast([P, REP, KVH, HD]), ALU.mult).then_inc(o_ready, 1)


def route(nc, logits, slot_id, gather_id, gate, consts):
    G, E = NT, EXPERTS
    with ExitStack() as s:
        def sb(nm, shape, dt=F32):
            return s.enter_context(nc.sbuf_tensor("r_" + nm, shape, dt))

        prb = sb("prb", [P, G, E])
        eq = sb("eq", [P, G, E])
        rest = sb("rest", [P, G, E])
        hot = [sb(f"hot{k}", [P, G, E]) for k in range(2)]
        top = [sb(f"top{k}", [P, G]) for k in range(2)]
        best = sb("best", [P, G])
        member = sb("member", [P, G * E], BF16)
        run = [sb(f"run{k}", [P, G, E]) for k in range(2)]
        place = sb("place", [P, G])
        expert = sb("expert", [P, G])
        keep = sb("keep", [P, G])
        lost = sb("lost", [P, G])
        ps = s.enter_context(nc.psum_tensor("r_ps", [P, 2, G * E], F32))
        chain = s.enter_context(nc.semaphore("r_chain"))
        exp_in, exp_out = s.enter_context(nc.semaphore("r_exp_in")), s.enter_context(nc.semaphore("r_exp_out"))
        mem_ready, cum_ready = s.enter_context(nc.semaphore("r_mem")), s.enter_context(nc.semaphore("r_cum"))
        blk = s.enter_context(nc.Block())

        @blk.scalar
        def _(act):
            act.wait_ge(exp_in, 1)
            act.activation(prb[:, :, :], prb[:, :, :], ACT.Exp).then_inc(exp_out, 1)

        @blk.tensor
        def _(pe):
            pe.wait_ge(mem_ready, 1)
            pe.matmul(ps[:, 0, :], consts["before"][:, :], member[:, :], start=True, stop=True)
            pe.matmul(ps[:, 1, :], consts["ones"][:, :], member[:, :], start=True, stop=True).then_inc(cum_ready, 1)

        @blk.vector
        def _(dve):
            steps = [0]

            def link(ins):
                steps[0] += 1
                ins.then_inc(chain, 1)
                dve.wait_ge(chain, steps[0])

            def wide(x):
                return x.unsqueeze(2).to_broadcast([P, G, E])

            link(dve.tensor_reduce(top[0][:, :], logits[:, :, :], AX.X, ALU.max))
            dve.tensor_tensor(prb[:, :, :], logits[:, :, :], wide(top[0][:, :]), ALU.subtract).then_inc(exp_in, 1)
            dve.wait_ge(exp_out, 1)
            link(dve.tensor_reduce(best[:, :], prb[:, :, :], AX.X, ALU.add))
            link(dve.reciprocal(best[:, :], best[:, :]))
            link(dve.tensor_tensor(prb[:, :, :], prb[:, :, :], wide(best[:, :]), ALU.mult))
            top_two(dve, link, prb[:, :, :], consts["desc16"][:, :].unsqueeze(1).to_broadcast([P, G, E]),
                    eq[:, :, :], [t[:, :] for t in top], best[:, :], [x[:, :, :] for x in hot], rest[:, :, :])
            dve.tensor_tensor(member[:, :].rearrange("p (g e) -> p g e", e=E), hot[0][:, :, :], hot[1][:, :, :],
                              ALU.add).then_inc(mem_ready, 1)
            dve.wait_ge(cum_ready, 1)
            link(dve.tensor_copy(run[0][:, :, :], ps[:, 1, :].rearrange("p (g e) -> p g e", e=E)))
            a, b, d = 0, 1, 1
            while d < G:
                link(dve.tensor_tensor(run[b][:, d:G, :], run[a][:, d:G, :], run[a][:, 0:G - d, :], ALU.add))
                link(dve.tensor_copy(run[b][:, 0:d, :], run[a][:, 0:d, :]))
                a, b, d = b, a, 2 * d
            link(dve.tensor_copy(run[b][:, 0, :], ps[:, 0, 0:E]))
            link(dve.tensor_tensor(run[b][:, 1:G, :], run[a][:, 0:G - 1, :],
                                   ps[:, 0, :].rearrange("p (g e) -> p g e", e=E)[:, 1:G, :], ALU.add))
            for k in range(2):
                link(dve.tensor_tensor(eq[:, :, :], run[b][:, :, :], hot[k][:, :, :], ALU.mult))
                link(dve.tensor_reduce(place[:, :], eq[:, :, :], AX.X, ALU.add))
                link(dve.tensor_tensor(eq[:, :, :], hot[k][:, :, :],
                                       consts["base16"][:, :].unsqueeze(1).to_broadcast([P, G, E]), ALU.mult))
                link(dve.tensor_reduce(expert[:, :], eq[:, :, :], AX.X, ALU.add))
                link(dve.tensor_scalar(keep[:, :], place[:, :], float(CAP), None, ALU.is_lt))
                link(dve.tensor_tensor(place[:, :], place[:, :], expert[:, :], ALU.add))
                link(dve.tensor_tensor(gate[:, :, k], top[k][:, :], keep[:, :], ALU.mult))
                link(dve.tensor_tensor(place[:, :], place[:, :], keep[:, :], ALU.mult))
                link(dve.tensor_copy(gather_id[:, :, k], place[:, :]))
                link(dve.tensor_scalar(lost[:, :], keep[:, :], -float(2 * SLOTROWS), float(2 * SLOTROWS),
                                       ALU.mult, ALU.add))
                link(dve.tensor_tensor(lost[:, :], place[:, :], lost[:, :], ALU.add))
                link(dve.tensor_copy(slot_id[:, :, k], lost[:, :]))


def experts(nc, Z, slot_id, consts, dram):
    E = EXPERTS
    FT = FFN // P
    with ExitStack() as s:
        def sb(nm, shape, dt=F32):
            return s.enter_context(nc.sbuf_tensor("e_" + nm, shape, dt))

        def sem(nm):
            return s.enter_context(nc.semaphore("e_" + nm))

        w1 = sb("w1", [P, 2, KT, FFN])
        w2 = sb("w2", [P, 2, FT, C])
        rows = sb("rows", [P, 2, CT, C])
        rowsT = sb("rowsT", [P, 2, KT, CAP])
        hid = sb("hid", [P, FT, CAP])
        outs = sb("outs", [P, 2, CT, C])
        RT = s.enter_context(nc.psum_tensor("e_RT", [P, 2 * 512], F32))
        OB = s.enter_context(nc.psum_tensor("e_OB", [P, 2, 512], F32))
        HB = s.enter_context(nc.psum_tensor("e_HB", [P, 2, 2, 512], F32))
        HC = CAP // 2
        scattered = sem("scattered")
        w_in = [sem("w_in0"), sem("w_in1")]
        rows_in = [sem("rows_in0"), sem("rows_in1")]
        t_full, t_free = sem("t_full"), sem("t_free")
        h_full, h_free = sem("h_full"), sem("h_free")
        o_full, o_free = sem("o_full"), sem("o_free")
        stored = [sem("stored0"), sem("stored1")]
        blk = s.enter_context(nc.Block())

        def turns(eng, body):
            for e in range(2):
                body(e, e, 0)
            with eng.Fori(1, E // 2 - 1) as pair:
                for e in range(2):
                    body(2 * pair + e, e, pair)
            for e in range(E - 2, E):
                body(e, e % 2, e // 2)

        def last(e):
            return isinstance(e, int) and e == E - 1

        @blk.sync
        def _(sp):
            def load_weights(e, par):
                sp.dma_start(w1[:, par, :, :], dram["w1"][:, bass.ds(e, 1), :, :].rearrange("p e k f -> p (e k) f"))\
                  .then_inc(w_in[par], 16)
                sp.dma_start(w2[:, par, :, :], dram["w2"][:, bass.ds(e, 1), :, :].rearrange("p e k c -> p (e k) c"))\
                  .then_inc(w_in[par], 16)

            def body(e, par, pair):
                if isinstance(e, int) and e < 2:
                    if e == 0:
                        load_weights(0, 0)
                        load_weights(1, 1)
                        sp.wait_ge(scattered, 16 * NT * TOPK)
                    sp.dma_start(rows[:, par, :, :], dram["rows_v"][:, bass.ds(CT * e, CT), :])\
                      .then_inc(rows_in[par], 16)
                    return
                sp.wait_ge(t_full, KT * (e - 1))
                sp.dma_start(rows[:, par, :, :], dram["rows_v"][:, bass.ds(CT * e, CT), :]).then_inc(rows_in[par], 16)
                sp.wait_ge(o_full, CT * (e - 1))
                load_weights(e, par)

            turns(sp, body)

        @blk.gpsimd
        def _(pool):
            for j in range(NT):
                for k in range(TOPK):
                    pool.indirect_dma_start(dram["rows"], bass.IndirectOffsetOnAxis(ap=slot_id[:, j, k:k + 1], axis=0),
                                            Z[:, j, :], None, bounds_check=SLOTROWS - 1,
                                            oob_is_err=False).then_inc(scattered, 16)

            def body(e, par, pair):
                pool.wait_ge(o_free, CT * (e + 1))
                pool.dma_start(dram["outs_v"][:, bass.ds(CT * e, CT), :], outs[:, par, :, :]).then_inc(stored[par], 16)

            turns(pool, body)
            for par in range(2):
                pool.wait_ge(stored[par], 16 * (E // 2))

        @blk.tensor
        def _(pe):
            def turn_over(e, par, pair, kt):
                if kt == 0:
                    pe.wait_ge(rows_in[par], 16 * (pair + 1))
                if not isinstance(e, int) or KT * e + kt > 0:
                    pe.wait_ge(t_free, KT * e + kt)
                for c in range(CT):
                    mm = pe.transpose(RT[:, c * P:(c + 1) * P], rows[:, par, c, kt * P:(kt + 1) * P],
                                      consts["identf"][:, :])
                mm.then_inc(t_full, 1)

            def body(e, par, pair):
                pe.wait_ge(w_in[par], 32 * (pair + 1))
                pe.wait_ge(t_free, KT * (e + 1))
                for f in range(FT):
                    r = FT * e + f
                    if not isinstance(r, int) or r >= 2:
                        pe.wait_ge(h_free, r - 1)
                    for half_ in range(2):
                        for kt in range(KT):
                            mm = pe.matmul(HB[:, f % 2, half_, 0:HC], w1[:, par, kt, f * P:(f + 1) * P],
                                           rowsT[:, par, kt, half_ * HC:(half_ + 1) * HC],
                                           start=(kt == 0), stop=(kt == KT - 1))
                    mm.then_inc(h_full, 1)
                    if f % 2 and not last(e):
                        turn_over(e + 1, 1 - par, pair + par, f // 2)
                pe.wait_ge(h_free, FT * (e + 1))
                for c in range(CT):
                    r = CT * e + c
                    if not isinstance(r, int) or r >= 2:
                        pe.wait_ge(o_free, r - 1)
                    for f in range(FT):
                        mm = pe.matmul(OB[:, (CT * par + c) % 2, 0:C], hid[:, f, c * P:(c + 1) * P],
                                       w2[:, par, f, :], start=(f == 0), stop=(f == FT - 1))
                    mm.then_inc(o_full, 1)

            for kt in range(KT):
                turn_over(0, 0, 0, kt)
            turns(pe, body)

        @blk.scalar
        def _(act):
            def body(e, par, pair):
                for f in range(FT):
                    act.wait_ge(h_full, FT * e + f + 1)
                    act.activation(hid[:, f, :].rearrange("p (a n) -> p a n", a=2), HB[:, f % 2, :, 0:HC],
                                   ACT.Gelu_apprx_tanh).then_inc(h_free, 1)

            turns(act, body)

        @blk.vector
        def _(dve):
            def copy_rows(e, par, kt):
                dve.wait_ge(t_full, KT * e + kt + 1)
                dve.tensor_copy(rowsT[:, par, kt, :], RT[:, 0:CAP]).then_inc(t_free, 1)

            def body(e, par, pair):
                if not last(e):
                    for kt in range(KT):
                        copy_rows(e + 1, 1 - par, kt)
                for c in range(CT):
                    dve.wait_ge(o_full, CT * e + c + 1)
                    if c == 0 and not (isinstance(pair, int) and pair == 0):
                        dve.wait_ge(stored[par], 16 * pair)
                    dve.tensor_copy(outs[:, par, c, :], OB[:, (CT * par + c) % 2, 0:C]).then_inc(o_free, 1)

            for kt in range(KT):
                copy_rows(0, 0, kt)
            turns(dve, body)


def two_layers(nc, d, out):
    rows_d = nc.dram_tensor("expert_rows", (SLOTROWS, C), F32, kind="Internal").ap()
    outs_d = nc.dram_tensor("expert_outs", (SLOTROWS, C), F32, kind="Internal").ap()
    out_v = out.rearrange("b (t p) c -> p (b t) c", p=P)
    x_v = d["x"].rearrange("b (t p) c -> p (b t) c", p=P)
    with ExitStack() as s:
        def sb(nm, shape, dt=F32, st=s):
            return st.enter_context(nc.sbuf_tensor(nm, shape, dt))

        X = sb("X", [P, NT, C])
        identf = sb("identf", [P, P])
        identb = sb("identb", [P, P], BF16)
        mask_kq = sb("mask_kq", [P, P], BF16)
        mask_qk = sb("mask_qk", [P, P], BF16)
        before = sb("before", [P, P], BF16)
        ones = sb("ones", [P, P], BF16)
        desc16 = sb("desc16", [P, EXPERTS])
        base16 = sb("base16", [P, EXPERTS])
        consts = dict(identf=identf, identb=identb, mask_kq=mask_kq, mask_qk=mask_qk, before=before,
                      ones=ones, desc16=desc16, base16=base16)
        zeroed = s.enter_context(nc.semaphore("zeroed"))

        with ExitStack() as l0:
            w = {}
            w["WA"] = sb("WA", [P, KT, GROUPS, 3 * GW], st=l0)
            w["WB"] = sb("WB", [P, KT, GROUPS, 3 * GW], st=l0)
            w["WoA"] = sb("WoA", [P, KT, C], st=l0)
            w["WoB"] = sb("WoB", [P, KT, C], st=l0)
            w["V"] = sb("V", [P, 4, C], st=l0)
            w["UT"] = sb("UT", [P, 4, C], st=l0)
            w["gS"] = sb("gS", [P, 4, BATCH], st=l0)
            w["bA"] = sb("bA", [P, GROUPS, 3 * GW], st=l0)
            w["bB"] = sb("bB", [P, GROUPS, 3 * GW], st=l0)
            w["bout"] = sb("bout", [P, C], st=l0)
            w["qkn"] = sb("qkn", [P, 2, HD], st=l0)
            with ExitStack() as g0:
                zeros = sb("zeros", [P, 2048], st=g0)
                stage = sb("stage", [P, 5, P], st=g0)
                b2 = sb("b2", [P, C], st=g0)
                S4 = sb("S4", [P, 4], st=g0)
                gw = dict(gw1=sb("gw1", [P, KT, 64], st=g0), gw2=sb("gw2", [64, 8], st=g0),
                          gb1=sb("gb1", [64, 1], st=g0), gb2=sb("gb2", [BATCH, 8], st=g0),
                          rep=sb("rep", [8, P], st=g0), desc8=sb("desc8", [BATCH, 8], st=g0))
                with ExitStack() as q:
                    x_in = q.enter_context(nc.semaphore("x_in"))
                    w_in = q.enter_context(nc.semaphore("w_in"))
                    z_set = q.enter_context(nc.semaphore("z_set"))
                    blk = q.enter_context(nc.Block())

                    @blk.sync
                    def _(sp):
                        for b in range(4):
                            sp.dma_start(X[:, 8 * b:8 * b + 8, :], x_v[:, 8 * b:8 * b + 8, :]).then_inc(x_in, 16)
                        sp.wait_ge(x_in, 64)

                    @blk.scalar
                    def _(act):
                        loads = [(stage[:, :, :], d["c_stage"]), (identf[:, :], d["c_ident"]),
                                 (desc16[:, :], d["c_desc16"].partition_broadcast(P)),
                                 (base16[:, :], d["c_base16"].partition_broadcast(P)),
                                 (w["WA"][:, :, :, :], d["WA"].rearrange("(k p) g n -> p k g n", p=P)),
                                 (w["WB"][:, :, :, :], d["WB"].rearrange("(k p) g n -> p k g n", p=P)),
                                 (w["WoA"][:, :, :], d["WoA"].rearrange("(k p) n -> p k n", p=P)),
                                 (w["WoB"][:, :, :], d["WoB"].rearrange("(k p) n -> p k n", p=P)),
                                 (w["V"][:, :, :], d["V4"].rearrange("j p n -> p j n")),
                                 (w["UT"][:, :, :], d["UT4"].rearrange("j p n -> p j n")),
                                 (w["bA"][:, :, :], d["bA"].partition_broadcast(P)),
                                 (w["bB"][:, :, :], d["bB"].partition_broadcast(P)),
                                 (w["bout"][:, :], d["boA"].partition_broadcast(P)),
                                 (b2[:, :], d["boB"].partition_broadcast(P)),
                                 (w["qkn"][:, 0, :], d["qn"].partition_broadcast(P)),
                                 (w["qkn"][:, 1, :], d["kn"].partition_broadcast(P)),
                                 (S4[:, :], d["S4"]),
                                 (gw["gw1"][:, :, :], d["gw1T"].rearrange("(k p) n -> p k n", p=P)),
                                 (gw["gw2"][:, :], d["gw2T"]), (gw["gb1"][:, :], d["gb1"]),
                                 (gw["gb2"][:, :], d["gb2"].partition_broadcast(BATCH)),
                                 (gw["rep"][:, :], d["c_rep"]),
                                 (gw["desc8"][:, :], d["c_desc8"].partition_broadcast(BATCH))]
                        for dst, src in loads:
                            act.dma_start(dst, src).then_inc(w_in, 16)
                        act.wait_ge(w_in, 16 * len(loads))

                    @blk.vector
                    def _(dve):
                        dve.memset(zeros[:, :], 0.0).then_inc(z_set, 1)
                        dve.memset(ones[:, :], 1.0)
                        dve.wait_ge(w_in, 16 * 23)
                        for dst, j in ((identb, 0), (mask_kq, 1), (mask_qk, 2), (before, 3)):
                            dve.tensor_copy(dst[:, :], stage[:, j, :])
                        dve.tensor_tensor(w["bout"][:, :], w["bout"][:, :], b2[:, :], ALU.add)

                    @blk.gpsimd
                    def _(pool):
                        pool.wait_ge(z_set, 1)
                        pool.wait_ge(x_in, 64)
                        pool.wait_ge(w_in, 16 * 23)
                        zv = rows_d.rearrange("(a p q) c -> a p (q c)", p=P, q=8)
                        for a in range(ZFILLS):
                            pool.dma_start(zv[a], zeros[:, :]).then_inc(zeroed, 16)

                layernorm(nc, "ln0", X, X, 1e-5)
                gates(nc, X, gw, w["gS"], consts, S4, zeroed)
            attention(nc, "L0", 0, X, X, w, consts, dict(x=x_v))

        XN = sb("XN", [P, NT, C])
        again = sb("again", [P, NT])
        gather_id = sb("gather_id", [P, NT, TOPK], U32)
        gate = sb("gate", [P, NT, TOPK])
        layernorm(nc, "ln1", X, XN, 1e-5, again)
        with ExitStack() as m:
            Z = sb("Z", [P, NT, C], st=m)
            logits = sb("logits", [P, NT, EXPERTS], st=m)
            slot_id = sb("slot_id", [P, NT, TOPK], U32, st=m)
            with ExitStack() as q:
                w = dict(qkv=sb("Dqkv", [P, KT, C + 8 * HD], st=q), proj=sb("Dproj", [P, KT, C], st=q),
                         router=sb("Drouter", [P, KT, EXPERTS], st=q), ln1w=sb("Dln1w", [P, C], st=q),
                         ln1b=sb("Dln1b", [P, C], st=q), ln2w=sb("Dln2w", [P, C], st=q),
                         ln2b=sb("Dln2b", [P, C], st=q), bo=sb("Dbo", [P, C], st=q))
                with ExitStack() as q2:
                    w_in = q2.enter_context(nc.semaphore("d_w_in"))
                    blk = q2.enter_context(nc.Block())

                    @blk.sync
                    def _(sp):
                        for dst, src in ((w["qkv"], "DqkvT"), (w["proj"], "DprojT"), (w["router"], "DrouterT")):
                            sp.dma_start(dst[:, :, :], d[src].rearrange("(k p) n -> p k n", p=P)).then_inc(w_in, 16)
                        for dst, src in ((w["ln1w"], "ln1w"), (w["ln1b"], "ln1b"), (w["ln2w"], "ln2w"),
                                         (w["ln2b"], "ln2b"), (w["bo"], "boC")):
                            sp.dma_start(dst[:, :], d[src].partition_broadcast(P)).then_inc(w_in, 16)
                        sp.wait_ge(w_in, 16 * 8)

                block_d(nc, X, XN, Z, again, logits, w, consts)
            route(nc, logits, slot_id, gather_id, gate, consts)
            experts(nc, Z, slot_id, consts,
                    dict(w1=d["w1T"].rearrange("e (k p) f -> p e k f", p=P),
                         w2=d["w2T"].rearrange("e (k p) c -> p e k c", p=P), rows=rows_d, outs=outs_d,
                         rows_v=rows_d.rearrange("(t p) c -> p t c", p=P),
                         outs_v=outs_d.rearrange("(t p) c -> p t c", p=P)))
        with ExitStack() as q:
            w = dict(WC=sb("WC", [P, KT, GROUPS, 3 * GW], st=q), WoC=sb("WoC", [P, KT, C], st=q),
                     bC=sb("bC", [P, GROUPS, 3 * GW], st=q), cos=sb("cos", [P, TPB, HD // 2], st=q),
                     sin=sb("sin", [P, TPB, HD // 2], st=q), gather_id=gather_id, gate=gate)
            with ExitStack() as q2:
                w_in = q2.enter_context(nc.semaphore("c_w_in"))
                blk = q2.enter_context(nc.Block())

                @blk.sync
                def _(sp):
                    sp.dma_start(w["WC"][:, :, :, :], d["WC"].rearrange("(k p) g n -> p k g n", p=P)).then_inc(w_in, 16)
                    sp.dma_start(w["WoC"][:, :, :], d["WoC"].rearrange("(k p) n -> p k n", p=P)).then_inc(w_in, 16)
                    sp.dma_start(w["bC"][:, :, :], d["bC"].partition_broadcast(P)).then_inc(w_in, 16)
                    sp.dma_start(w["cos"][:, :, :], d["c_cos"].rearrange("(t p) n -> p t n", p=P)).then_inc(w_in, 16)
                    sp.dma_start(w["sin"][:, :, :], d["c_sin"].rearrange("(t p) n -> p t n", p=P)).then_inc(w_in, 16)
                    sp.wait_ge(w_in, 16 * 5)

            attention(nc, "L1", 1, X, XN, w, consts, dict(out=out_v, outs=outs_d))


def kernel(**inputs):
    import numpy as np
    import concourse.bacc as _bacc
    from concourse import mybir as _mybir
    from concourse.bass_utils import run_bass_kernel_spmd as _run

    a = {k: np.asarray(v) for k, v in inputs.items()}

    def grouped(parts):
        return np.stack([m.reshape(m.shape[0], GROUPS, GW) for m in parts], axis=2).reshape(-1, GROUPS, 3 * GW)

    def grouped_bias(parts):
        return np.stack([m.reshape(GROUPS, GW) for m in parts], axis=1).reshape(GROUPS, 3 * GW)

    n = {}
    n["x"] = a["L0_attn_x"]
    wa = a["L0_attn_W_qkv"]
    n["WA"] = grouped([wa[:, 0:C], wa[:, C:2 * C], wa[:, 2 * C:]])
    ba = a["L0_attn_b_qkv"]
    n["bA"] = grouped_bias([ba[0:C], ba[C:2 * C], ba[2 * C:]])
    n["WoA"] = a["L0_attn_W_proj"]
    n["boA"] = a["L0_attn_b_proj"]
    n["qn"], n["kn"] = a["L0_attn_qn_w"], a["L0_attn_kn_w"]
    n["WB"] = grouped([a[f"L0_ffn_{p}Wm"].T for p in "qkv"])
    n["bB"] = grouped_bias([a[f"L0_ffn_{p}b"] for p in "qkv"])
    n["WoB"] = a["L0_ffn_oWm"].T
    n["boB"] = a["L0_ffn_ob"]
    n["V4"] = np.stack([a[f"L0_ffn_{p}V"].reshape(P, C) for p in "qkvo"])
    n["UT4"] = np.stack([a[f"L0_ffn_{p}U"].transpose(0, 2, 1).reshape(P, C) for p in "qkvo"])
    n["S4"] = np.stack([a[f"L0_ffn_{p}S"].reshape(P) for p in "qkvo"], axis=1)
    n["gw1T"], n["gw2T"] = a["L0_ffn_gw1"].T, a["L0_ffn_gw2"].T
    n["gb1"], n["gb2"] = a["L0_ffn_gb1"].reshape(-1, 1), a["L0_ffn_gb2"]
    n["WC"] = grouped([a[f"L1_attn_W{p}"].T for p in "qkv"])
    n["bC"] = grouped_bias([a[f"L1_attn_b{p}"] for p in "qkv"])
    n["WoC"], n["boC"] = a["L1_attn_Wo"].T, a["L1_attn_bo"]
    n["DqkvT"] = a["L1_ffn_qkv_weight"].T
    n["DprojT"] = a["L1_ffn_proj_weight"].T
    n["DrouterT"] = a["L1_ffn_router_weight"].T
    for m in ("ln1", "ln2"):
        n[m + "w"], n[m + "b"] = a[f"L1_ffn_{m}_weight"], a[f"L1_ffn_{m}_bias"]
    n["w1T"] = a["L1_ffn_moe_w1"].transpose(0, 2, 1)
    n["w2T"] = a["L1_ffn_moe_w2"].transpose(0, 2, 1)

    f = np.float32
    i = np.arange(P)
    behind = np.where(i[:, None] > i[None, :], f(NEG), f(0))
    n["c_ident"] = np.eye(P, dtype=f)
    n["c_stage"] = np.stack([np.eye(P, dtype=f), behind, behind.T, (i[:, None] < i[None, :]).astype(f),
                             np.zeros((P, P), f)], axis=1)
    n["c_desc16"] = f(EXPERTS) - np.arange(EXPERTS, dtype=f)
    n["c_base16"] = f(CAP) * np.arange(EXPERTS, dtype=f)
    n["c_desc8"] = f(8) - np.arange(8, dtype=f)
    n["c_rep"] = (np.arange(8)[:, None] == i[None, :] // 16).astype(f)
    theta = (f(1.0) / f(10000.0)) ** (f(2.0) * np.arange(HD // 2, dtype=f) / f(HD))
    angle = np.arange(1, SEQ + 1, dtype=f)[:, None] * theta.astype(f)
    n["c_cos"], n["c_sin"] = np.cos(angle).astype(f), np.sin(angle).astype(f)

    nc = _bacc.Bacc("TRN2", target_bir_lowering=False, num_devices=1)
    arrays, d = {}, {}
    for name, arr in n.items():
        arr = np.ascontiguousarray(arr)
        arrays[f"in_{name}"] = arr
        d[name] = nc.dram_tensor(f"in_{name}", arr.shape, _mybir.dt.from_np(arr.dtype), kind="ExternalInput").ap()
    out = nc.dram_tensor("out_0", (BATCH, SEQ, C), F32, kind="ExternalOutput").ap()
    two_layers(nc, d, out)
    r = _run(nc, [arrays], core_ids=[0])
    return r.results[0]["out_0"]
```

```python
from contextlib import ExitStack

import concourse.bass as bass
from concourse import mybir

F32 = mybir.dt.float32
BF16 = mybir.dt.bfloat16
I32 = mybir.dt.int32
U32 = mybir.dt.uint32
ALU = mybir.AluOpType
ACT = mybir.ActivationFunctionType
AX = mybir.AxisListType

P = 128
BATCH, SEQ, C = 8, 512, 256
HEADS, HD = 16, 16
TOK = BATCH * SEQ
NT = TOK // P
TPB = SEQ // P
KT = C // P
GH = 4
GROUPS = HEADS // GH
GW = GH * HD
CYCLE = 8

SLOTS = 7
QPART = (0, 0, 0, 1, 1, 1, 2)
KPART = (0, 1, 2, 0, 1, 2, 0)
MPARTS = 3
NEG = -1.0e30

EXPERTS, FFN, TOPK = 16, 512, 2
CAP = -(-TOK * TOPK * 5 // (EXPERTS * 4))
SLOTROWS = EXPERTS * CAP
CT = CAP // P
GATES_LOADS = 23
ZFILLS = SLOTROWS // (8 * P)


def layernorm(nc, name, src, dst, eps, again=None, loads=(), arriving=None, stats=None,
              pooling=None):
    SPAN, BY_VECTOR = 8, 5
    with ExitStack() as s:
        ready = stats is not None
        if not ready:
            stats = s.enter_context(nc.sbuf_tensor(name + "_stats", [P, NT, 6], F32))
        mv = s.enter_context(nc.sbuf_tensor(name + "_mv", [P, NT, 2], F32))
        half = s.enter_context(nc.sbuf_tensor(name + "_half", [P, NT], F32))
        vare = s.enter_context(nc.sbuf_tensor(name + "_vare", [P, NT], F32))
        rstd = s.enter_context(nc.sbuf_tensor(name + "_rstd", [P, NT], F32))
        nmr = s.enter_context(nc.sbuf_tensor(name + "_nmr", [P, NT], F32))
        stat_done = s.enter_context(nc.semaphore(name + "_stat_done"))
        aggr_done = s.enter_context(nc.semaphore(name + "_aggr_done"))
        var_done = s.enter_context(nc.semaphore(name + "_var_done"))
        rstd_done = s.enter_context(nc.semaphore(name + "_rstd_done"))
        nmr_done = s.enter_context(nc.semaphore(name + "_nmr_done"))
        half_done = s.enter_context(nc.semaphore(name + "_half_done"))
        mean_set = s.enter_context(nc.semaphore(name + "_mean_set"))
        by_vector = s.enter_context(nc.semaphore(name + "_by_vector"))
        by_scalar = s.enter_context(nc.semaphore(name + "_by_scalar"))
        blk = s.enter_context(nc.Block())

        if loads:
            @blk.sync
            def _(sp):
                for to, fro, semaphore in loads:
                    sp.dma_start(to, fro).then_inc(semaphore, 16)

        @blk.vector
        def _(dve):
            if pooling is not None:
                dve.memset(pooling[0][:, :], 0.0).then_inc(mean_set, 1)
                dve.wait_ge(mean_set, 1)
                dve.memset(pooling[0][:, 0:BATCH * BATCH:BATCH + 1], 1.0 / SEQ).then_inc(mean_set, 1)
            if not ready:
                for b in range(BATCH):
                    dve.wait_ge(arriving[b], 16)
                    for j in range(TPB * b, TPB * (b + 1)):
                        dve.bn_stats(stats[:, j, :], src[:, j, :]).then_inc(stat_done, 1)
                dve.wait_ge(stat_done, NT)
            for j in range(NT):
                ins = dve.bn_aggr(mv[:, j, :], stats[:, j, :])
            ins.then_inc(aggr_done, 1)
            dve.wait_ge(aggr_done, 1)
            dve.tensor_scalar(vare[:, :], mv[:, :, 1], eps, None, ALU.add).then_inc(var_done, 1)
            dve.wait_ge(rstd_done, 1)
            dve.scalar_tensor_tensor(out=nmr[:, :], in0=mv[:, :, 0], scalar=-1.0, in1=rstd[:, :],
                                     op0=ALU.mult, op1=ALU.mult).then_inc(nmr_done, 1)
            if again is not None:
                dve.tensor_tensor(vare[:, :], mv[:, :, 1], rstd[:, :], ALU.mult).then_inc(var_done, 1)
                dve.wait_ge(var_done, 2)
                dve.tensor_tensor(vare[:, :], vare[:, :], rstd[:, :], ALU.mult).then_inc(var_done, 1)
                dve.wait_ge(var_done, 3)
                dve.tensor_scalar(vare[:, :], vare[:, :], eps, None, ALU.add).then_inc(var_done, 1)
            with dve.Fori(0, NT // SPAN) as a:
                for t in range(BY_VECTOR):
                    j = SPAN * a + t
                    dve.tensor_scalar(dst[:, bass.ds(j, 1), :], src[:, bass.ds(j, 1), :],
                                      mv[:, bass.ds(j, 1), 0], rstd[:, bass.ds(j, 1)],
                                      ALU.subtract, ALU.mult).then_inc(by_vector, 1)

        @blk.scalar
        def _(act):
            act.wait_ge(nmr_done, 1)
            with act.Fori(0, NT // SPAN) as a:
                for t in range(BY_VECTOR, SPAN):
                    j = SPAN * a + t
                    act.activation(dst[:, bass.ds(j, 1), :], src[:, bass.ds(j, 1), :], ACT.Identity,
                                   scale=rstd[:, bass.ds(j, 1)], bias=nmr[:, bass.ds(j, 1)])\
                       .then_inc(by_scalar, 1)

        if pooling is not None:
            mean, tokens, pooled = pooling

            @blk.tensor
            def _(pe):
                pe.wait_ge(mean_set, 2)
                for j in range(NT):
                    span, t = divmod(j, SPAN)
                    if t < BY_VECTOR:
                        pe.wait_ge(by_vector, BY_VECTOR * span + t + 1)
                    else:
                        pe.wait_ge(by_scalar, (SPAN - BY_VECTOR) * span + t - BY_VECTOR + 1)
                    b = j // TPB
                    mm = pe.matmul(tokens, mean[:, b * BATCH:(b + 1) * BATCH], dst[:, j, :],
                                   start=(j == 0), stop=(j == NT - 1))
                mm.then_inc(pooled, 1)

        @blk.gpsimd
        def _(pool):
            pool.memset(half[:, :], -0.5).then_inc(half_done, 1)
            pool.wait_ge(half_done, 1)
            pool.wait_ge(var_done, 1)
            pool.tensor_tensor(rstd[:, :], vare[:, :], half[:, :], ALU.pow).then_inc(rstd_done, 1)
            if again is not None:
                pool.wait_ge(var_done, 4)
                pool.tensor_tensor(again[:, :], vare[:, :], half[:, :], ALU.pow)


def attention(nc, name, layer, X, XN, w, consts, dram):
    L0 = layer == 0
    QD = HD if L0 else HD // 2
    SROWS = SLOTS * QD
    KROWS = SROWS + MPARTS
    ABOVE = 1 if L0 else 2
    PITCH = SROWS if L0 else P // ABOVE
    TROWS = ABOVE * PITCH
    MROW_DMAS = MPARTS * ABOVE
    UPB = CYCLE if L0 else GROUPS
    NU = BATCH * UPB
    TURNS = NU // CYCLE
    causal = not L0

    def kind(i):
        return "C" if not L0 else ("A" if i % CYCLE < GROUPS else "B")

    def live(n, k):
        return 0 <= n + k < NU

    OT_AT = {1: "B", 5: "A"} if L0 else {1: "C", 5: "C"}

    def rounds(n):
        r = []
        i = n % CYCLE
        if live(n, 6) and kind(i + 6) == "B":
            r.append((0, "weff"))
        if not L0 and live(n, 6):
            r.append((1, "proj"))
        if i in OT_AT and 0 <= n - 5 < NU:
            r.append((2, "ot"))
            if not (L0 and i == 5):
                r.append((3, "outproj"))
        if live(n, -1):
            r.append((4, "norm"))
        if L0 and live(n, 6):
            r.append((5, "proj"))
        if L0 and i == 1 and 0 <= n < NU:
            r.append((6, "weffo"))
        if i in ((1,) if L0 else (1, 5)) and live(n, 7):
            r.append((7, "xt"))
        return r

    first = -6
    last = NU + 1

    def total(f, n):
        if isinstance(n, tuple):
            turn, i = n
            per = sum(f(m) for m in range(CYCLE, 2 * CYCLE))
            return (turn - 1) * per + sum(f(m) for m in range(first, CYCLE + i))
        return sum(f(m) for m in range(first, n))

    def whole(n):
        return n if not isinstance(n, tuple) else CYCLE + n[1]

    def unit(n, k):
        return n + k if not isinstance(n, tuple) else n[0] * CYCLE + (n[1] + k)

    def wait(eng, semaphore, value):
        if isinstance(value, int) and value <= 0:
            return
        eng.wait_ge(semaphore, value)

    def ma_count(n, what):
        names = [x for _, x in rounds(whole(n))]
        return total(lambda m: len(rounds(m)), n) + names.index(what) + 1

    def xt_count(n):
        return total(lambda m: sum(x == "xt" for _, x in rounds(m)), n)

    def back(n, k):
        return n - k if not isinstance(n, tuple) else (n[0], n[1] - k)

    STACK_AT, ROWS_AT = ((0, 2, 4, 6), 5) if L0 else ((0, 2), 4)

    def mb_rounds(n):
        rounds_ = ([(p, k) for k, p in enumerate(STACK_AT)] if live(n, 3) else []) + \
                  ([(ROWS_AT, "rows")] if live(n, 1) else [])
        return [what for _, what in sorted(rounds_)]

    def mb_count(n, what=None):
        before = total(lambda m: len(mb_rounds(m)), n)
        return before if what is None else before + mb_rounds(whole(n)).index(what) + 1

    def steps(eng, step):
        for n in range(first, CYCLE):
            step(n)
        if TURNS > 2:
            with eng.Fori(1, TURNS - 1) as turn:
                for i in range(CYCLE):
                    step((turn, i))
        for n in range(NU - CYCLE, last + 1):
            step(n)

    with ExitStack() as s:
        def sb(nm, shape, dt=F32):
            return s.enter_context(nc.sbuf_tensor(name + nm, shape, dt))

        def sem(nm):
            return s.enter_context(nc.semaphore(name + nm))

        identf, identb = consts["identf"], consts["identb"]
        xs = sb("xs", [P, TPB, C])
        xT = sb("xT", [P, KT, SEQ])
        qkf = sb("qkf", [P, 2, 2, TPB * GH * HD])
        qkw = sb("qkw", [P, 2, 2, TPB * GH * QD])
        part = [sb(f"part{j}", [P, 2, TPB * GH * QD], BF16) for j in range(3)]
        rest = sb("rest", [P, 2, TPB * GH * QD])
        slots = sb("slots", [P, 2, 2, TPB * GH, PITCH], BF16)
        stack = sb("stack", [P, 4, 2, GH // ABOVE, SEQ], BF16)
        vbuf = sb("vbuf", [P, CYCLE, TPB, GH, 32])
        mx = sb("mx", [P, 2, TPB * GH])
        mres = sb("mres", [P, TPB * GH])
        minus = sb("minus", [P, TPB, GH])
        carry = sb("carry", [P, 3])
        spare = sb("spare", [P, 2])
        mparts = sb("mparts", [P, TPB, MPARTS, GH], BF16)
        mrows = sb("mrows", [MPARTS * GH, SEQ], BF16)
        prob = sb("prob", [P, 2, GH, SEQ])
        oT = sb("oT", [P, SEQ])
        rsum = sb("rsum", [P, TPB, GH])
        onA = sb("onA", [P, TPB, C])
        onB = sb("onB", [P, TPB, C])
        otA = sb("otA", [P, KT, SEQ])
        otB = sb("otB", [P, KT, SEQ]) if L0 else otA
        if L0:
            sq = sb("sq", [P, 2 * TPB * GH * HD])
            ms = sb("ms", [P, 2 * TPB * GH])
            rstd = sb("rstd", [P, 2 * TPB * GH])
            neghalf = sb("neghalf", [P, 2 * TPB * GH])
            xin = sb("xin", [P, TPB, C])
            us = sb("us", [P, 4, C])
            weff = sb("weff", [P, KT, 3 * GW])
            weffo = sb("weffo", [P, KT, C])
        else:
            rot = sb("rot", [P, 3, TPB * GH, HD // 2])
            RING = 4
            got = sb("got", [P, RING, TOPK, C])
            got_sem = [sem(f"got{i}") for i in range(RING)]
            added = sem("added")

        SC = s.enter_context(nc.psum_tensor(name + "SC", [P, 2, SEQ], F32))
        MX = s.enter_context(nc.psum_tensor(name + "MX", [P, 2, SEQ], F32))
        OV = s.enter_context(nc.psum_tensor(name + "OV", [P, SEQ], F32))
        MB = s.enter_context(nc.psum_tensor(name + "MB", [P, 8, P], BF16))
        MA = s.enter_context(nc.psum_tensor(name + "MA", [P, 1024], F32))

        ma_full = sem("ma_full")
        ma_free = sem("ma_free")
        mb_full = sem("mb_full")
        mb_free = sem("mb_free")
        score_ready = sem("score_ready")
        exp_done = sem("exp_done")
        smax_ready = sem("smax_ready")
        max_done = sem("max_done")
        pv_done = sem("pv_done")
        ov_read = sem("ov_read")
        qk_ready = sem("qk_ready")
        v_ready = sem("v_ready")
        sq_ready = sem("sq_ready")
        ss_ready = sem("ss_ready")
        ms_ready = sem("ms_ready")
        pool_norm = sem("pool_norm")
        split_done = sem("split_done")
        slots_done = sem("slots_done")
        mprep = sem("mprep")
        mrow_sent = sem("mrow_sent")
        xs_loaded = sem("xs_loaded")
        xin_loaded = sem("xin_loaded")
        xin_biased = sem("xin_biased")
        us_done = sem("us_done")
        recip_done = sem("recip_done")
        init = sem("init")
        ones_set = sem("ones_set")
        loads_in = sem("loads_in")
        pool_init = sem("pool_init")
        out_sent = sem("out_sent")

        MM_NORM = {"A": 3, "B": 1, "C": 6}

        def norm_steps(m):
            return MM_NORM[kind(m + 5)] if live(m, 5) else 0

        def a_units(k):
            return lambda m: int(live(m, k) and kind(m + k) == "A")

        def has(n, k):
            return live(whole(n), k)

        def stack_place(h):
            return (h % ABOVE) * PITCH, h // ABOVE

        def max_head(i):
            return i if L0 else i ^ 1

        def arrived(eng):
            if dram["loads"]:
                eng.wait_ge(loads_in, 16 * len(dram["loads"]))

        blk = s.enter_context(nc.Block())

        @blk.sync
        def _(sp):
            def load_xs(batch):
                sp.dma_start(xs[:, :, :], XN[:, bass.ds(batch * TPB, TPB), :]).then_inc(xs_loaded, 16)

            load_xs(0)
            for dst, src in dram["loads"]:
                sp.dma_start(dst, src).then_inc(loads_in, 16)

            def step(n):
                w_ = whole(n)
                i = w_ % CYCLE
                if i in ((0,) if L0 else (0, 4)) and (isinstance(n, tuple) or 0 < (w_ + 8) // UPB < BATCH):
                    past = back(n, 7 if L0 else 3)
                    if isinstance(past, int) and "xt" not in [x for _, x in rounds(past)]:
                        sp.wait_ge(ma_full, 1)
                    else:
                        sp.wait_ge(ma_full, ma_count(past, "xt") + 1)
                    load_xs((w_ + 8) // UPB if isinstance(n, int) else n[0] * (CYCLE // UPB) + (i + 8) // UPB)
                if has(n, 1):
                    sp.wait_ge(mb_free, mb_count(n, "rows"))
                    for j in range(MPARTS):
                        for e in range(ABOVE):
                            at = e * PITCH + SROWS + j
                            sp.dma_start(stack[at:at + 1, (w_ + 1) % 4, 0, :, :],
                                         mrows[j * GH + e * (GH // ABOVE):j * GH + (e + 1) * (GH // ABOVE), :])\
                              .then_inc(mrow_sent, 16)
                if L0 and i == 2 and 0 <= w_ < NU:
                    batch = w_ // CYCLE if isinstance(n, int) else n[0]
                    if isinstance(n, tuple) or n > CYCLE:
                        sp.wait_ge(ma_free, ma_count(back(n, 1), "outproj") + 1)
                    sp.dma_start(xin[:, :, :], dram["x"][:, bass.ds(batch * TPB, TPB), :]).then_inc(xin_loaded, 16)
                if not L0 and "outproj" in [x for _, x in rounds(w_)]:
                    batch = (w_ - 5) // UPB if isinstance(n, int) else 2 * n[0] + (n[1] - 5) // UPB
                    sp.wait_ge(ma_free, ma_count(n, "outproj") + 1)
                    sp.dma_start(dram["out"][:, bass.ds(batch * TPB, TPB), :],
                                 X[:, bass.ds(batch * TPB, TPB), :]).then_inc(out_sent, 16)

            steps(sp, step)
            if not L0:
                sp.wait_ge(out_sent, 16 * BATCH)

        @blk.tensor
        def _(pe):
            def xt_round(n):
                wait(pe, xs_loaded, 16 if n is None else 16 * (xt_count(n) + 2))
                for t in range(TPB):
                    for kt in range(KT):
                        mm = pe.transpose(MA[:, kt * SEQ + t * P:kt * SEQ + (t + 1) * P],
                                          xs[:, t, kt * P:(kt + 1) * P], identf[:, :])
                mm.then_inc(ma_full, 1)

            def ma_round(n, what):
                w_ = whole(n)
                i = w_ % CYCLE
                wait(pe, ma_free, ma_count(n, what))
                if what == "weff":
                    g = (i + 6) % GROUPS
                    nb = (w_ + 6) // CYCLE if isinstance(n, int) else n[0] + (n[1] + 6) // CYCLE
                    wait(pe, us_done, 4 * (nb + 1))
                    for kt in range(KT):
                        for j in range(3):
                            mm = pe.matmul(MA[:, kt * 3 * GW + j * GW:kt * 3 * GW + (j + 1) * GW],
                                           w["V"][:, j, kt * P:(kt + 1) * P], us[:, j, g * GW:(g + 1) * GW],
                                           start=True, stop=True)
                elif what == "weffo":
                    for kt in range(KT):
                        mm = pe.matmul(MA[:, kt * SEQ:kt * SEQ + C], w["V"][:, 3, kt * P:(kt + 1) * P],
                                       us[:, 3, :], start=True, stop=True)
                elif what == "proj":
                    kd = kind(i + 6)
                    g = (i + 6) % GROUPS
                    for t in range(TPB):
                        for kt in range(KT):
                            rhs = weff[:, kt, :] if kd == "B" else w["W" + kd][:, kt, g, :]
                            mm = pe.matmul(MA[:, t * C:t * C + 3 * GW], xT[:, kt, t * P:(t + 1) * P], rhs,
                                           start=(kt == 0), stop=(kt == KT - 1))
                elif what == "ot":
                    src = onB if i == 1 else onA
                    for t in range(TPB):
                        for kt in range(KT):
                            mm = pe.transpose(MA[:, kt * SEQ + t * P:kt * SEQ + (t + 1) * P],
                                              src[:, t, kt * P:(kt + 1) * P], identf[:, :])
                elif what == "outproj":
                    pairs = [(otA, w["WoA"]), (otB, weffo)] if L0 else [(otA, w["WoC"])]
                    for t in range(TPB):
                        for q, (ot, wo) in enumerate(pairs):
                            for kt in range(KT):
                                mm = pe.matmul(MA[:, t * C:(t + 1) * C], ot[:, kt, t * P:(t + 1) * P],
                                               wo[:, kt, :], start=(q == 0 and kt == 0),
                                               stop=(q == len(pairs) - 1 and kt == KT - 1))
                elif what == "norm":
                    wait(pe, ov_read, unit(n, 0))
                    for t in range(TPB):
                        mm = pe.transpose(MA[:, t * P:(t + 1) * P], oT[:, t * P:(t + 1) * P], identf[:, :])
                mm.then_inc(ma_full, 1)

            def stack_round(n, r):
                wait(pe, slots_done, 6 * (unit(n, 3) + 1))
                wait(pe, mb_free, mb_count(n, r) - 1)
                for j in range(8):
                    if L0:
                        qk, t, h, block = r // 2, 2 * (r % 2) + j // GH, j % GH, (j % GH) * 2 + j // GH
                    else:
                        qk, t, h, block = r, j % TPB, 2 * (j // TPB), j
                    mm = pe.transpose(MB[0:TROWS, block, :],
                                      slots[:, (whole(n) + 3) % 2, qk, t * GH + h:t * GH + h + ABOVE, :]
                                      .rearrange("p a s -> p (a s)"), identb[:, :])
                mm.then_inc(mb_full, 1)

            def mrow_round(n):
                wait(pe, mprep, 5 * (unit(n, 1) + 1))
                wait(pe, mb_free, mb_count(n, "rows") - 1)
                for t in range(TPB):
                    mm = pe.transpose(MB[0:MPARTS * GH, t, :], mparts[:, t, :, :], identb[:, :])
                mm.then_inc(mb_full, 1)

            def score(n, sl, h):
                u4 = whole(n) % 4
                if sl == 0 and h == 0:
                    wait(pe, mrow_sent, 16 * MROW_DMAS * (unit(n, 0) + 1))
                wait(pe, exp_done, 16 * unit(n, 0) + 4 * sl + h - 1)
                lo = sl * P if causal else 0
                at, hs = stack_place(h)
                mm = pe.matmul(SC[:, h % 2, lo:SEQ], stack[at:at + KROWS, u4, 1, hs, sl * P:(sl + 1) * P],
                               stack[at:at + KROWS, u4, 0, hs, lo:SEQ], start=True, stop=not causal)
                if causal:
                    mm = pe.matmul(SC[:, h % 2, lo:lo + P], identb[:, :], consts["mask_kq"][:, :],
                                   start=False, stop=True)
                mm.then_inc(score_ready, 1)

            def maxmm(n, sl, i):
                u4 = (whole(n) + 2) % 4
                if sl == 0 and i == 0:
                    wait(pe, mb_free, mb_count(n))
                wait(pe, max_done, 16 * unit(n, 2) + 4 * sl + i - 1)
                hi = (sl + 1) * P if causal else SEQ
                at, hs = stack_place(max_head(i))
                mm = pe.matmul(MX[:, i % 2, 0:hi], stack[at:at + SROWS, u4, 0, hs, sl * P:(sl + 1) * P],
                               stack[at:at + SROWS, u4, 1, hs, 0:hi], start=True, stop=not causal)
                if causal:
                    mm = pe.matmul(MX[:, i % 2, hi - P:hi], identb[:, :], consts["mask_qk"][:, :],
                                   start=False, stop=True)
                mm.then_inc(smax_ready, 1)

            def pv(n, k, sl, h):
                v8 = (whole(n) + k) % CYCLE
                u = unit(n, k)
                wait(pe, exp_done, 16 * u + 4 * sl + h + 1)
                if sl == 0 and h == 0:
                    wait(pe, ov_read, u)
                    wait(pe, v_ready, u + 1)
                lo = sl * P if causal else 0
                mm = pe.matmul(OV[32 * h:32 * h + 32, lo:SEQ], vbuf[:, v8, sl, h, :],
                               prob[:, sl % 2, h, lo:SEQ], start=(sl == 0), stop=(sl == TPB - 1),
                               skip_group_check=True)
                if h == GH - 1:
                    mm.then_inc(pv_done, 1)

            xt_round(None)
            pe.wait_ge(init, 2)
            arrived(pe)

            PV_HEADS = ((0,), (1,), (2,), (3,))
            PV_LATE = ((), (0,), (1, 2), (3,))

            def step(n):
                r = dict(rounds(whole(n)))
                for p in range(8):
                    sl, hp = p // 2, p % 2
                    if p in r:
                        if r[p] == "xt":
                            wait(pe, ma_free, ma_count(n, "xt"))
                            xt_round(n)
                        else:
                            ma_round(n, r[p])
                    if has(n, 3) and p in STACK_AT:
                        stack_round(n, STACK_AT.index(p))
                    if has(n, 1) and p == ROWS_AT:
                        mrow_round(n)
                    for h in (2 * hp, 2 * hp + 1):
                        if has(n, 0):
                            score(n, sl, h)
                        if has(n, 2):
                            maxmm(n, sl, h)
                        for hv in (PV_LATE if sl == 1 else PV_HEADS)[h]:
                            if sl == 0:
                                if has(n, -1):
                                    pv(n, -1, TPB - 1, hv)
                            elif has(n, 0):
                                pv(n, 0, sl - 1, hv)

            steps(pe, step)

        @blk.scalar
        def _(act):
            STACK_COPIES = [(p, half) for p in STACK_AT for half in range(2)]
            act.wait_ge(ma_full, 1)
            act.copy(xT[:, :, :], MA[:, :].rearrange("p (k n) -> p k n", k=KT)).then_inc(ma_free, 1)
            for dst, src in dram["aside"]:
                act.dma_start(dst, src).then_inc(dram["aside_done"], 16)
            for u in range(4 if L0 else 0):
                act.copy(stack[96:P, u, 1, :, :].rearrange("p h n -> p (h n)"),
                         consts["ones"][96:P, 0:1].to_broadcast([P - 96, GH * SEQ])).then_inc(ones_set, 1)
            if L0:
                act.wait_ge(ones_set, 4)

            def step(n):
                w_ = whole(n)
                r = dict(rounds(w_))
                for p in range(8):
                    sl, hp = p // 2, p % 2
                    if r.get(p) in ("xt", "ot"):
                        wait(act, ma_full, ma_count(n, r[p]) + 1)
                        if r[p] == "xt":
                            dst = xT
                        else:
                            dst = otB if L0 and w_ % CYCLE == 1 else otA
                        act.copy(dst[:, :, :], MA[:, :].rearrange("p (k n) -> p k n", k=KT)).then_inc(ma_free, 1)
                    if has(n, 1) and p == ROWS_AT:
                        wait(act, mb_full, mb_count(n, "rows"))
                        wait(act, mrow_sent, 16 * MROW_DMAS * unit(n, 1))
                        act.copy(mrows[:, :].rearrange("p (t n) -> p t n", t=TPB),
                                 MB[0:MPARTS * GH, 0:TPB, :]).then_inc(mb_free, 1)
                    if p == 2 and has(n, -1):
                        wait(act, pv_done, 4 * unit(n, 0))
                        if has(n, -2):
                            wait(act, ma_full, ma_count(back(n, 1), "norm") + 1)
                        act.copy(oT[:, :], OV[:, :]).then_inc(ov_read, 1)
                    for h in (2 * hp, 2 * hp + 1):
                        if has(n, 0):
                            wait(act, score_ready, 16 * unit(n, 0) + 4 * sl + h + 1)
                            wait(act, pv_done, 4 * unit(n, 0) + sl - 1)
                            lo = sl * P if causal else 0
                            act.activation(prob[:, sl % 2, h, lo:SEQ], SC[:, h % 2, lo:SEQ], ACT.Exp,
                                           scale=float(HD) ** -0.5).then_inc(exp_done, 1)
                        if has(n, 3) and (p, h % 2) in STACK_COPIES:
                            rr, pair = divmod(STACK_COPIES.index((p, h % 2)), 2)
                            wait(act, mb_full, mb_count(n, rr))
                            if L0:
                                dst = stack[0:TROWS, (w_ + 3) % 4, rr // 2, 2 * pair:2 * pair + 2,
                                            (rr % 2) * 2 * P:(rr % 2 + 1) * 2 * P]
                                src = MB[0:TROWS, 4 * pair:4 * pair + 4, :].rearrange("p (h t) n -> p h (t n)", h=2)
                            else:
                                dst = stack[:, (w_ + 3) % 4, rr, pair, :]
                                src = MB[:, 4 * pair:4 * pair + 4, :].rearrange("p t n -> p (t n)")
                            copied = act.copy(dst, src)
                            if pair:
                                copied.then_inc(mb_free, 1)

            steps(act, step)
            if dram["aside"]:
                act.wait_ge(dram["aside_done"], 16 * len(dram["aside"]))

        @blk.vector
        def _(dve):
            dve.memset(vbuf[:, :, :, :, :].rearrange("p a t h d -> p (a t h d)"), 1.0).then_inc(init, 1)
            if L0:
                dve.memset(neghalf[:, :], -0.5).then_inc(init, 1)
            else:
                dve.memset(slots[:, :, :, :, SROWS:PITCH].rearrange("p u q a s -> p (u q a) s"), 1.0)\
                   .then_inc(init, 1)
            dve.memset(spare[:, :], 0.0).then_inc(init, 1)
            dve.wait_ge(init, 3)
            arrived(dve)

            def gate_factors(batch):
                for j in range(4):
                    dve.tensor_scalar(us[:, j, :], w["UT"][:, j, :], w["gS"][:, j, bass.ds(batch, 1)], None,
                                      ALU.mult).then_inc(us_done, 1)

            def ma_round(n, what):
                w_ = whole(n)
                i = w_ % CYCLE
                wait(dve, ma_full, ma_count(n, what) + 1)
                if what == "weff":
                    g = (i + 6) % GROUPS
                    dve.tensor_tensor(weff[:, :, :], MA[:, 0:KT * 3 * GW].rearrange("p (k n) -> p k n", k=KT),
                                      w["WB"][:, :, g, :], ALU.add).then_inc(ma_free, 1)
                elif what == "weffo":
                    dve.tensor_tensor(weffo[:, :, :], MA[:, :].rearrange("p (k n) -> p k n", k=KT)[:, :, 0:C],
                                      w["WoB"][:, :, :], ALU.add).then_inc(ma_free, 1)
                elif what == "proj":
                    kd = kind(i + 6)
                    g = (i + 6) % GROUPS
                    u = unit(n, 6)
                    ps = MA[:, :].rearrange("p (t n) -> p t n", t=TPB)
                    bias = w["b" + kd]
                    wait(dve, pool_norm, total(norm_steps, n))
                    if has(n, -1):
                        wait(dve, pv_done, 4 * unit(n, -1))
                    dve.tensor_tensor(
                        vbuf[:, (w_ + 6) % CYCLE, :, :, 0:HD],
                        ps[:, :, 2 * GW:3 * GW].rearrange("p t (h d) -> p t h d", h=GH),
                        bias[:, g, 2 * GW:3 * GW].rearrange("p (h d) -> p h d", h=GH).unsqueeze(1)
                        .to_broadcast([P, TPB, GH, HD]), ALU.add).then_inc(v_ready, 1)
                    for qk in range(2):
                        dve.tensor_tensor(
                            qkf[:, (w_ + 6) % 2, qk, :].rearrange("p (t n) -> p t n", t=TPB),
                            ps[:, :, qk * GW:(qk + 1) * GW],
                            bias[:, g, qk * GW:(qk + 1) * GW].unsqueeze(1).to_broadcast([P, TPB, GW]),
                            ALU.add).then_inc((qk_ready, ma_free)[qk], 1)
                elif what == "outproj":
                    res = MA[:, :].rearrange("p (t n) -> p t n", t=TPB)
                    if L0:
                        batch = (w_ - 9) // CYCLE if isinstance(n, int) else n[0] - 1
                        wait(dve, xin_biased, batch + 1)
                        dve.tensor_tensor(X[:, bass.ds(batch * TPB, TPB), :], res, xin[:, :, :],
                                          ALU.add).then_inc(ma_free, 1)
                    else:
                        batch = (w_ - 5) // UPB if isinstance(n, int) else 2 * n[0] + (n[1] - 5) // UPB
                        rows = X[:, bass.ds(batch * TPB, TPB), :]
                        wait(dve, added, TOPK * TPB * (batch + 1))
                        dve.tensor_tensor(rows, res, rows, ALU.add).then_inc(ma_free, 1)
                elif what == "norm":
                    u = unit(n, -1)
                    g = (w_ - 1) % GROUPS
                    dst = onA if (w_ - 1) % CYCLE < GROUPS else onB
                    o = MA[:, 0:SEQ].rearrange("p (t h d) -> p t h d", t=TPB, h=GH)
                    dve.reciprocal(rsum[:, :, :], o[:, :, :, HD]).then_inc(recip_done, 1)
                    wait(dve, recip_done, u + 1)
                    dve.tensor_tensor(dst[:, :, g * GW:(g + 1) * GW].rearrange("p t (h d) -> p t h d", h=GH),
                                      o[:, :, :, 0:HD],
                                      rsum[:, :, :].unsqueeze(3).to_broadcast([P, TPB, GH, HD]),
                                      ALU.mult).then_inc(ma_free, 1)

            def squares_sum(n, j):
                k = total(a_units(5), n)
                if j == 1:
                    wait(dve, ss_ready, k + 1)
                    dve.tensor_scalar(ms[:, :], ms[:, :], 1.0 / HD, 1e-6, ALU.mult, ALU.add).then_inc(ms_ready, 1)
                    return
                wait(dve, sq_ready, k + 1)
                wait(dve, pool_norm, total(norm_steps, n))
                dve.tensor_reduce(ms[:, :], sq[:, :].rearrange("p (a d) -> p a d", d=HD), AX.X,
                                  ALU.add).then_inc(ss_ready, 1)

            def split(n, j):
                u = unit(n, 4)
                src = qkw[:, (whole(n) + 4) % 2, :, :]
                if j == 0:
                    wait(dve, pool_norm, total(norm_steps, n))
                    wait(dve, slots_done, 6 * u)
                    dve.tensor_copy(part[0][:, :, :], src).then_inc(split_done, 1)
                    return
                wait(dve, split_done, 4 * u + j)
                if j == 1:
                    ins = dve.tensor_tensor(rest[:, :, :], src, part[0][:, :, :], ALU.subtract)
                elif j == 2:
                    ins = dve.tensor_copy(part[1][:, :, :], rest[:, :, :])
                else:
                    ins = dve.tensor_tensor(part[2][:, :, :], rest[:, :, :], part[1][:, :, :], ALU.subtract)
                ins.then_inc(split_done, 1)

            def lay_slots(n, j):
                u = unit(n, 4)
                qk = j // 3
                src = [part[k][:, qk, :].rearrange("p (a d) -> p a d", d=QD) for k in range(3)]
                dst = slots[:, (whole(n) + 4) % 2, qk, :, 0:SROWS].rearrange("p a (s d) -> p a s d", d=QD)
                if j == 0:
                    wait(dve, split_done, 4 * (u + 1))
                    wait(dve, mb_full, mb_count(n))
                k = j % 3
                wide, at = ((3, slice(0, 3)), (3, slice(3, 6)), (1, slice(6, 7)),
                            (3, slice(0, 7, 3)), (2, slice(1, 5, 3)), (2, slice(2, 6, 3)))[j]
                dve.tensor_copy(dst[:, :, at, :], src[k].unsqueeze(2).to_broadcast([P, TPB * GH, wide, QD]))\
                   .then_inc(slots_done, 1)

            def statistics(n):
                batch = (whole(n) - 9) // CYCLE if isinstance(n, int) else n[0] - 1
                wait(dve, ma_free, ma_count(n, "outproj") + 1)
                dve.tensor_copy(spare[:, 1:2], spare[:, 0:1])
                for t in range(TPB):
                    j = batch * TPB + t
                    dve.bn_stats(dram["stats"][:, bass.ds(j, 1), :], X[:, bass.ds(j, 1), :])

            def add_experts(n):
                j = unit(n, 0)
                ring = whole(n) % RING
                turn_ = j // RING if isinstance(j, int) else n[0] * (CYCLE // RING) + n[1] // RING
                wait(dve, got_sem[ring], 16 * TOPK * (turn_ + 1))
                row = X[:, bass.ds(j, 1), :]
                for k in range(TOPK):
                    if k:
                        wait(dve, added, TOPK * j + k)
                    dve.scalar_tensor_tensor(out=row, in0=got[:, ring:ring + 1, k, :],
                                             scalar=w["gate"][:, bass.ds(j, 1), k], in1=row,
                                             op0=ALU.mult, op1=ALU.add).then_inc(added, 1)

            if L0:
                gate_factors(0)

            SPLIT_AT = (1, 3, 5, 7) if L0 else (0, 1, 2, 3)
            SLOTS_AT = (8, 9, 11, 12, 13, 14) if L0 else (4, 5, 6, 8, 9, 10)

            def step(n):
                w_ = whole(n)
                r = dict(rounds(w_))
                for p in range(8):
                    sl, hp = p // 2, p % 2
                    if p in r and r[p] not in ("xt", "ot"):
                        ma_round(n, r[p])
                    if L0 and p == 4 and w_ % CYCLE == 3 and 0 <= w_ < NU - CYCLE:
                        batch = w_ // CYCLE + 1 if isinstance(n, int) else n[0] + 1
                        wait(dve, ma_full, ma_count(back(n, 2), "weffo") + 1)
                        gate_factors(batch)
                    for h in (2 * hp, 2 * hp + 1):
                        m = 2 * p + h % 2
                        if has(n, 2):
                            u = unit(n, 2)
                            wait(dve, smax_ready, 16 * u + 4 * sl + h + 1)
                            if sl == 0 and h == 0:
                                wait(dve, mprep, 5 * unit(n, 1))
                            hi = (sl + 1) * P if causal else SEQ
                            at, hs = stack_place(max_head(h))
                            place = sl * GH + at // PITCH * (GH // ABOVE) + hs
                            dve.tensor_reduce(mx[:, (w_ + 2) % 2, place:place + 1],
                                              MX[:, h % 2, 0:hi], AX.X, ALU.max).then_inc(max_done, 1)
                        if m in (0, 2) and has(n, 5) and kind(w_ + 5) == "A":
                            squares_sum(n, m // 2)
                        if L0 and m == 15 and "outproj" in r.values():
                            statistics(n)
                        if m in SPLIT_AT and has(n, 4):
                            split(n, SPLIT_AT.index(m))
                        if not L0 and m == 15 and has(n, 0):
                            add_experts(n)
                        if m in SLOTS_AT and has(n, 4):
                            lay_slots(n, SLOTS_AT.index(m))

            steps(dve, step)

        @blk.gpsimd
        def _(pool):
            pool.memset(minus[:, :, :], -1.0).then_inc(pool_init, 1)
            pool.memset(carry[:, :], 0.0).then_inc(pool_init, 1)
            pool.wait_ge(pool_init, 2)
            pool.wait_ge(init, 2)
            arrived(pool)

            def maxima(n):
                u = unit(n, 1)
                m = mx[:, (whole(n) + 1) % 2, :]
                wait(pool, max_done, 16 * (u + 1))
                if has(n, 0):
                    wait(pool, mb_full, mb_count(back(n, 1), "rows"))
                mv = m.rearrange("p (t h) -> p t h", t=TPB)
                rv = mres[:, :].rearrange("p (t h) -> p t h", t=TPB)
                pool.tensor_tensor(mparts[:, :, 0, :], mv, minus[:, :, :], ALU.mult).then_inc(mprep, 1)
                wait(pool, mprep, 5 * u + 1)
                pool.tensor_tensor(rv, mv, mparts[:, :, 0, :], ALU.add).then_inc(mprep, 1)
                wait(pool, mprep, 5 * u + 2)
                pool.tensor_tensor(mparts[:, :, 1, :], rv, minus[:, :, :], ALU.mult).then_inc(mprep, 1)
                wait(pool, mprep, 5 * u + 3)
                pool.tensor_tensor(rv, rv, mparts[:, :, 1, :], ALU.add).then_inc(mprep, 1)
                wait(pool, mprep, 5 * u + 4)
                pool.tensor_tensor(mparts[:, :, 2, :], rv, minus[:, :, :], ALU.mult).then_inc(mprep, 1)

            def norm_qk(n):
                w_ = whole(n)
                kd = kind(w_ + 5)
                u = unit(n, 5)
                src, dst = qkf[:, (w_ + 5) % 2, :, :], qkw[:, (w_ + 5) % 2, :, :]
                done = total(norm_steps, n)
                wait(pool, ma_free, ma_count(back(n, 1), "proj") + 1)
                wait(pool, pool_norm, done)
                wait(pool, split_done, 4 * unit(n, 4))
                if kd == "B":
                    pool.tensor_tensor(carry[:, 2:3], carry[:, 0:1], carry[:, 0:1], ALU.add)
                    pool.tensor_copy(dst, src).then_inc(pool_norm, 1)
                elif kd == "A":
                    wait(pool, ms_ready, total(a_units(5), n) + 1)
                    pool.tensor_tensor(rstd[:, :], ms[:, :], neghalf[:, :], ALU.pow).then_inc(pool_norm, 1)
                    wait(pool, pool_norm, done + 1)
                    d3 = dst.rearrange("p q (a d) -> p (q a) d", d=HD)
                    pool.tensor_tensor(d3, src.rearrange("p q (a d) -> p (q a) d", d=HD),
                                       rstd[:, :].unsqueeze(2).to_broadcast([P, 2 * TPB * GH, HD]),
                                       ALU.mult).then_inc(pool_norm, 1)
                    wait(pool, pool_norm, done + 2)
                    d4 = dst.rearrange("p q (a d) -> p q a d", d=HD)
                    pool.tensor_tensor(d4, d4, w["qkn"][:, :, :].unsqueeze(2)
                                       .to_broadcast([P, 2, TPB * GH, HD]), ALU.mult).then_inc(pool_norm, 1)
                else:
                    for qk in range(2):
                        ue = src[:, qk, :].rearrange("p (t h d e) -> p t h d e", t=TPB, h=GH, e=2)[:, :, :, :, 0]
                        uo = src[:, qk, :].rearrange("p (t h d e) -> p t h d e", t=TPB, h=GH, e=2)[:, :, :, :, 1]
                        r0 = rot[:, 0, :, :].rearrange("p (t h) d -> p t h d", t=TPB)
                        r1 = rot[:, 1, :, :].rearrange("p (t h) d -> p t h d", t=TPB)
                        cb = w["cos"][:, :, :].unsqueeze(2).to_broadcast([P, TPB, GH, HD // 2])
                        sb_ = w["sin"][:, :, :].unsqueeze(2).to_broadcast([P, TPB, GH, HD // 2])
                        pool.tensor_tensor(r0, ue, cb, ALU.mult).then_inc(pool_norm, 1)
                        pool.tensor_tensor(r1, uo, sb_, ALU.mult).then_inc(pool_norm, 1)
                        wait(pool, pool_norm, done + 3 * qk + 2)
                        out = dst[:, qk, :].rearrange("p (a d) -> p a d", d=QD)
                        pool.tensor_tensor(out, rot[:, 0, :, :], rot[:, 1, :, :],
                                           ALU.subtract).then_inc(pool_norm, 1)
                        wait(pool, pool_norm, done + 3 * qk + 3)

            def squares(n):
                u = unit(n, 6)
                wait(pool, ma_free, ma_count(n, "proj") + 1)
                wait(pool, ss_ready, total(a_units(6), n))
                src = qkf[:, (whole(n) + 6) % 2, :, :].rearrange("p q n -> p (q n)")
                pool.tensor_tensor(sq[:, :], src, src, ALU.mult).then_inc(sq_ready, 1)

            def fetch(j):
                if j >= RING:
                    wait(pool, added, TOPK * (j - RING + 1))
                for k in range(TOPK):
                    pool.indirect_dma_start(got[:, j % RING, k, :], None, dram["outs"],
                                            bass.IndirectOffsetOnAxis(ap=w["gather_id"][:, j, k:k + 1], axis=0),
                                            bounds_check=SLOTROWS - 1, oob_is_err=False)\
                        .then_inc(got_sem[j % RING], 16)

            def step(n):
                w_ = whole(n)
                if has(n, 1):
                    maxima(n)
                if has(n, 5):
                    norm_qk(n)
                if L0 and w_ % CYCLE == 3 and 0 <= w_ < NU:
                    batch = w_ // CYCLE if isinstance(n, int) else n[0]
                    wait(pool, xin_loaded, 16 * (batch + 1))
                    pool.tensor_tensor(xin[:, :, :], xin[:, :, :],
                                       w["bout"][:, :].unsqueeze(1).to_broadcast([P, TPB, C]),
                                       ALU.add).then_inc(xin_biased, 1)
                if has(n, 6) and kind(w_ + 6) == "A":
                    squares(n)
                if not L0 and 0 <= n + 2 < NT:
                    fetch(n + 2)

            if L0:
                steps(pool, step)
            else:
                for n in range(first, last + 1):
                    step(n)


def top_two(dve, link, vals, desc, eq, top, best, hot, rest):
    p_, g_, e_ = vals.shape
    cur = vals
    for k in range(2):
        link(dve.tensor_reduce(top[k], cur, AX.X, ALU.max))
        link(dve.tensor_tensor(eq, cur, top[k].unsqueeze(2).to_broadcast([p_, g_, e_]), ALU.is_equal))
        link(dve.tensor_tensor(eq, eq, desc, ALU.mult))
        link(dve.tensor_reduce(best, eq, AX.X, ALU.max))
        link(dve.tensor_tensor(hot[k], eq, best.unsqueeze(2).to_broadcast([p_, g_, e_]), ALU.is_equal))
        if k == 0:
            link(dve.tensor_scalar(eq, hot[0], NEG, None, ALU.mult))
            link(dve.tensor_tensor(rest, vals, eq, ALU.add))
            cur = rest


def gates(nc, XN, gate_w, gS, consts, S4, begin):
    E, GHID = 8, 64
    with ExitStack() as s:
        def sb(nm, shape, dt=F32):
            return s.enter_context(nc.sbuf_tensor("gate_" + nm, shape, dt))

        pooled = sb("pooled", [P, KT, BATCH])
        rowsum = sb("rowsum", [BATCH, C])
        hid = sb("hid", [GHID, BATCH])
        logit = sb("logit", [BATCH, 1, E])
        eq = sb("eq", [BATCH, 1, E])
        rest = sb("rest", [BATCH, 1, E])
        hot = [sb(f"hot{k}", [BATCH, 1, E]) for k in range(2)]
        top = [sb(f"top{k}", [BATCH, 1]) for k in range(2)]
        best = sb("best", [BATCH, 1])
        gap, e2, den, g1, g2 = (sb(nm, [BATCH, 1]) for nm in ("gap", "e2", "den", "g1", "g2"))
        gate = sb("gate", [BATCH, E])
        gateT = sb("gateT", [E, BATCH])
        ps = s.enter_context(nc.psum_tensor("gate_ps", [P, 5, 512], F32))
        chain = s.enter_context(nc.semaphore("gate_chain"))
        mm_done = s.enter_context(nc.semaphore("gate_mm"))
        rows_ready = s.enter_context(nc.semaphore("gate_rows_ready"))
        for_pe = s.enter_context(nc.semaphore("gate_for_pe"))
        exp_in = s.enter_context(nc.semaphore("gate_exp_in"))
        exp_out = s.enter_context(nc.semaphore("gate_exp_out"))
        blk = s.enter_context(nc.Block())

        @blk.tensor
        def _(pe):
            pe.wait_ge(begin["w_in"], 16 * GATES_LOADS)
            pe.wait_ge(rows_ready, 1)
            for kt in range(KT):
                mm = pe.transpose(ps[:, 1, kt * BATCH:(kt + 1) * BATCH], rowsum[:, kt * P:(kt + 1) * P],
                                  consts["identf"][0:BATCH, 0:BATCH])
            mm.then_inc(mm_done, 1)
            pe.wait_ge(for_pe, 1)
            for kt in range(KT):
                mm = pe.matmul(ps[0:GHID, 0, 0:BATCH], gate_w["gw1"][:, kt, :], pooled[:, kt, :],
                               start=(kt == 0), stop=(kt == KT - 1))
            mm.then_inc(mm_done, 1)
            pe.wait_ge(for_pe, 2)
            pe.matmul(ps[0:BATCH, 2, 0:E], hid[:, :], gate_w["gw2"][:, :], start=True, stop=True).then_inc(mm_done, 1)
            pe.wait_ge(for_pe, 3)
            pe.transpose(ps[0:E, 3, 0:BATCH], gate[:, :], consts["identf"][0:BATCH, 0:BATCH]).then_inc(mm_done, 1)
            pe.wait_ge(for_pe, 4)
            pe.matmul(ps[:, 4, 0:BATCH], gate_w["rep"][:, :], gateT[:, :], start=True, stop=True).then_inc(mm_done, 1)

        @blk.scalar
        def _(act):
            act.wait_ge(exp_in, 1)
            act.activation(e2[:, :], gap[:, :], ACT.Exp).then_inc(exp_out, 1)

        @blk.vector
        def _(dve):
            steps = [0]

            def link(ins):
                steps[0] += 1
                ins.then_inc(chain, 1)
                dve.wait_ge(chain, steps[0])

            dve.wait_ge(begin["pooled"], 1)
            dve.tensor_copy(rowsum[:, :], begin["tokens"]).then_inc(rows_ready, 1)
            dve.memset(begin["zeros"][:, :], 0.0)
            dve.memset(consts["ones"][:, :], 1.0)
            dve.wait_ge(begin["w_in"], 16 * GATES_LOADS)
            for i, nm in enumerate(("identb", "mask_kq", "mask_qk", "before")):
                dve.tensor_copy(consts[nm][:, :], begin["stage"][:, i, :])
            dve.tensor_tensor(begin["bout"][:, :], begin["bout"][:, :], begin["b2"][:, :], ALU.add)
            dve.wait_ge(mm_done, 1)
            dve.tensor_copy(pooled[:, :, :], ps[:, 1, 0:KT * BATCH].rearrange("p (k b) -> p k b", k=KT)).then_inc(for_pe, 1)
            dve.wait_ge(mm_done, 2)
            dve.tensor_scalar(hid[:, :], ps[0:GHID, 0, 0:BATCH], gate_w["gb1"][:, 0:1], 0.0, ALU.add,
                              ALU.max).then_inc(for_pe, 1)
            dve.wait_ge(mm_done, 3)
            link(dve.tensor_tensor(logit[:, 0, :], ps[0:BATCH, 2, 0:E], gate_w["gb2"][:, :], ALU.add))
            top_two(dve, link, logit[:, :, :], gate_w["desc8"][:, :].unsqueeze(1), eq[:, :, :],
                    [t[:, :] for t in top], best[:, :], [h[:, :, :] for h in hot], rest[:, :, :])
            dve.tensor_tensor(gap[:, :], top[1][:, :], top[0][:, :], ALU.subtract).then_inc(exp_in, 1)
            dve.wait_ge(exp_out, 1)
            link(dve.tensor_scalar(den[:, :], e2[:, :], 1.0, None, ALU.add))
            link(dve.reciprocal(g1[:, :], den[:, :]))
            link(dve.tensor_tensor(g2[:, :], g1[:, :], e2[:, :], ALU.mult))
            link(dve.tensor_scalar(gate[:, :], hot[0][:, 0, :], g1[:, 0:1], None, ALU.mult))
            dve.scalar_tensor_tensor(out=gate[:, :], in0=hot[1][:, 0, :], scalar=g2[:, 0:1], in1=gate[:, :],
                                     op0=ALU.mult, op1=ALU.add).then_inc(for_pe, 1)
            dve.wait_ge(mm_done, 4)
            dve.tensor_copy(gateT[:, :], ps[0:E, 3, 0:BATCH]).then_inc(for_pe, 1)
            dve.wait_ge(mm_done, 5)
            for j in range(4):
                dve.tensor_scalar(gS[:, j, :], ps[:, 4, 0:BATCH], S4[:, j:j + 1], None, ALU.mult)


def block_d(nc, X, XN, Z, again, logits, w, consts):
    S = BATCH
    KVH = 4
    REP = HEADS // KVH
    KV = KVH * HD
    QKV = C + 2 * KV
    Xv = X[:, :, :].rearrange("p (s t) c -> p s t c", t=TPB)
    XNv = XN[:, :, :].rearrange("p (s t) c -> p s t c", t=TPB)
    Zv = Z[:, :, :].rearrange("p (s t) c -> p s t c", t=TPB)
    Lv = logits[:, :, :].rearrange("p (s t) e -> p s t e", t=TPB)
    with ExitStack() as s_:
        def sb(nm, shape, dt=F32):
            return s_.enter_context(nc.sbuf_tensor("d_" + nm, shape, dt))

        def sem(nm):
            return s_.enter_context(nc.semaphore("d_" + nm))

        z = sb("z", [P, S, C])
        zT = sb("zT", [P, KT, S * P])
        q = sb("q", [P, 2, S, C])
        kv = sb("kv", [P, 2, S, 2, KV])
        prod = sb("prod", [P, S, C])
        prod2 = sb("prod2", [P, 2, S, C])
        sc = sb("sc", [P, S, S, HEADS])
        top = sb("top", [P, S, HEADS])
        sums = sb("sums", [P, S, HEADS])
        den = sb("den", [P, S, HEADS])
        o = sb("o", [P, S, C])
        h = sb("h", [P, S, C])
        stats = sb("stats", [P, S, 6])
        mv = sb("mv", [P, S, 2])
        vare = sb("vare", [P, S])
        nmu = sb("nmu", [P, S])
        rstd = sb("rstd", [P, S])
        nmr = sb("nmr", [P, S])
        half = sb("half", [P, S])
        carry = sb("carry", [P, 2])
        T = s_.enter_context(nc.psum_tensor("d_T", [P, 2, 4, P], F32))
        Y = s_.enter_context(nc.psum_tensor("d_Y", [P, 2, 512], F32))
        H = s_.enter_context(nc.psum_tensor("d_H", [P, S, C], F32))

        t_full, t_free = sem("t_full"), sem("t_free")
        y_full, y_free = sem("y_full"), sem("y_free")
        h_full = sem("h_full")
        chain = sem("chain")
        scaled = sem("scaled")
        zw = sem("zw")
        x_biased = sem("x_biased")
        sc_ready, ex_ready = sem("sc_ready"), sem("ex_ready")
        pp_ready, pp_read = sem("pp_ready"), sem("pp_read")
        o_ready, var_ready = sem("o_ready"), sem("var_ready")
        rstd_ready, normed = sem("rstd_ready"), sem("normed")
        ln_ready = sem("ln_ready")
        half_done = sem("half_done")

        jobs = [("front", 0)]
        for b in range(TPB + 1):
            jobs += ([("oproj", b - 1)] if b else []) + ([("front", b + 1)] if b + 1 < TPB else []) + \
                    ([("router", b - 1)] if b else [])
        TR = 2 * KT

        def t_before(job):
            return TR * jobs.index(job)

        def y_before(job):
            return S * sum(what != "oproj" for what, _ in jobs[:jobs.index(job)])

        PP = 1 + S

        def wait(eng, semaphore, value):
            if value > 0:
                eng.wait_ge(semaphore, value)

        def ln1(eng, b):
            wait(eng, scaled, b + 1)
            eng.tensor_tensor(z[:, :, :], z[:, :, :], w["ln1w"][:, :].unsqueeze(1).to_broadcast([P, S, C]),
                              ALU.mult).then_inc(zw, 1)
            wait(eng, zw, 2 * b + 1)
            eng.tensor_tensor(z[:, :, :], z[:, :, :], w["ln1b"][:, :].unsqueeze(1).to_broadcast([P, S, C]),
                              ALU.add).then_inc(zw, 1)

        blk = s_.enter_context(nc.Block())

        @blk.tensor
        def _(pe):
            def turn_over(job, src):
                for j in range(TR):
                    kt, half_ = divmod(j, 2)
                    r = t_before(job) + j
                    wait(pe, t_free, r - 1)
                    for i in range(4):
                        mm = pe.transpose(T[:, r % 2, i, :], src(4 * half_ + i, kt), consts["identf"][:, :])
                    mm.then_inc(t_full, 1)
                wait(pe, t_free, t_before(job) + TR)

            def product(out, s, wt):
                for kt in range(KT):
                    mm = pe.matmul(out, zT[:, kt, s * P:(s + 1) * P], wt[:, kt, :],
                                   start=(kt == 0), stop=(kt == KT - 1))
                return mm

            for job in jobs:
                what, b = job
                if what == "front":
                    wait(pe, zw, 2 * (b + 1))
                    turn_over(job, lambda s, kt: z[:, s, kt * P:(kt + 1) * P])
                    wt, width = w["qkv"], QKV
                elif what == "oproj":
                    wait(pe, o_ready, S * (b + 1))
                    turn_over(job, lambda s, kt: o[:, s, kt * P:(kt + 1) * P])
                    wait(pe, var_ready, b)
                    for s in range(S):
                        product(H[:, s, :], s, w["proj"]).then_inc(h_full, 1)
                    continue
                else:
                    wait(pe, ln_ready, 2 * (b + 1))
                    turn_over(job, lambda s, kt: Zv[:, s, b, kt * P:(kt + 1) * P])
                    wt, width = w["router"], EXPERTS
                for s in range(S):
                    r = y_before(job) + s
                    wait(pe, y_free, r - 1)
                    product(Y[:, r % 2, 0:width], s, wt).then_inc(y_full, 1)

        @blk.scalar
        def _(act):
            def scale(b):
                if b:
                    wait(act, t_full, t_before(("front", b - 1)) + TR)
                for s in range(S):
                    j = TPB * s + b
                    mm = act.activation(z[:, s, :], XNv[:, s, b, :], ACT.Copy, scale=again[:, j:j + 1])
                mm.then_inc(scaled, 1)

            def copy_back(job):
                for j in range(TR):
                    kt, half_ = divmod(j, 2)
                    r = t_before(job) + j
                    wait(act, t_full, r + 1)
                    act.copy(zT[:, kt, half_ * 4 * P:(half_ + 1) * 4 * P],
                             T[:, r % 2, :, :].rearrange("p j n -> p (j n)")).then_inc(t_free, 1)

            def front(b):
                job = ("front", b)
                copy_back(job)
                wait(act, o_ready, S * (b - 1))
                for s in range(S):
                    r = y_before(job) + s
                    wait(act, y_full, r + 1)
                    act.copy(q[:, b % 2, s, :].rearrange("p (r g d) -> p g r d", g=KVH, d=HD),
                             Y[:, r % 2, 0:C].rearrange("p (g r d) -> p g r d", g=KVH, d=HD))
                    act.copy(kv[:, b % 2, s, :, :].rearrange("p a d -> p (a d)"),
                             Y[:, r % 2, C:QKV]).then_inc(y_free, 1)

            scale(0)
            front(0)
            for b in range(TPB + 1):
                if b + 1 < TPB:
                    scale(b + 1)
                if b:
                    copy_back(("oproj", b - 1))
                if 0 < b < TPB - 1:
                    front(b + 1)
                if b < TPB:
                    wait(act, sc_ready, b + 1)
                    act.activation(sc[:, :, :, :].rearrange("p s m h -> p (s m h)"),
                                   sc[:, :, :, :].rearrange("p s m h -> p (s m h)"), ACT.Exp,
                                   scale=float(HD) ** -0.5).then_inc(ex_ready, 1)
                if b == 0:
                    front(1)
                if b:
                    wait(act, rstd_ready, 2 * b)
                    for s in range(S):
                        mm = act.activation(Zv[:, s, b - 1, :], h[:, s, :], ACT.Identity,
                                            scale=rstd[:, s:s + 1], bias=nmr[:, s:s + 1])
                    mm.then_inc(normed, 1)
                    job = ("router", b - 1)
                    copy_back(job)
                    for s in range(S):
                        r = y_before(job) + s
                        wait(act, y_full, r + 1)
                        act.copy(Lv[:, s, b - 1, :], Y[:, r % 2, 0:EXPERTS]).then_inc(y_free, 1)

        @blk.gpsimd
        def _(pool):
            pool.memset(half[:, :], -0.5).then_inc(half_done, 1)
            pool.wait_ge(half_done, 1)
            for b in range(TPB + 1):
                if b < TPB:
                    wait(pool, y_free, y_before(("front", b)) + S)
                    wait(pool, pp_read, PP * b - 1)
                    pool.tensor_tensor(
                        prod2[:, (PP * b) % 2, :, :].rearrange("p m (r n) -> p m r n", r=REP),
                        q[:, b % 2, S - 1, :].rearrange("p (r n) -> p r n", r=REP).unsqueeze(1)
                        .to_broadcast([P, S, REP, KV]),
                        kv[:, b % 2, :, 0, :].unsqueeze(2).to_broadcast([P, S, REP, KV]), ALU.mult).then_inc(pp_ready, 1)
                if b + 1 < TPB:
                    ln1(pool, b + 1)
                if b < TPB:
                    xo = Xv[:, :, b, :]
                    pool.tensor_tensor(xo, xo, w["bo"][:, :].unsqueeze(1).to_broadcast([P, S, C]),
                                       ALU.add).then_inc(x_biased, 1)
                if b < TPB:
                    wait(pool, ex_ready, b + 1)
                for i in range(S):
                    if b and i == 2:
                        wait(pool, var_ready, b)
                        wait(pool, normed, b - 1)
                        pool.tensor_tensor(rstd[:, :], vare[:, :], half[:, :], ALU.pow).then_inc(rstd_ready, 1)
                        wait(pool, rstd_ready, 2 * b - 1)
                        pool.tensor_tensor(nmr[:, :], nmu[:, :], rstd[:, :], ALU.mult).then_inc(rstd_ready, 1)
                    if b < TPB:
                        s = S - 1 - i
                        m = s + 1
                        r = PP * b + 1 + i
                        wait(pool, pp_read, r - 1)
                        pool.tensor_tensor(
                            prod2[:, r % 2, 0:m, :].rearrange("p m (r g d) -> p m r g d", r=REP, d=HD),
                            kv[:, b % 2, 0:m, 1, :].rearrange("p m (g d) -> p m g d", g=KVH).unsqueeze(2)
                            .to_broadcast([P, m, REP, KVH, HD]),
                            sc[:, s, 0:m, :].rearrange("p m (r g) -> p m r g", r=REP).unsqueeze(4)
                            .to_broadcast([P, m, REP, KVH, HD]), ALU.mult).then_inc(pp_ready, 1)

        @blk.vector
        def _(dve):
            n = [0]

            def link(ins):
                n[0] += 1
                ins.then_inc(chain, 1)
                dve.wait_ge(chain, n[0])

            def by_head(rows, m):
                return rows.rearrange("p m (h d) -> p (m h) d", d=HD)

            def ln2(b):
                wait(dve, normed, b + 1)
                zo = Zv[:, :, b, :]
                dve.tensor_tensor(zo, zo, w["ln2w"][:, :].unsqueeze(1).to_broadcast([P, S, C]),
                                  ALU.mult).then_inc(ln_ready, 1)
                wait(dve, ln_ready, 2 * b + 1)
                dve.tensor_tensor(zo, zo, w["ln2b"][:, :].unsqueeze(1).to_broadcast([P, S, C]),
                                  ALU.add).then_inc(ln_ready, 1)

            link(dve.memset(carry[:, :], 0.0))
            ln1(dve, 0)
            for b in range(TPB + 1):
                if b < TPB:
                    link(dve.memset(sc[:, :, :, :].rearrange("p s m h -> p (s m h)"), NEG))
                    for s in range(S - 1):
                        m = s + 1
                        wait(dve, y_free, y_before(("front", b)) + m)
                        link(dve.tensor_tensor(
                            prod[:, 0:m, :].rearrange("p m (r n) -> p m r n", r=REP),
                            q[:, b % 2, s, :].rearrange("p (r n) -> p r n", r=REP).unsqueeze(1)
                            .to_broadcast([P, m, REP, KV]),
                            kv[:, b % 2, 0:m, 0, :].unsqueeze(2).to_broadcast([P, m, REP, KV]), ALU.mult))
                        link(dve.tensor_reduce(sc[:, s, 0:m, :].rearrange("p m h -> p (m h)"),
                                               by_head(prod[:, 0:m, :], m), AX.X, ALU.add))
                    wait(dve, pp_ready, PP * b + 1)
                    dve.tensor_reduce(sc[:, S - 1, :, :].rearrange("p m h -> p (m h)"),
                                      by_head(prod2[:, (PP * b) % 2, :, :], S), AX.X, ALU.add).then_inc(pp_read, 1)
                    wait(dve, pp_read, PP * b + 1)
                    by_key = sc[:, :, :, :].rearrange("p s m h -> p s h m")
                    link(dve.tensor_reduce(top[:, :, :], by_key, AX.X, ALU.max))
                    dve.tensor_tensor(sc[:, :, :, :], sc[:, :, :, :],
                                      top[:, :, :].unsqueeze(2).to_broadcast([P, S, S, HEADS]),
                                      ALU.subtract).then_inc(sc_ready, 1)
                if b:
                    wait(dve, normed, b - 1)
                    for i in range(0, S, 2):
                        wait(dve, h_full, S * (b - 1) + i + 2)
                        ins = dve.tensor_tensor(h[:, i:i + 2, :], H[:, i:i + 2, :], XNv[:, i:i + 2, b - 1, :], ALU.add)
                    link(ins)
                    for s in range(S):
                        ins = dve.bn_stats(stats[:, s, :], h[:, s, :])
                    link(ins)
                    dve.tensor_copy(carry[:, 1:2], carry[:, 0:1])
                    for s in range(S):
                        ins = dve.bn_aggr(mv[:, s, :], stats[:, s, :])
                    link(ins)
                    wait(dve, rstd_ready, 2 * (b - 1))
                    dve.tensor_scalar(nmu[:, :], mv[:, :, 0], -1.0, None, ALU.mult)
                    dve.tensor_scalar(vare[:, :], mv[:, :, 1], 1e-5, None, ALU.add).then_inc(var_ready, 1)
                    wait(dve, x_biased, b)
                    xo = Xv[:, :, b - 1, :]
                    dve.tensor_tensor(xo, xo, h[:, :, :], ALU.add)
                if b < TPB:
                    wait(dve, ex_ready, b + 1)
                    link(dve.tensor_reduce(sums[:, :, :], by_key, AX.X, ALU.add))
                    link(dve.reciprocal(den[:, :, :], sums[:, :, :]))
                if b < TPB:
                    if b:
                        wait(dve, t_full, t_before(("oproj", b - 1)) + TR)
                    for i in range(S):
                        if b and i == 2:
                            ln2(b - 1)
                        s = S - 1 - i
                        m = s + 1
                        r = PP * b + 1 + i
                        wait(dve, pp_ready, r + 1)
                        dve.tensor_reduce(prod[:, s, :], prod2[:, r % 2, 0:m, :].rearrange("p m c -> p c m"),
                                          AX.X, ALU.add).then_inc(pp_read, 1)
                        wait(dve, pp_read, r + 1)
                        dve.tensor_tensor(o[:, s, :].rearrange("p (g r d) -> p r g d", g=KVH, d=HD),
                                          prod[:, s, :].rearrange("p (r g d) -> p r g d", g=KVH, d=HD),
                                          den[:, s, :].rearrange("p (r g) -> p r g", g=KVH).unsqueeze(3)
                                          .to_broadcast([P, REP, KVH, HD]), ALU.mult).then_inc(o_ready, 1)
            ln2(TPB - 1)


def route(nc, logits, slot_id, gather_id, gate, consts):
    G, E = NT, EXPERTS
    with ExitStack() as s:
        def sb(nm, shape, dt=F32):
            return s.enter_context(nc.sbuf_tensor("r_" + nm, shape, dt))

        prb = sb("prb", [P, G, E])
        eq = sb("eq", [P, G, E])
        rest = sb("rest", [P, G, E])
        hot = [sb(f"hot{k}", [P, G, E]) for k in range(2)]
        top = [sb(f"top{k}", [P, G]) for k in range(2)]
        best = sb("best", [P, G])
        member = sb("member", [P, G * E], BF16)
        run = [sb(f"run{k}", [P, G, E]) for k in range(2)]
        place = sb("place", [P, G])
        expert = sb("expert", [P, G])
        keep = sb("keep", [P, G])
        lost = sb("lost", [P, G])
        ps = s.enter_context(nc.psum_tensor("r_ps", [P, 2, G * E], F32))
        chain = s.enter_context(nc.semaphore("r_chain"))
        exp_in, exp_out = s.enter_context(nc.semaphore("r_exp_in")), s.enter_context(nc.semaphore("r_exp_out"))
        mem_ready, cum_ready = s.enter_context(nc.semaphore("r_mem")), s.enter_context(nc.semaphore("r_cum"))
        blk = s.enter_context(nc.Block())

        @blk.scalar
        def _(act):
            act.wait_ge(exp_in, 1)
            act.activation(prb[:, :, :], prb[:, :, :], ACT.Exp).then_inc(exp_out, 1)

        @blk.tensor
        def _(pe):
            pe.wait_ge(mem_ready, 1)
            pe.matmul(ps[:, 0, :], consts["before"][:, :], member[:, :], start=True, stop=True)
            pe.matmul(ps[:, 1, :], consts["ones"][:, :], member[:, :], start=True, stop=True).then_inc(cum_ready, 1)

        @blk.vector
        def _(dve):
            steps = [0]

            def link(ins):
                steps[0] += 1
                ins.then_inc(chain, 1)
                dve.wait_ge(chain, steps[0])

            def wide(x):
                return x.unsqueeze(2).to_broadcast([P, G, E])

            link(dve.tensor_reduce(top[0][:, :], logits[:, :, :], AX.X, ALU.max))
            dve.tensor_tensor(prb[:, :, :], logits[:, :, :], wide(top[0][:, :]), ALU.subtract).then_inc(exp_in, 1)
            dve.wait_ge(exp_out, 1)
            link(dve.tensor_reduce(best[:, :], prb[:, :, :], AX.X, ALU.add))
            link(dve.reciprocal(best[:, :], best[:, :]))
            link(dve.tensor_tensor(prb[:, :, :], prb[:, :, :], wide(best[:, :]), ALU.mult))
            top_two(dve, link, prb[:, :, :], consts["desc16"][:, :].unsqueeze(1).to_broadcast([P, G, E]),
                    eq[:, :, :], [t[:, :] for t in top], best[:, :], [x[:, :, :] for x in hot], rest[:, :, :])
            dve.tensor_tensor(member[:, :].rearrange("p (g e) -> p g e", e=E), hot[0][:, :, :], hot[1][:, :, :],
                              ALU.add).then_inc(mem_ready, 1)
            dve.wait_ge(cum_ready, 1)
            link(dve.tensor_copy(run[0][:, :, :], ps[:, 1, :].rearrange("p (g e) -> p g e", e=E)))
            a, b, d = 0, 1, 1
            while d < G:
                link(dve.tensor_tensor(run[b][:, d:G, :], run[a][:, d:G, :], run[a][:, 0:G - d, :], ALU.add))
                link(dve.tensor_copy(run[b][:, 0:d, :], run[a][:, 0:d, :]))
                a, b, d = b, a, 2 * d
            link(dve.tensor_copy(run[b][:, 0, :], ps[:, 0, 0:E]))
            link(dve.tensor_tensor(run[b][:, 1:G, :], run[a][:, 0:G - 1, :],
                                   ps[:, 0, :].rearrange("p (g e) -> p g e", e=E)[:, 1:G, :], ALU.add))
            for k in range(2):
                link(dve.tensor_tensor(eq[:, :, :], run[b][:, :, :], hot[k][:, :, :], ALU.mult))
                link(dve.tensor_reduce(place[:, :], eq[:, :, :], AX.X, ALU.add))
                link(dve.tensor_tensor(eq[:, :, :], hot[k][:, :, :],
                                       consts["base16"][:, :].unsqueeze(1).to_broadcast([P, G, E]), ALU.mult))
                link(dve.tensor_reduce(expert[:, :], eq[:, :, :], AX.X, ALU.add))
                link(dve.tensor_scalar(keep[:, :], place[:, :], float(CAP), None, ALU.is_lt))
                link(dve.tensor_tensor(place[:, :], place[:, :], expert[:, :], ALU.add))
                link(dve.tensor_tensor(gate[:, :, k], top[k][:, :], keep[:, :], ALU.mult))
                link(dve.tensor_tensor(place[:, :], place[:, :], keep[:, :], ALU.mult))
                link(dve.tensor_copy(gather_id[:, :, k], place[:, :]))
                link(dve.tensor_scalar(lost[:, :], keep[:, :], -float(2 * SLOTROWS), float(2 * SLOTROWS),
                                       ALU.mult, ALU.add))
                link(dve.tensor_tensor(lost[:, :], place[:, :], lost[:, :], ALU.add))
                link(dve.tensor_copy(slot_id[:, :, k], lost[:, :]))


def experts(nc, Z, slot_id, consts, dram):
    E = EXPERTS
    FT = FFN // P
    with ExitStack() as s:
        def sb(nm, shape, dt=F32):
            return s.enter_context(nc.sbuf_tensor("e_" + nm, shape, dt))

        def sem(nm):
            return s.enter_context(nc.semaphore("e_" + nm))

        w1 = sb("w1", [P, 2, KT, FFN])
        w2 = sb("w2", [P, 2, FT, C])
        rows = sb("rows", [P, 2, CT, C])
        rowsT = sb("rowsT", [P, 2, KT, CAP])
        hid = sb("hid", [P, FT, CAP])
        outs = sb("outs", [P, 2, CT, C])
        RT = s.enter_context(nc.psum_tensor("e_RT", [P, 2 * 512], F32))
        OB = s.enter_context(nc.psum_tensor("e_OB", [P, 2, 512], F32))
        HB = s.enter_context(nc.psum_tensor("e_HB", [P, 2, 2, 512], F32))
        HC = CAP // 2
        scattered = sem("scattered")
        w_in = [sem("w_in0"), sem("w_in1")]
        rows_in = [sem("rows_in0"), sem("rows_in1")]
        t_full, t_free = sem("t_full"), sem("t_free")
        h_full, h_free = sem("h_full"), sem("h_free")
        o_full, o_free = sem("o_full"), sem("o_free")
        stored = [sem("stored0"), sem("stored1")]
        blk = s.enter_context(nc.Block())

        def turns(eng, body):
            for e in range(2):
                body(e, e, 0)
            with eng.Fori(1, E // 2 - 1) as pair:
                for e in range(2):
                    body(2 * pair + e, e, pair)
            for e in range(E - 2, E):
                body(e, e % 2, e // 2)

        def last(e):
            return isinstance(e, int) and e == E - 1

        @blk.sync
        def _(sp):
            def load_weights(e, par):
                sp.dma_start(w1[:, par, :, :], dram["w1"][:, bass.ds(e, 1), :, :].rearrange("p e k f -> p (e k) f"))\
                  .then_inc(w_in[par], 16)
                sp.dma_start(w2[:, par, :, :], dram["w2"][:, bass.ds(e, 1), :, :].rearrange("p e k c -> p (e k) c"))\
                  .then_inc(w_in[par], 16)

            def body(e, par, pair):
                if isinstance(e, int) and e < 2:
                    if e == 0:
                        load_weights(0, 0)
                        load_weights(1, 1)
                        sp.wait_ge(scattered, 16 * NT * TOPK)
                    sp.dma_start(rows[:, par, :, :], dram["rows_v"][:, bass.ds(CT * e, CT), :])\
                      .then_inc(rows_in[par], 16)
                    return
                sp.wait_ge(t_full, KT * (e - 1))
                sp.dma_start(rows[:, par, :, :], dram["rows_v"][:, bass.ds(CT * e, CT), :]).then_inc(rows_in[par], 16)
                sp.wait_ge(o_full, CT * (e - 1))
                load_weights(e, par)

            turns(sp, body)

        @blk.gpsimd
        def _(pool):
            for j in range(NT):
                for k in range(TOPK):
                    pool.indirect_dma_start(dram["rows"], bass.IndirectOffsetOnAxis(ap=slot_id[:, j, k:k + 1], axis=0),
                                            Z[:, j, :], None, bounds_check=SLOTROWS - 1,
                                            oob_is_err=False).then_inc(scattered, 16)

            def body(e, par, pair):
                pool.wait_ge(o_free, CT * (e + 1))
                pool.dma_start(dram["outs_v"][:, bass.ds(CT * e, CT), :], outs[:, par, :, :]).then_inc(stored[par], 16)

            turns(pool, body)
            for par in range(2):
                pool.wait_ge(stored[par], 16 * (E // 2))

        @blk.tensor
        def _(pe):
            def turn_over(e, par, pair, kt):
                if kt == 0:
                    pe.wait_ge(rows_in[par], 16 * (pair + 1))
                if not isinstance(e, int) or KT * e + kt > 0:
                    pe.wait_ge(t_free, KT * e + kt)
                for c in range(CT):
                    mm = pe.transpose(RT[:, c * P:(c + 1) * P], rows[:, par, c, kt * P:(kt + 1) * P],
                                      consts["identf"][:, :])
                mm.then_inc(t_full, 1)

            def body(e, par, pair):
                pe.wait_ge(w_in[par], 32 * (pair + 1))
                pe.wait_ge(t_free, KT * (e + 1))
                for f in range(FT):
                    r = FT * e + f
                    if not isinstance(r, int) or r >= 2:
                        pe.wait_ge(h_free, r - 1)
                    for half_ in range(2):
                        for kt in range(KT):
                            mm = pe.matmul(HB[:, f % 2, half_, 0:HC], w1[:, par, kt, f * P:(f + 1) * P],
                                           rowsT[:, par, kt, half_ * HC:(half_ + 1) * HC],
                                           start=(kt == 0), stop=(kt == KT - 1))
                    mm.then_inc(h_full, 1)
                    if f % 2 and not last(e):
                        turn_over(e + 1, 1 - par, pair + par, f // 2)
                pe.wait_ge(h_free, FT * (e + 1))
                for c in range(CT):
                    r = CT * e + c
                    if not isinstance(r, int) or r >= 2:
                        pe.wait_ge(o_free, r - 1)
                    for f in range(FT):
                        mm = pe.matmul(OB[:, (CT * par + c) % 2, 0:C], hid[:, f, c * P:(c + 1) * P],
                                       w2[:, par, f, :], start=(f == 0), stop=(f == FT - 1))
                    mm.then_inc(o_full, 1)

            for kt in range(KT):
                turn_over(0, 0, 0, kt)
            turns(pe, body)

        @blk.scalar
        def _(act):
            def body(e, par, pair):
                for f in range(FT):
                    act.wait_ge(h_full, FT * e + f + 1)
                    act.activation(hid[:, f, :].rearrange("p (a n) -> p a n", a=2), HB[:, f % 2, :, 0:HC],
                                   ACT.Gelu_apprx_tanh).then_inc(h_free, 1)

            turns(act, body)

        @blk.vector
        def _(dve):
            def copy_rows(e, par, kt):
                dve.wait_ge(t_full, KT * e + kt + 1)
                dve.tensor_copy(rowsT[:, par, kt, :], RT[:, 0:CAP]).then_inc(t_free, 1)

            def body(e, par, pair):
                if not last(e):
                    for kt in range(KT):
                        copy_rows(e + 1, 1 - par, kt)
                for c in range(CT):
                    dve.wait_ge(o_full, CT * e + c + 1)
                    if c == 0 and not (isinstance(pair, int) and pair == 0):
                        dve.wait_ge(stored[par], 16 * pair)
                    dve.tensor_copy(outs[:, par, c, :], OB[:, (CT * par + c) % 2, 0:C]).then_inc(o_free, 1)

            for kt in range(KT):
                copy_rows(0, 0, kt)
            turns(dve, body)


def two_layers(nc, d, out):
    rows_d = nc.dram_tensor("expert_rows", (SLOTROWS, C), F32, kind="Internal").ap()
    outs_d = nc.dram_tensor("expert_outs", (SLOTROWS, C), F32, kind="Internal").ap()
    out_v = out.rearrange("b (t p) c -> p (b t) c", p=P)
    x_v = d["x"].rearrange("b (t p) c -> p (b t) c", p=P)
    with ExitStack() as s:
        def sb(nm, shape, dt=F32, st=s):
            return st.enter_context(nc.sbuf_tensor(nm, shape, dt))

        X = sb("X", [P, NT, C])
        identf = sb("identf", [P, P])
        identb = sb("identb", [P, P], BF16)
        mask_kq = sb("mask_kq", [P, P], BF16)
        mask_qk = sb("mask_qk", [P, P], BF16)
        before = sb("before", [P, P], BF16)
        ones = sb("ones", [P, P], BF16)
        desc16 = sb("desc16", [P, EXPERTS])
        base16 = sb("base16", [P, EXPERTS])
        consts = dict(identf=identf, identb=identb, mask_kq=mask_kq, mask_qk=mask_qk, before=before,
                      ones=ones, desc16=desc16, base16=base16)
        zeroed = s.enter_context(nc.semaphore("zeroed"))

        stats = sb("stats", [P, NT, 6])

        with ExitStack() as l0:
            w = {}
            w["WA"] = sb("WA", [P, KT, GROUPS, 3 * GW], st=l0)
            w["WB"] = sb("WB", [P, KT, GROUPS, 3 * GW], st=l0)
            w["WoA"] = sb("WoA", [P, KT, C], st=l0)
            w["WoB"] = sb("WoB", [P, KT, C], st=l0)
            w["V"] = sb("V", [P, 4, C], st=l0)
            w["UT"] = sb("UT", [P, 4, C], st=l0)
            w["gS"] = sb("gS", [P, 4, BATCH], st=l0)
            w["bA"] = sb("bA", [P, GROUPS, 3 * GW], st=l0)
            w["bB"] = sb("bB", [P, GROUPS, 3 * GW], st=l0)
            w["bout"] = sb("bout", [P, C], st=l0)
            w["qkn"] = sb("qkn", [P, 2, HD], st=l0)
            zeros = sb("zeros", [P, 2048], st=l0)
            with ExitStack() as g0:
                stage = sb("stage", [P, 5, P], st=g0)
                b2 = sb("b2", [P, C], st=g0)
                S4 = sb("S4", [P, 4], st=g0)
                gw = dict(gw1=sb("gw1", [P, KT, 64], st=g0), gw2=sb("gw2", [64, 8], st=g0),
                          gb1=sb("gb1", [64, 1], st=g0), gb2=sb("gb2", [BATCH, 8], st=g0),
                          rep=sb("rep", [8, P], st=g0), desc8=sb("desc8", [BATCH, 8], st=g0))
                x_in = [g0.enter_context(nc.semaphore(f"x_in{b}")) for b in range(BATCH)]
                w_in = g0.enter_context(nc.semaphore("w_in"))
                mean = sb("mean", [P, BATCH * BATCH], st=g0)
                tokens = g0.enter_context(nc.psum_tensor("tokens", [P, 512], F32))
                pooled = g0.enter_context(nc.semaphore("pooled"))
                x_loads = [(X[:, TPB * b:TPB * (b + 1), :], x_v[:, TPB * b:TPB * (b + 1), :], x_in[b])
                           for b in range(BATCH)]
                loads = [(stage[:, :, :], d["c_stage"]), (identf[:, :], d["c_ident"]),
                         (desc16[:, :], d["c_desc16"].partition_broadcast(P)),
                         (base16[:, :], d["c_base16"].partition_broadcast(P)),
                         (w["WA"][:, :, :, :], d["WA"].rearrange("(k p) g n -> p k g n", p=P)),
                         (w["WB"][:, :, :, :], d["WB"].rearrange("(k p) g n -> p k g n", p=P)),
                         (w["WoA"][:, :, :], d["WoA"].rearrange("(k p) n -> p k n", p=P)),
                         (w["WoB"][:, :, :], d["WoB"].rearrange("(k p) n -> p k n", p=P)),
                         (w["V"][:, :, :], d["V4"].rearrange("j p n -> p j n")),
                         (w["UT"][:, :, :], d["UT4"].rearrange("j p n -> p j n")),
                         (w["bA"][:, :, :], d["bA"].partition_broadcast(P)),
                         (w["bB"][:, :, :], d["bB"].partition_broadcast(P)),
                         (w["bout"][:, :], d["boA"].partition_broadcast(P)),
                         (b2[:, :], d["boB"].partition_broadcast(P)),
                         (w["qkn"][:, 0, :], d["qn"].partition_broadcast(P)),
                         (w["qkn"][:, 1, :], d["kn"].partition_broadcast(P)),
                         (S4[:, :], d["S4"]),
                         (gw["gw1"][:, :, :], d["gw1T"].rearrange("(k p) n -> p k n", p=P)),
                         (gw["gw2"][:, :], d["gw2T"]), (gw["gb1"][:, :], d["gb1"]),
                         (gw["gb2"][:, :], d["gb2"].partition_broadcast(BATCH)),
                         (gw["rep"][:, :], d["c_rep"]),
                         (gw["desc8"][:, :], d["c_desc8"].partition_broadcast(BATCH))]
                assert len(loads) == GATES_LOADS
                layernorm(nc, "ln0", X, X, 1e-5, loads=x_loads + [(to, fro, w_in) for to, fro in loads],
                          arriving=x_in, pooling=(mean, tokens[0:BATCH, 0:C], pooled))
                gates(nc, X, gw, w["gS"], consts, S4, dict(w_in=w_in, stage=stage, bout=w["bout"], b2=b2, zeros=zeros,
                                                      tokens=tokens[0:BATCH, 0:C], pooled=pooled))
            zfill = [(rows_d.rearrange("(a p q) c -> a p (q c)", p=P, q=8)[a], zeros[:, :]) for a in range(ZFILLS)]
            attention(nc, "L0", 0, X, X, w, consts, dict(x=x_v, loads=[], aside=zfill, aside_done=zeroed, stats=stats))

        XN = sb("XN", [P, NT, C])
        again = sb("again", [P, NT])
        gather_id = sb("gather_id", [P, NT, TOPK], U32)
        gate = sb("gate", [P, NT, TOPK])
        layernorm(nc, "ln1", X, XN, 1e-5, again, stats=stats)
        with ExitStack() as m:
            Z = sb("Z", [P, NT, C], st=m)
            logits = sb("logits", [P, NT, EXPERTS], st=m)
            slot_id = sb("slot_id", [P, NT, TOPK], U32, st=m)
            with ExitStack() as q:
                w = dict(qkv=sb("Dqkv", [P, KT, C + 8 * HD], st=q), proj=sb("Dproj", [P, KT, C], st=q),
                         router=sb("Drouter", [P, KT, EXPERTS], st=q), ln1w=sb("Dln1w", [P, C], st=q),
                         ln1b=sb("Dln1b", [P, C], st=q), ln2w=sb("Dln2w", [P, C], st=q),
                         ln2b=sb("Dln2b", [P, C], st=q), bo=sb("Dbo", [P, C], st=q))
                with ExitStack() as q2:
                    w_in = q2.enter_context(nc.semaphore("d_w_in"))
                    blk = q2.enter_context(nc.Block())

                    @blk.sync
                    def _(sp):
                        for dst, src in ((w["qkv"], "DqkvT"), (w["proj"], "DprojT"), (w["router"], "DrouterT")):
                            sp.dma_start(dst[:, :, :], d[src].rearrange("(k p) n -> p k n", p=P)).then_inc(w_in, 16)
                        for dst, src in ((w["ln1w"], "ln1w"), (w["ln1b"], "ln1b"), (w["ln2w"], "ln2w"),
                                         (w["ln2b"], "ln2b"), (w["bo"], "boC")):
                            sp.dma_start(dst[:, :], d[src].partition_broadcast(P)).then_inc(w_in, 16)
                        sp.wait_ge(w_in, 16 * 8)

                block_d(nc, X, XN, Z, again, logits, w, consts)
            route(nc, logits, slot_id, gather_id, gate, consts)
            experts(nc, Z, slot_id, consts,
                    dict(w1=d["w1T"].rearrange("e (k p) f -> p e k f", p=P),
                         w2=d["w2T"].rearrange("e (k p) c -> p e k c", p=P), rows=rows_d, outs=outs_d,
                         rows_v=rows_d.rearrange("(t p) c -> p t c", p=P),
                         outs_v=outs_d.rearrange("(t p) c -> p t c", p=P)))
        with ExitStack() as q:
            w = dict(WC=sb("WC", [P, KT, GROUPS, 3 * GW], st=q), WoC=sb("WoC", [P, KT, C], st=q),
                     bC=sb("bC", [P, GROUPS, 3 * GW], st=q), cos=sb("cos", [P, TPB, HD // 2], st=q),
                     sin=sb("sin", [P, TPB, HD // 2], st=q), gather_id=gather_id, gate=gate)
            loads = [(w["WC"][:, :, :, :], d["WC"].rearrange("(k p) g n -> p k g n", p=P)),
                     (w["WoC"][:, :, :], d["WoC"].rearrange("(k p) n -> p k n", p=P)),
                     (w["bC"][:, :, :], d["bC"].partition_broadcast(P)),
                     (w["cos"][:, :, :], d["c_cos"].rearrange("(t p) n -> p t n", p=P)),
                     (w["sin"][:, :, :], d["c_sin"].rearrange("(t p) n -> p t n", p=P))]
            attention(nc, "L1", 1, X, XN, w, consts, dict(out=out_v, outs=outs_d, loads=loads, aside=[]))


def kernel(**inputs):
    import numpy as np
    import concourse.bacc as _bacc
    from concourse import mybir as _mybir
    from concourse.bass_utils import run_bass_kernel_spmd as _run

    a = {k: np.asarray(v) for k, v in inputs.items()}

    def grouped(parts):
        return np.stack([m.reshape(m.shape[0], GROUPS, GW) for m in parts], axis=2).reshape(-1, GROUPS, 3 * GW)

    def grouped_bias(parts):
        return np.stack([m.reshape(GROUPS, GW) for m in parts], axis=1).reshape(GROUPS, 3 * GW)

    n = {}
    n["x"] = a["L0_attn_x"]
    wa = a["L0_attn_W_qkv"]
    n["WA"] = grouped([wa[:, 0:C], wa[:, C:2 * C], wa[:, 2 * C:]])
    ba = a["L0_attn_b_qkv"]
    n["bA"] = grouped_bias([ba[0:C], ba[C:2 * C], ba[2 * C:]])
    n["WoA"] = a["L0_attn_W_proj"]
    n["boA"] = a["L0_attn_b_proj"]
    n["qn"], n["kn"] = a["L0_attn_qn_w"], a["L0_attn_kn_w"]
    n["WB"] = grouped([a[f"L0_ffn_{p}Wm"].T for p in "qkv"])
    n["bB"] = grouped_bias([a[f"L0_ffn_{p}b"] for p in "qkv"])
    n["WoB"] = a["L0_ffn_oWm"].T
    n["boB"] = a["L0_ffn_ob"]
    n["V4"] = np.stack([a[f"L0_ffn_{p}V"].reshape(P, C) for p in "qkvo"])
    n["UT4"] = np.stack([a[f"L0_ffn_{p}U"].transpose(0, 2, 1).reshape(P, C) for p in "qkvo"])
    n["S4"] = np.stack([a[f"L0_ffn_{p}S"].reshape(P) for p in "qkvo"], axis=1)
    n["gw1T"], n["gw2T"] = a["L0_ffn_gw1"].T, a["L0_ffn_gw2"].T
    n["gb1"], n["gb2"] = a["L0_ffn_gb1"].reshape(-1, 1), a["L0_ffn_gb2"]
    n["WC"] = grouped([a[f"L1_attn_W{p}"].T for p in "qkv"])
    n["bC"] = grouped_bias([a[f"L1_attn_b{p}"] for p in "qkv"])
    n["WoC"], n["boC"] = a["L1_attn_Wo"].T, a["L1_attn_bo"]
    n["DqkvT"] = a["L1_ffn_qkv_weight"].T
    n["DprojT"] = a["L1_ffn_proj_weight"].T
    n["DrouterT"] = a["L1_ffn_router_weight"].T
    for m in ("ln1", "ln2"):
        n[m + "w"], n[m + "b"] = a[f"L1_ffn_{m}_weight"], a[f"L1_ffn_{m}_bias"]
    n["w1T"] = a["L1_ffn_moe_w1"].transpose(0, 2, 1)
    n["w2T"] = a["L1_ffn_moe_w2"].transpose(0, 2, 1)

    f = np.float32
    i = np.arange(P)
    behind = np.where(i[:, None] > i[None, :], f(NEG), f(0))
    n["c_ident"] = np.eye(P, dtype=f)
    n["c_stage"] = np.stack([np.eye(P, dtype=f), behind, behind.T, (i[:, None] < i[None, :]).astype(f),
                             np.zeros((P, P), f)], axis=1)
    n["c_desc16"] = f(EXPERTS) - np.arange(EXPERTS, dtype=f)
    n["c_base16"] = f(CAP) * np.arange(EXPERTS, dtype=f)
    n["c_desc8"] = f(8) - np.arange(8, dtype=f)
    n["c_rep"] = (np.arange(8)[:, None] == i[None, :] // 16).astype(f)
    theta = (f(1.0) / f(10000.0)) ** (f(2.0) * np.arange(HD // 2, dtype=f) / f(HD))
    angle = np.arange(1, SEQ + 1, dtype=f)[:, None] * theta.astype(f)
    n["c_cos"], n["c_sin"] = np.cos(angle).astype(f), np.sin(angle).astype(f)

    nc = _bacc.Bacc("TRN2", target_bir_lowering=False, num_devices=1)
    arrays, d = {}, {}
    for name, arr in n.items():
        arr = np.ascontiguousarray(arr)
        arrays[f"in_{name}"] = arr
        d[name] = nc.dram_tensor(f"in_{name}", arr.shape, _mybir.dt.from_np(arr.dtype), kind="ExternalInput").ap()
    out = nc.dram_tensor("out_0", (BATCH, SEQ, C), F32, kind="ExternalOutput").ap()
    two_layers(nc, d, out)
    r = _run(nc, [arrays], core_ids=[0])
    return r.results[0]["out_0"]
```
